# Optimizing a Trainium2 kernel written in Bass

```python
import numpy as np
import jax
import jax.numpy as jnp

def _softmax(x, axis=-1):
    return jax.nn.softmax(x, axis=axis)

def _gelu(x):
    return jax.nn.gelu(x, approximate=True)

def _silu(x):
    return jax.nn.silu(x)

def _sigmoid(x):
    return jax.nn.sigmoid(x)

def _layernorm(x, axis=-1, eps=1e-05):
    m = jnp.mean(x, axis=axis, keepdims=True)
    v = jnp.var(x, axis=axis, keepdims=True)
    return (x - m) / jnp.sqrt(v + eps)

def _scatter_add(tgt, idx, src, axis=0):
    return tgt.at[idx].add(src)

def _segment_sum(src, seg, n):
    return jax.ops.segment_sum(src, seg, n)
kernel_name = 'mk_sandwich_d2_jaxref_r8_255d4e'

def setup_inputs(seed: int=0):
    np.random.seed(seed)
    _w = jnp.asarray

    def _L0_attn_setup():
        import jax, jax.numpy as jnp
        import numpy as np
        B, N, H = (2, 512, 256)
        NH, HD = (16, 128)
        BLK = 32
        EPS = 1e-06

        def _lightning_attn(x, slope_rate, w_qkv, w_gate, w_out, norm_w):
            b, n, _ = x.shape
            h, d = (NH, HD)
            nb = n // BLK
            qkv = jax.nn.silu(jnp.einsum('bnf,of->bno', x, w_qkv))
            qkv = qkv.reshape(b, n, h, 3 * d)
            q, k, v = jnp.split(qkv, 3, axis=-1)
            q = q.transpose(0, 2, 1, 3)
            k = k.transpose(0, 2, 1, 3)
            v = v.transpose(0, 2, 1, 3)
            s = slope_rate.astype(jnp.float32)
            arr = jnp.arange(1, BLK + 1, dtype=jnp.float32)
            q_decay = jnp.exp(-s * arr[:, None])
            k_decay = jnp.exp(-s * (BLK - arr)[:, None])
            idx = arr[:, None] - arr[None, :]
            diag_decay = jnp.where(idx >= 0, jnp.exp(-s * idx), 0.0)
            block_decay = jnp.exp(-s * BLK)
            qb = q.reshape(b, h, nb, BLK, d).transpose(2, 0, 1, 3, 4)
            kb = k.reshape(b, h, nb, BLK, d).transpose(2, 0, 1, 3, 4)
            vb = v.reshape(b, h, nb, BLK, d).transpose(2, 0, 1, 3, 4)

            def step(kv, blk):
                qi, ki, vi = blk
                o_inter = jnp.einsum('bhmd,bhde->bhme', qi * q_decay, kv)
                qk = jnp.einsum('bhmd,bhnd->bhmn', qi, ki) * diag_decay
                o_intra = jnp.einsum('bhmn,bhne->bhme', qk, vi)
                kv_new = block_decay * kv + jnp.einsum('bhmd,bhme->bhde', ki * k_decay, vi)
                return (kv_new, o_inter + o_intra)
            kv0 = jnp.zeros((b, h, d, d), dtype=jnp.float32)
            _, out = jax.lax.scan(step, kv0, (qb, kb, vb))
            out = out.transpose(1, 2, 0, 3, 4).reshape(b, h, n, d)
            out = out.transpose(0, 2, 1, 3).reshape(b, n, h * d)
            var = jnp.mean(out * out, axis=-1, keepdims=True)
            out = norm_w * (out * jax.lax.rsqrt(var + EPS))
            gate = jax.nn.sigmoid(jnp.einsum('bnf,of->bno', x, w_gate))
            return jnp.einsum('bno,fo->bnf', gate * out, w_out)
        key = jax.random.key(seed)
        ks = jax.random.split(key, 5)
        scale = 0.02
        x = jax.random.normal(ks[0], (B, N, H), dtype=jnp.float32)
        slopes = (1.0 / 2.0 ** (8.0 * np.arange(1, NH + 1) / NH)).astype(np.float32)
        slope_rate = jnp.asarray(slopes).reshape(NH, 1, 1)
        w_qkv = jax.random.normal(ks[1], (3 * NH * HD, H), dtype=jnp.float32) * scale
        w_gate = jax.random.normal(ks[2], (NH * HD, H), dtype=jnp.float32) * scale
        w_out = jax.random.normal(ks[3], (H, NH * HD), dtype=jnp.float32) * scale
        norm_w = jnp.ones((NH * HD,), dtype=jnp.float32)
        return {'hidden_states': x, 'slope_rate': slope_rate, 'w_qkv': w_qkv, 'w_gate': w_gate, 'w_out': w_out, 'norm_w': norm_w}
    _L0_attn_in = _L0_attn_setup()

    def _L0_ffn_setup():
        import jax, jax.numpy as jnp
        import numpy as np
        H = 256
        I = 176
        E = 16
        K = 2
        SI = I * 2

        def _swiglu(gu, inter):
            g, u = (gu[..., :inter], gu[..., inter:])
            return jax.nn.silu(g) * u
        key = jax.random.key(seed)
        ks = jax.random.split(key, 6)
        s = 0.02
        hidden_states = jax.random.normal(ks[0], (1, 128, H), dtype=jnp.float32)
        gate_w = jax.random.normal(ks[1], (E, H), dtype=jnp.float32) * s
        w_gate_up = jax.random.normal(ks[2], (E, H, 2 * I), dtype=jnp.float32) * s
        w_down = jax.random.normal(ks[3], (E, I, H), dtype=jnp.float32) * s
        shared_gate_up = jax.random.normal(ks[4], (H, 2 * SI), dtype=jnp.float32) * s
        shared_down = jax.random.normal(ks[5], (SI, H), dtype=jnp.float32) * s
        return {'hidden_states': hidden_states, 'gate_w': gate_w, 'w_gate_up': w_gate_up, 'w_down': w_down, 'shared_gate_up': shared_gate_up, 'shared_down': shared_down}
    _L0_ffn_in = _L0_ffn_setup()

    def _L1_attn_setup():
        import jax, jax.numpy as jnp
        import numpy as np
        EMBED_DIM = 256
        NUM_HEADS = 16
        HEAD_DIM = EMBED_DIM // NUM_HEADS
        NUM_KV_GROUPS = 2
        WINDOW = 32
        KV_DIM = NUM_KV_GROUPS * HEAD_DIM
        key = jax.random.key(seed)
        ks = jax.random.split(key, 9)
        B, L, C = (2, 512, EMBED_DIM)
        s = 1.0 / np.sqrt(C)
        return {'x': jax.random.normal(ks[0], (B, L, C), dtype=jnp.float32), 'Wq': jax.random.normal(ks[1], (C, C), dtype=jnp.float32) * s, 'bq': jnp.zeros((C,), dtype=jnp.float32), 'Wk': jax.random.normal(ks[2], (C, KV_DIM), dtype=jnp.float32) * s, 'bk': jnp.zeros((KV_DIM,), dtype=jnp.float32), 'Wv': jax.random.normal(ks[3], (C, KV_DIM), dtype=jnp.float32) * s, 'bv': jnp.zeros((KV_DIM,), dtype=jnp.float32), 'Wo': jax.random.normal(ks[4], (C, C), dtype=jnp.float32) * s, 'bo': jnp.zeros((C,), dtype=jnp.float32)}
    _L1_attn_in = _L1_attn_setup()

    def _L1_ffn_setup():
        import jax, jax.numpy as jnp
        import numpy as np
        HIDDEN = 256
        INTER = 1024
        BATCH, LOCAL_SEQ = (2, 512)
        key = jax.random.key(seed)
        k1, k2, k3 = jax.random.split(key, 3)
        h_shard = jax.random.normal(k1, (BATCH, LOCAL_SEQ, HIDDEN), dtype=jnp.float32)
        w_gate_up = jax.random.normal(k2, (2 * INTER, HIDDEN), dtype=jnp.float32) * 0.02
        w_down = jax.random.normal(k3, (HIDDEN, INTER), dtype=jnp.float32) * 0.02
        return {'h_shard': h_shard, 'w_gate_up': w_gate_up, 'w_down': w_down}
    _L1_ffn_in = _L1_ffn_setup()
    _d = {'L0_attn_hidden_states': _L0_attn_in['hidden_states'], 'L0_attn_slope_rate': _L0_attn_in['slope_rate'], 'L0_attn_w_qkv': _L0_attn_in['w_qkv'], 'L0_attn_w_gate': _L0_attn_in['w_gate'], 'L0_attn_w_out': _L0_attn_in['w_out'], 'L0_attn_norm_w': _L0_attn_in['norm_w'], 'L0_ffn_gate_w': _L0_ffn_in['gate_w'], 'L0_ffn_w_gate_up': _L0_ffn_in['w_gate_up'], 'L0_ffn_w_down': _L0_ffn_in['w_down'], 'L0_ffn_shared_gate_up': _L0_ffn_in['shared_gate_up'], 'L0_ffn_shared_down': _L0_ffn_in['shared_down'], 'L1_attn_Wq': _L1_attn_in['Wq'], 'L1_attn_bq': _L1_attn_in['bq'], 'L1_attn_Wk': _L1_attn_in['Wk'], 'L1_attn_bk': _L1_attn_in['bk'], 'L1_attn_Wv': _L1_attn_in['Wv'], 'L1_attn_bv': _L1_attn_in['bv'], 'L1_attn_Wo': _L1_attn_in['Wo'], 'L1_attn_bo': _L1_attn_in['bo'], 'L1_ffn_w_gate_up': _L1_ffn_in['w_gate_up'], 'L1_ffn_w_down': _L1_ffn_in['w_down']}
    _x0 = _d['L0_attn_hidden_states']
    _d['L0_attn_hidden_states'] = jax.random.normal(jax.random.fold_in(jax.random.key(seed), 1), (2, 1024, 256), dtype=_x0.dtype)
    del _x0
    return _d

def reference(L0_attn_hidden_states, L0_attn_slope_rate, L0_attn_w_qkv, L0_attn_w_gate, L0_attn_w_out, L0_attn_norm_w, L0_ffn_gate_w, L0_ffn_w_gate_up, L0_ffn_w_down, L0_ffn_shared_gate_up, L0_ffn_shared_down, L1_attn_Wq, L1_attn_bq, L1_attn_Wk, L1_attn_bk, L1_attn_Wv, L1_attn_bv, L1_attn_Wo, L1_attn_bo, L1_ffn_w_gate_up, L1_ffn_w_down):

    def _L0_attn_ref(hidden_states, slope_rate, w_qkv, w_gate, w_out, norm_w):
        import jax, jax.numpy as jnp
        import numpy as np
        B, N, H = (2, 512, 256)
        NH, HD = (16, 128)
        BLK = 32
        EPS = 1e-06

        def _lightning_attn(x, slope_rate, w_qkv, w_gate, w_out, norm_w):
            b, n, _ = x.shape
            h, d = (NH, HD)
            nb = n // BLK
            qkv = jax.nn.silu(jnp.einsum('bnf,of->bno', x, w_qkv))
            qkv = qkv.reshape(b, n, h, 3 * d)
            q, k, v = jnp.split(qkv, 3, axis=-1)
            q = q.transpose(0, 2, 1, 3)
            k = k.transpose(0, 2, 1, 3)
            v = v.transpose(0, 2, 1, 3)
            s = slope_rate.astype(jnp.float32)
            arr = jnp.arange(1, BLK + 1, dtype=jnp.float32)
            q_decay = jnp.exp(-s * arr[:, None])
            k_decay = jnp.exp(-s * (BLK - arr)[:, None])
            idx = arr[:, None] - arr[None, :]
            diag_decay = jnp.where(idx >= 0, jnp.exp(-s * idx), 0.0)
            block_decay = jnp.exp(-s * BLK)
            qb = q.reshape(b, h, nb, BLK, d).transpose(2, 0, 1, 3, 4)
            kb = k.reshape(b, h, nb, BLK, d).transpose(2, 0, 1, 3, 4)
            vb = v.reshape(b, h, nb, BLK, d).transpose(2, 0, 1, 3, 4)

            def step(kv, blk):
                qi, ki, vi = blk
                o_inter = jnp.einsum('bhmd,bhde->bhme', qi * q_decay, kv)
                qk = jnp.einsum('bhmd,bhnd->bhmn', qi, ki) * diag_decay
                o_intra = jnp.einsum('bhmn,bhne->bhme', qk, vi)
                kv_new = block_decay * kv + jnp.einsum('bhmd,bhme->bhde', ki * k_decay, vi)
                return (kv_new, o_inter + o_intra)
            kv0 = jnp.zeros((b, h, d, d), dtype=jnp.float32)
            _, out = jax.lax.scan(step, kv0, (qb, kb, vb))
            out = out.transpose(1, 2, 0, 3, 4).reshape(b, h, n, d)
            out = out.transpose(0, 2, 1, 3).reshape(b, n, h * d)
            var = jnp.mean(out * out, axis=-1, keepdims=True)
            out = norm_w * (out * jax.lax.rsqrt(var + EPS))
            gate = jax.nn.sigmoid(jnp.einsum('bnf,of->bno', x, w_gate))
            return jnp.einsum('bno,fo->bnf', gate * out, w_out)
        return _lightning_attn(hidden_states, slope_rate, w_qkv, w_gate, w_out, norm_w)

    def _L0_ffn_ref(hidden_states, gate_w, w_gate_up, w_down, shared_gate_up, shared_down):
        import jax, jax.numpy as jnp
        import numpy as np
        H = 256
        I = 176
        E = 16
        K = 2
        SI = I * 2

        def _swiglu(gu, inter):
            g, u = (gu[..., :inter], gu[..., inter:])
            return jax.nn.silu(g) * u
        orig_shape = hidden_states.shape
        x = hidden_states.reshape(-1, H)
        logits = jnp.einsum('th,eh->te', x, gate_w)
        scores = jax.nn.softmax(logits, axis=-1)
        topk_w, topk_idx = jax.lax.top_k(scores, K)
        combine = jnp.sum(jax.nn.one_hot(topk_idx, E, dtype=x.dtype) * topk_w[..., None], axis=1)
        gu = jnp.einsum('th,ehj->etj', x, w_gate_up)
        h = _swiglu(gu, I)
        y = jnp.einsum('eti,eih,te->th', h, w_down, combine)
        gu_s = x @ shared_gate_up
        y = y + _swiglu(gu_s, SI) @ shared_down
        return y.reshape(orig_shape)

    def _L1_attn_ref(x, Wq, bq, Wk, bk, Wv, bv, Wo, bo):
        import jax, jax.numpy as jnp
        import numpy as np
        EMBED_DIM = 256
        NUM_HEADS = 16
        HEAD_DIM = EMBED_DIM // NUM_HEADS
        NUM_KV_GROUPS = 2
        WINDOW = 32
        KV_DIM = NUM_KV_GROUPS * HEAD_DIM
        B, L, C = x.shape
        W = WINDOW
        H, G, D = (NUM_HEADS, NUM_KV_GROUPS, HEAD_DIM)
        R = H // G
        pad_l = (W - L % W) % W
        xp = jnp.pad(x, ((0, 0), (0, pad_l), (0, 0)))
        Lp = xp.shape[1]
        q = (xp @ Wq + bq).reshape(B, Lp, H, D).transpose(0, 2, 1, 3)
        k = (xp @ Wk + bk).reshape(B, Lp, G, D).transpose(0, 2, 1, 3)
        v = (xp @ Wv + bv).reshape(B, Lp, G, D).transpose(0, 2, 1, 3)
        num_windows = (Lp - W) // (W // 2) + 1
        starts = jnp.arange(num_windows) * (W // 2)
        idx = starts[:, None] + jnp.arange(W)
        qw = q[:, :, idx, :]
        kw = k[:, :, idx, :]
        vw = v[:, :, idx, :]
        qg = qw.reshape(B, R, G, num_windows, W, D)
        scale = 1.0 / np.sqrt(D)
        scores = jnp.einsum('brgnqd,bgnkd->brgnqk', qg, kw) * scale
        attn = jax.nn.softmax(scores, axis=-1)
        og = jnp.einsum('brgnqk,bgnkd->brgnqd', attn, vw)
        o = og.reshape(B, H, num_windows, W, D)
        o = o.transpose(0, 2, 3, 1, 4).reshape(B, num_windows * W, H * D)
        o = o[:, :L, :]
        return o @ Wo + bo

    def _L1_ffn_ref(h_shard, w_gate_up, w_down):
        import jax, jax.numpy as jnp
        import numpy as np
        HIDDEN = 256
        INTER = 1024
        BATCH, LOCAL_SEQ = (2, 512)
        batch, local_seq, hidden = h_shard.shape
        gate_up = jnp.einsum('bsh,oh->bso', h_shard, w_gate_up)
        gate, up = jnp.split(gate_up, 2, axis=-1)
        h = jax.nn.silu(gate) * up
        out = jnp.einsum('bsi,hi->bsh', h, w_down)
        return out
    x = L0_attn_hidden_states
    x = x + _layernorm(_L0_attn_ref(_layernorm(x, axis=-1), L0_attn_slope_rate, L0_attn_w_qkv, L0_attn_w_gate, L0_attn_w_out, L0_attn_norm_w), axis=-1)
    x = x + _layernorm(_L0_ffn_ref(_layernorm(x, axis=-1), L0_ffn_gate_w, L0_ffn_w_gate_up, L0_ffn_w_down, L0_ffn_shared_gate_up, L0_ffn_shared_down), axis=-1)
    x = x + _layernorm(_L1_attn_ref(_layernorm(x, axis=-1), L1_attn_Wq, L1_attn_bq, L1_attn_Wk, L1_attn_bk, L1_attn_Wv, L1_attn_bv, L1_attn_Wo, L1_attn_bo), axis=-1)
    x = x + _layernorm(_L1_ffn_ref(_layernorm(x, axis=-1), L1_ffn_w_gate_up, L1_ffn_w_down), axis=-1)
    return x

_drawn_inputs = setup_inputs


def setup_inputs(seed=0):
    import zlib

    import numpy as np

    out = dict(_drawn_inputs(seed))
    spreads = {'L0_attn_norm_w': (1.0, 0.2),
     'L1_attn_bq': (0.0, 0.1),
     'L1_attn_bk': (0.0, 0.1),
     'L1_attn_bv': (0.0, 0.1),
     'L1_attn_bo': (0.0, 0.1)}
    factors = {}
    for name, (base, spread) in spreads.items():
        noise = np.random.default_rng([zlib.crc32(name.encode()), seed]).standard_normal(out[name].shape)
        drawn = base * np.exp(spread * noise) if base else spread * noise
        out[name] = jnp.asarray(drawn.astype(out[name].dtype))
    for name, factor in factors.items():
        out[name] = (out[name] * factor).astype(out[name].dtype)
    return out
```

```python
import numpy as np
import concourse.bass as bass
from concourse import mybir
from concourse.alu_op_type import AluOpType as ALU
from contextlib import ExitStack

F32 = mybir.dt.float32
F32R = mybir.dt.float32r
BF16 = mybir.dt.bfloat16
I32 = mybir.dt.int32
ACT = mybir.ActivationFunctionType
AX = mybir.AxisListType

P = 128
BATCH, SEQ, HID = 2, 1024, 256
TOK = BATCH * SEQ
TT = TOK // P
KT = HID // P
SEG = 512
SEGS = TOK // SEG
TPS = SEG // P

NH, HD = 16, 128
BLK = 32
RMS_EPS, LN_EPS = 1e-6, 1e-5
PAIRS = NH // 2
DMA = 16


def three_passes(nc, out, lhs, rhs, first=True, last=True, skip=False):
    (lh, ll), (rh, rl) = lhs, rhs
    nc.tensor.matmul(out, lh, rh, start=first, stop=False, skip_group_check=skip)
    nc.tensor.matmul(out, lh, rl, start=False, stop=False, skip_group_check=skip)
    return nc.tensor.matmul(out, ll, rh, start=False, stop=last, skip_group_check=skip)


class Keep:
    pass


class Scope:

    def __init__(self, nc, name):
        self.nc, self.name, self.stack, self.sems = nc, name, ExitStack(), []

    def __enter__(self):
        self.stack.__enter__()
        return self

    def __exit__(self, *a):
        numbers = sorted(s.num for s in self.sems)
        while numbers:
            n = 1
            while n < len(numbers) and numbers[n] == numbers[0] + n:
                n += 1
            self.nc.gpsimd.sem_clear(range(numbers[0], numbers[0] + n))
            numbers = numbers[n:]
        return self.stack.__exit__(*a)

    def sb(self, name, shape, dt=F32):
        return self.stack.enter_context(self.nc.sbuf_tensor(f"{self.name}_{name}", shape, dt))

    def banks(self, n, first=0):
        return [self.stack.enter_context(self.nc.psum_tensor(f"{self.name}_bank{i}", [P, SEG], F32)) for i in range(n)]

    def sem(self, name):
        self.sems.append(self.stack.enter_context(self.nc.semaphore(f"{self.name}_{name}")))
        return self.sems[-1]


class Chain:

    def __init__(self, eng, sem, base=0):
        self.eng, self.sem, self.base, self.n = eng, sem, base, 0

    def step(self, ins):
        self.n += 1
        ins.then_inc(self.sem, 1)

    def link(self, ins):
        self.step(ins)
        self.wait()

    def wait(self):
        self.eng.wait_ge(self.sem, self.base + self.n)


def constants(nc, keep, slope):
    with Scope(nc, "const") as c:
        slopes = c.sb("slopes", [P, NH])
        neg = c.sb("neg", [P, NH])
        ages = c.sb("ages", [P, P])
        rows = c.sb("rows", [P, P])
        cols = c.sb("cols", [P, 1])
        s_in, pool, dve, act = c.sem("slopes_in"), c.sem("pool"), c.sem("dve"), c.sem("act")
        with nc.Block() as block:
            @block.sync
            def _(sp):
                sp.dma_start(slopes[:], slope.rearrange("h a b -> (a b) h").broadcast_to([P, NH])).then_inc(s_in, DMA)

            @block.gpsimd
            def _(eng):
                chain = Chain(eng, pool)
                chain.step(eng.iota(ages[:], pattern=[[1, P]], base=0, channel_multiplier=-1, allow_small_or_imprecise_dtypes=True))
                chain.step(eng.iota(rows[:], pattern=[[1, P]], base=1, channel_multiplier=0, allow_small_or_imprecise_dtypes=True))
                chain.step(eng.iota(cols[:], pattern=[[0, 1]], base=P - 1, channel_multiplier=-1, allow_small_or_imprecise_dtypes=True))
                chain.link(eng.memset(keep.ident[:], 0.0))
                chain.step(eng.affine_select(out=keep.ident[:], in_=keep.ident[:], compare_op=ALU.not_equal, fill=1.0,
                                             base=0, pattern=[[-1, P]], channel_multiplier=1))
                eng.wait_ge(act, 2 * NH + 2)
                for h in range(NH):
                    chain.step(eng.affine_select(out=keep.decay_mask[:, h, :], in_=keep.decay_mask[:, h, :], compare_op=ALU.is_ge,
                                                 fill=0.0, base=0, pattern=[[1, P]], channel_multiplier=-1))

            @block.vector
            def _(eng):
                eng.wait_ge(s_in, DMA)
                eng.tensor_scalar(neg[:], slopes[:], -1.0, None, ALU.mult).then_inc(dve, 1)
                eng.wait_ge(pool, 3)
                eng.tensor_scalar(ages[:], ages[:], 0.0, None, ALU.max).then_inc(dve, 1)

            @block.scalar
            def _(eng):
                eng.wait_ge(pool, 3)
                eng.wait_ge(dve, 2)
                for h in range(NH):
                    s = neg[:, h:h + 1]
                    eng.activation(keep.decay_mask[:, h, :], ages[:], ACT.Exp, scale=s).then_inc(act, 1)
                    eng.activation(keep.query_decay[:, h, :], rows[:], ACT.Exp, scale=s).then_inc(act, 1)
                eng.activation(keep.key_decay[:], neg[:], ACT.Exp, scale=cols[:, 0:1]).then_inc(act, 1)
                eng.activation(keep.chunk_decay[:], neg[:], ACT.Exp, scale=float(P)).then_inc(act, 1)




def norm_stage(nc, keep, name, y=None, out=None, normed=None):
    sources = ["y"] * (y is not None) + ["x"] * (out is None)
    rounds = len(sources)
    steps = {"y": 2 * TPS + 3 + (out is None), "x": 2 * TPS + 3}
    steps_pass = sum(steps[s] for s in sources)
    tensor = {"y": y, "x": keep.x}
    with Scope(nc, name) as c:
        stats = c.sb("stats", [P, TPS, 6])
        mean_var = c.sb("mean_var", [P, TPS, 2])
        spread, root, scale, shift = (c.sb(n, [P, TPS]) for n in ("spread", "root", "scale", "shift"))
        z = c.sb("z", [P, TPS, HID])
        banks = c.banks(KT)
        own = c.sem("own")
        spread_ready, root_ready, affine_ready, z_ready = (c.sem(n) for n in ("spread", "root", "affine", "z"))
        turned, high_ready, low_ready, x_ready, stored = (c.sem(n) for n in ("turned", "high", "low", "x", "stored"))

        def tile(a, g, j):
            return a[:, bass.ds(g * TPS + j, 1), :].rearrange("p a f -> p (a f)")

        with nc.Block() as block:
            @block.vector
            def _(eng):
                with eng.Fori(0, SEGS) as g:
                    chain = Chain(eng, own, g * steps_pass)
                    for r, s in enumerate(sources):
                        n = g * rounds + r + 1
                        chain.step(eng.memset(spread[:, 0:2], LN_EPS))
                        for j in range(TPS):
                            chain.step(eng.bn_stats(stats[:, j, :], tile(tensor[s], g, j)))
                        chain.wait()
                        chain.step(eng.memset(spread[:, 2:4], LN_EPS))
                        for j in range(TPS):
                            chain.step(eng.bn_aggr(mean_var[:, j, :], stats[:, j, :]))
                        chain.wait()
                        eng.tensor_tensor(spread[:], spread[:], mean_var[:, :, 1], ALU.add).then_inc(spread_ready, 1)
                        eng.wait_ge(root_ready, n)
                        chain.link(eng.reciprocal(scale[:], root[:]))
                        eng.scalar_tensor_tensor(shift[:], mean_var[:, :, 0], -1.0, scale[:], ALU.mult, ALU.mult).then_inc(affine_ready, 1)
                        if s == "y":
                            eng.wait_ge(z_ready, n)
                            xs = keep.x[:, bass.ds(g * TPS, TPS), :]
                            if out is None:
                                chain.link(eng.tensor_tensor(xs, xs, z[:], ALU.add))
                            else:
                                eng.tensor_tensor(xs, xs, z[:], ALU.add).then_inc(x_ready, 1)
                        else:
                            for k in range(KT):
                                eng.wait_ge(high_ready, g * KT + k + 1)
                                at = keep.xT_hi[:, k, bass.ds(g * SEG, SEG)]
                                eng.tensor_tensor(keep.xT_lo[:, k, bass.ds(g * SEG, SEG)], banks[k][:], at.bitcast(F32),
                                                  ALU.subtract).then_inc(low_ready, 1)

            @block.scalar
            def _(eng):
                with eng.Fori(0, SEGS) as g:
                    for r, s in enumerate(sources):
                        n = g * rounds + r + 1
                        eng.wait_ge(spread_ready, n)
                        eng.activation(root[:], spread[:], ACT.Sqrt).then_inc(root_ready, 1)
                        eng.wait_ge(affine_ready, n)
                        for j in range(TPS):
                            last = eng.activation(z[:, j, :], tile(tensor[s], g, j), ACT.Identity,
                                                  scale=scale[:, j:j + 1], bias=shift[:, j:j + 1])
                        last.then_inc(z_ready, 1)
                        if s == "x":
                            for k in range(KT):
                                eng.wait_ge(turned, g * KT + k + 1)
                                eng.activation(keep.xT_hi[:, k, bass.ds(g * SEG, SEG)], banks[k][:], ACT.Copy).then_inc(high_ready, 1)
                            if normed is not None:
                                eng.wait_ge(stored, g * DMA + DMA)

            if out is None:
                @block.tensor
                def _(eng):
                    with eng.Fori(0, SEGS) as g:
                        eng.wait_ge(z_ready, g * rounds + rounds)
                        for k in range(KT):
                            for j in range(TPS):
                                last = eng.transpose(banks[k][:, j * P:(j + 1) * P], z[:, j, k * P:(k + 1) * P], keep.ident[:])
                            last.then_inc(turned, 1)
            if normed is not None:
                @block.sync
                def _(sp):
                    with sp.Fori(0, SEGS) as g:
                        sp.wait_ge(z_ready, g * rounds + rounds)
                        sp.dma_start(normed[:, bass.ds(g * TPS, TPS), :], z[:]).then_inc(stored, DMA)
                    sp.wait_ge(stored, SEGS * DMA)
            if out is not None:
                @block.sync
                def _(sp):
                    with sp.Fori(0, SEGS) as g:
                        sp.wait_ge(x_ready, g + 1)
                        sp.dma_start(out[:, bass.ds(g * TPS, TPS), :], keep.x[:, bass.ds(g * TPS, TPS), :]).then_inc(stored, DMA)
                    sp.wait_ge(stored, SEGS * DMA)


def linear_attention(nc, keep, w_pairs, wout_pairs, norm_w):
    with Scope(nc, "lin") as c:
        raw = c.sb("raw", [P, KT, 1024])
        w_hi, w_lo = c.sb("w_hi", [P, KT, 1024], F32R), c.sb("w_lo", [P, KT, 1024], F32R)
        raw_out = c.sb("raw_out", [P, 2, HID])
        wo_hi, wo_lo = c.sb("wo_hi", [P, 2, HID], F32R), c.sb("wo_lo", [P, 2, HID], F32R)
        norm_in = c.sb("norm_in", [P, NH])
        two = lambda n, dt=F32: c.sb(n, [P, 2, SEG], dt)
        q, k, kd, o, th, sq, qd, st, g = (two(n) for n in ("q", "k", "kd", "o", "th", "sq", "qd", "st", "g"))
        g_hi, g_lo = two("g_hi", F32R), two("g_lo", F32R)
        v = c.sb("v", [P, TPS, 2, HD])
        state = c.sb("state", [P, 2, TPS, HD])
        mask, q_dec = c.sb("mask", [P, 2, P]), c.sb("q_dec", [P, 2, P])
        k_dec, c_dec, half_norm = c.sb("k_dec", [P, 2]), c.sb("c_dec", [P, 2]), c.sb("half_norm", [P, 2])
        bank = c.banks(8)
        sem = c.sem
        raw_in, raw_out_in, norm_sem = sem("raw_in"), sem("raw_out_in"), sem("norm_in")
        w_hi_done, w_lo_done, wo_done, wo_hi_done = sem("w_hi"), sem("w_lo"), sem("wo"), sem("wo_hi")
        q_mm, k_mm, v_mm, g_mm, t_mm, s_mm, d_mm, o_mm, w_mm = (sem(n + "_mm") for n in "qkvgtsdow")
        q_sb, k_sb, v_sb, th_sb, kd_sb, o_sb, sq_sb = (sem(n + "_sb") for n in ("q", "k", "v", "th", "kd", "o", "sq"))
        qd_sb, st_sb, state_sb, g_sb, acc_sb, squares_sb = (sem(n + "_sb") for n in ("qd", "st", "state", "g", "acc", "squares"))
        heads_sb, own, zeroed = sem("heads"), sem("own"), sem("zeroed")
        C4 = lambda ap: ap.rearrange("p (c i) -> p c i", c=TPS)

        def states(t, seg, a, n):
            hp28 = (t - seg) // 4 * 28 if isinstance(t, int) else None
            base = hp28 if hp28 is not None else (t - seg) * 7
            return base + (0, 8, 14, 22)[seg] + a * (4 - seg % 2) + n

        def n_states(seg):
            return 4 - seg % 2

        COL = {("q", 0): 0, ("k", 0): 1, ("q", 1): 2, ("k", 1): 3, ("g", 0): 4, ("g", 1): 5}

        def pe_pass(pe, hp, first):
            def project(job, a, to, seg):
                cols = slice(COL[job, a] * P, (COL[job, a] + 1) * P)
                toks = slice(seg * SEG, (seg + 1) * SEG)
                for f in range(KT):
                    last = three_passes(nc, to[:], (w_hi[:, f, cols], w_lo[:, f, cols]),
                                        (keep.xT_hi[:, f, toks], keep.xT_lo[:, f, toks]), f == 0, f == KT - 1)
                return last

            pe.wait_ge(w_hi_done, 2 * hp + 2)
            pe.wait_ge(w_lo_done, 2 * hp + 2)
            for seg in range(SEGS):
                t = 4 * hp + seg
                start = first and seg == 0
                if not start:
                    pe.wait_ge(o_sb, 2 * t - 1)
                project("q", 0, bank[0], seg).then_inc(q_mm, 1)
                if not start:
                    pe.wait_ge(o_sb, 2 * t)
                project("k", 0, bank[1], seg).then_inc(k_mm, 1)
                if not start:
                    pe.wait_ge(st_sb, 2 * t - 1)
                project("q", 1, bank[2], seg).then_inc(q_mm, 1)
                if not start:
                    pe.wait_ge(st_sb, 2 * t)
                project("k", 1, bank[3], seg).then_inc(k_mm, 1)
                for b in range(2):
                    if not (first and seg <= 1):
                        pe.wait_ge(acc_sb, 2 * t - 3 + b)
                    for j in range(2):
                        toks = slice(seg * SEG + (2 * b + j) * P, seg * SEG + (2 * b + j + 1) * P)
                        for f in range(KT):
                            last = three_passes(nc, bank[4 + b][:, j * HID:(j + 1) * HID],
                                                (keep.xT_hi[:, f, toks], keep.xT_lo[:, f, toks]),
                                                (w_hi[:, f, 768:1024], w_lo[:, f, 768:1024]), f == 0, f == KT - 1)
                    last.then_inc(v_mm, 1)
                for a in range(2):
                    if not start:
                        s1 = (seg - 1) % SEGS
                        pe.wait_ge(state_sb, states(t - 1, s1, a, n_states(s1)))
                    project("g", a, bank[6 + a], seg).then_inc(g_mm, 1)
                for a in range(2):
                    pe.wait_ge(k_sb, 2 * t + 1 + a)
                    pe.wait_ge(q_sb, 2 * t + 1)
                    for j in range(TPS):
                        last = pe.transpose(bank[a][:, j * P:(j + 1) * P], k[:, a, j * P:(j + 1) * P], keep.ident[:])
                    last.then_inc(t_mm, 1)
                for a in range(2):
                    pe.wait_ge(q_sb, 2 * t + 2)
                    pe.wait_ge(k_sb, 2 * t + 2)
                    for j in range(TPS):
                        cols = slice(j * P, (j + 1) * P)
                        last = pe.matmul(bank[2 + a][:, cols], k[:, a, cols], q[:, a, cols], start=True, stop=True)
                    last.then_inc(s_mm, 1)
                if not start:
                    if seg == 1:
                        pe.wait_ge(wo_done, 2 * hp + 2)
                    out_projection(pe, t - 1, 2 * t + 2)
                for a in range(2):
                    pe.wait_ge(th_sb, 2 * t + 1 + a)
                    pe.wait_ge(kd_sb, 2 * t + 1 + a)
                    pe.wait_ge(v_sb, 2 * t + 2)
                    for j in range(TPS):
                        last = pe.matmul(bank[6 + a][:, j * P:(j + 1) * P], kd[:, a, j * P:(j + 1) * P], v[:, j, a, :], start=True, stop=True)
                    last.then_inc(d_mm, 1)
                for a in range(2):
                    pe.wait_ge(st_sb, 2 * t + 1 + a)
                    pe.wait_ge(qd_sb, 2 * t + 1 + a)
                    pe.wait_ge(kd_sb, 2 * t + 1 + a)
                    for j in range(TPS):
                        cols = slice(j * P, (j + 1) * P)
                        fresh = seg % 2 == 0 and j == 0
                        last = pe.matmul(bank[a][:, cols], v[:, j, a, :], st[:, a, cols], start=True, stop=fresh)
                        if not fresh:
                            if j:
                                pe.wait_ge(state_sb, states(t, seg, a, j))
                            last = pe.matmul(bank[a][:, cols], state[:, a, j, :], qd[:, a, cols], start=False, stop=True)
                    last.then_inc(o_mm, 1)

        def out_projection(pe, t, v_count):
            pe.wait_ge(v_sb, v_count)
            pe.wait_ge(g_sb, 2 * t + 2)
            for f in range(KT):
                for a in range(2):
                    last = three_passes(nc, bank[4 + f][:], (wo_hi[:, a, f * P:(f + 1) * P], wo_lo[:, a, f * P:(f + 1) * P]),
                                        (g_hi[:, a, :], g_lo[:, a, :]), a == 0, a == 1)
                last.then_inc(w_mm, 1)

        def act_split(act, hp):
            act.wait_ge(raw_in, DMA * (hp + 1))
            for f in range(KT):
                act.activation(w_hi[:, f, :], raw[:, f, :], ACT.Copy).then_inc(w_hi_done, 1)

        def act_pass(act, hp, first, last):
            for seg in range(SEGS):
                t = 4 * hp + seg
                start = first and seg == 0
                for a in range(2):
                    act.wait_ge(q_mm, 2 * t + 1 + a)
                    if not start:
                        act.wait_ge(qd_sb, 2 * t - 1 + a)
                    act.activation(q[:, a, :], bank[2 * a][:], ACT.Silu).then_inc(q_sb, 1)
                    act.wait_ge(k_mm, 2 * t + 1 + a)
                    act.activation(k[:, a, :], bank[2 * a + 1][:], ACT.Silu).then_inc(k_sb, 1)
                for b in range(2):
                    act.wait_ge(v_mm, 2 * t + 1 + b)
                    act.activation(v[:, 2 * b:2 * b + 2, :, :].rearrange("p c a e -> p (c a e)"), bank[4 + b][:], ACT.Silu).then_inc(v_sb, 1)
                for a in range(2):
                    act.wait_ge(g_mm, 2 * t + 1 + a)
                    if not start:
                        act.wait_ge(g_sb, 2 * t - 1 + a)
                    act.activation(th[:, a, :], bank[6 + a][:], ACT.Tanh, scale=0.5).then_inc(th_sb, 1)
                if seg == SEGS - 1 and not last:
                    act_split(act, hp + 1)
                if seg == 0:
                    act.wait_ge(heads_sb, hp + 1)
                for a in range(2):
                    act.wait_ge(t_mm, 2 * t + 1 + a)
                    act.activation(kd[:, a, :], bank[a][:], ACT.Copy, scale=k_dec[:, a:a + 1]).then_inc(kd_sb, 1)
                for a in range(2):
                    act.wait_ge(o_mm, 2 * t + 1 + a)
                    act.activation(o[:, a, :], bank[a][:], ACT.Copy).then_inc(o_sb, 1)
                    act.wait_ge(o_sb, 2 * t + 1 + a)
                    if not start:
                        act.wait_ge(squares_sb, 2 * t - 1 + a)
                    act.activation(sq[:, a, :], o[:, a, :], ACT.Square).then_inc(sq_sb, 1)

        def gate(dve, chain, t):
            for a in range(2):
                dve.wait_ge(o_sb, 2 * t + 1 + a)
                dve.wait_ge(th_sb, 2 * t + 1 + a)
                chain.link(dve.tensor_scalar(g[:, a, :], th[:, a, :], 1.0, half_norm[:, a:a + 1], ALU.add, ALU.mult))
                chain.link(dve.tensor_tensor(g[:, a, :], g[:, a, :], o[:, a, :], ALU.mult))
                chain.link(dve.tensor_copy(g_hi[:, a, :], g[:, a, :]))
                dve.tensor_tensor(g_lo[:, a, :], g[:, a, :], g_hi[:, a, :].bitcast(F32), ALU.subtract).then_inc(g_sb, 1)

        def dve_split(dve, hp):
            for f in range(KT):
                dve.wait_ge(w_hi_done, 2 * hp + 1 + f)
                dve.tensor_tensor(w_lo[:, f, :], raw[:, f, :], w_hi[:, f, :].bitcast(F32), ALU.subtract).then_inc(w_lo_done, 1)

        def accumulate(dve, t, seg):
            for f in range(KT):
                dve.wait_ge(w_mm, 2 * t + 1 + f)
                part = keep.acc[:, f, seg * SEG:(seg + 1) * SEG]
                dve.tensor_tensor(part, part, bank[4 + f][:], ALU.add).then_inc(acc_sb, 1)

        def dve_pass(dve, hp, first, last, chain):
            for seg in range(SEGS):
                t = 4 * hp + seg
                start = first and seg == 0
                if not start:
                    gate(dve, chain, t - 1)
                if seg == 0:
                    two = bass.ds(2 * hp, 2)
                    chain.step(dve.tensor_copy(mask[:], keep.decay_mask[:, two, :]))
                    chain.step(dve.tensor_copy(q_dec[:], keep.query_decay[:, two, :]))
                    chain.step(dve.tensor_copy(k_dec[:], keep.key_decay[:, two]))
                    chain.step(dve.tensor_copy(c_dec[:], keep.chunk_decay[:, two]))
                    dve.tensor_scalar(half_norm[:], norm_in[:, two], 0.5, None, ALU.mult).then_inc(heads_sb, 1)
                    dve.wait_ge(heads_sb, hp + 1)
                for a in range(2):
                    dve.wait_ge(q_sb, 2 * t + 1 + a)
                    dve.tensor_tensor(C4(qd[:, a, :]), C4(q[:, a, :]), q_dec[:, a:a + 1, :].broadcast_to([P, TPS, P]),
                                      ALU.mult).then_inc(qd_sb, 1)
                for a in range(2):
                    dve.wait_ge(s_mm, 2 * t + 1 + a)
                    dve.tensor_tensor(C4(st[:, a, :]), C4(bank[2 + a][:]), mask[:, a:a + 1, :].broadcast_to([P, TPS, P]),
                                      ALU.mult).then_inc(st_sb, 1)
                if seg == SEGS - 1 and not last:
                    dve_split(dve, hp + 1)
                if not start:
                    accumulate(dve, t - 1, (seg - 1) % SEGS)
                if seg == 0:
                    dve.wait_ge(raw_out_in, DMA * (hp + 1))
                    dve.tensor_copy(wo_hi[:], raw_out[:]).then_inc(wo_done, 1)
                    dve.wait_ge(wo_done, 2 * hp + 1)
                    dve.tensor_tensor(wo_lo[:], raw_out[:], wo_hi[:].bitcast(F32), ALU.subtract).then_inc(wo_done, 1)
                for a in range(2):
                    dve.wait_ge(d_mm, 2 * t + 1 + a)
                    for j in range(n_states(seg)):
                        grown = bank[6 + a][:, j * P:(j + 1) * P]
                        new = state[:, a, (j + 1) % TPS, :]
                        if seg % 2 == 0 and j == 0:
                            dve.tensor_copy(new, grown).then_inc(state_sb, 1)
                        else:
                            dve.wait_ge(state_sb, states(t, seg, a, j) if j else states(t - 1, seg - 1, a, n_states(seg - 1)))
                            dve.scalar_tensor_tensor(new, state[:, a, j, :], c_dec[:, a:a + 1], grown, ALU.mult, ALU.add).then_inc(state_sb, 1)

        def pool_pass(pool, hp):
            for seg in range(SEGS):
                part = keep.squares[:, seg * SEG:(seg + 1) * SEG]
                for a in range(2):
                    n = 2 * (4 * hp + seg) + a
                    pool.wait_ge(sq_sb, n + 1)
                    if a:
                        pool.wait_ge(squares_sb, n)
                    pool.tensor_tensor(part, part, sq[:, a, :], ALU.add).then_inc(squares_sb, 1)

        STEPS_FIRST, STEPS = 1 + 4 + 6 * (SEGS - 1), 4 + 6 * SEGS
        with nc.Block() as block:
            @block.sync
            def _(sp):
                sp.dma_start(raw[:], w_pairs[0]).then_inc(raw_in, DMA)
                sp.dma_start(norm_in[:], norm_w).then_inc(norm_sem, DMA)
                sp.dma_start(raw_out[:], wout_pairs[0]).then_inc(raw_out_in, DMA)
                with sp.Fori(0, PAIRS - 1) as hp:
                    sp.wait_ge(w_lo_done, 2 * hp + 2)
                    sp.dma_start(raw[:], w_pairs[bass.ds(hp + 1, 1)].rearrange("a p k n -> (a p) k n")).then_inc(raw_in, DMA)
                    sp.wait_ge(wo_done, 2 * hp + 2)
                    sp.dma_start(raw_out[:], wout_pairs[bass.ds(hp + 1, 1)].rearrange("a p k n -> (a p) k n")).then_inc(raw_out_in, DMA)

            @block.gpsimd
            def _(pool):
                pool.memset(keep.squares[:], 0.0).then_inc(zeroed, 1)
                pool.wait_ge(zeroed, 1)
                with pool.Fori(0, PAIRS) as hp:
                    pool_pass(pool, hp)

            @block.vector
            def _(dve):
                chain = Chain(dve, own)
                chain.link(dve.memset(keep.acc[:], 0.0))
                dve.wait_ge(norm_sem, DMA)
                dve_split(dve, 0)
                dve_pass(dve, 0, True, False, chain)
                assert chain.n == STEPS_FIRST
                with dve.Fori(1, PAIRS - 1) as hp:
                    chain = Chain(dve, own, (hp - 1) * STEPS + STEPS_FIRST)
                    dve_pass(dve, hp, False, False, chain)
                    assert chain.n == STEPS
                chain = Chain(dve, own, (PAIRS - 2) * STEPS + STEPS_FIRST)
                dve_pass(dve, PAIRS - 1, False, True, chain)
                gate(dve, chain, 4 * PAIRS - 1)
                accumulate(dve, 4 * PAIRS - 1, SEGS - 1)

            @block.scalar
            def _(act):
                act_split(act, 0)
                act_pass(act, 0, True, False)
                with act.Fori(1, PAIRS - 1) as hp:
                    act_pass(act, hp, False, False)
                act_pass(act, PAIRS - 1, False, True)

            @block.tensor
            def _(pe):
                pe_pass(pe, 0, True)
                with pe.Fori(1, PAIRS) as hp:
                    pe_pass(pe, hp, False)
                out_projection(pe, 4 * PAIRS - 1, 8 * PAIRS)


def rms_to_tokens(nc, keep, y):
    with Scope(nc, "rms") as c:
        ones = c.sb("ones", [P, 2])
        spread, root, factor = (c.sb(n, [P, TT]) for n in ("spread", "root", "factor"))
        bank = c.banks(5)
        ones_ready, sums, spread_ready, root_ready, factor_ready, turned, y_ready = (
            c.sem(n) for n in ("ones", "sums", "spread", "root", "factor", "turned", "y"))
        with nc.Block() as block:
            @block.vector
            def _(dve):
                dve.memset(ones[:], 1.0).then_inc(ones_ready, 1)
                dve.wait_ge(sums, 1)
                dve.tensor_scalar(spread[:], bank[4][:, 0:2 * TT].rearrange("p (t a) -> p t a", a=2)[:, :, 0],
                                  1.0 / (NH * HD), RMS_EPS, ALU.mult, ALU.add).then_inc(spread_ready, 1)
                dve.wait_ge(root_ready, 1)
                dve.reciprocal(factor[:], root[:]).then_inc(factor_ready, 1)

            @block.tensor
            def _(pe):
                pe.wait_ge(ones_ready, 1)
                for t in range(TT):
                    last = pe.matmul(bank[4][:, 2 * t:2 * t + 2], keep.squares[:, t * P:(t + 1) * P], ones[:], start=True, stop=True)
                last.then_inc(sums, 1)
                for t in range(TT):
                    to = bank[t // 2 % 4]
                    if t >= 8 and t % 2 == 0:
                        pe.wait_ge(y_ready, t - 6)
                    for f in range(KT):
                        last = pe.transpose(to[:, t % 2 * HID + f * P:t % 2 * HID + (f + 1) * P], keep.acc[:, f, t * P:(t + 1) * P], keep.ident[:])
                    last.then_inc(turned, 1)

            @block.scalar
            def _(act):
                act.wait_ge(spread_ready, 1)
                act.activation(root[:], spread[:], ACT.Sqrt).then_inc(root_ready, 1)
                act.wait_ge(factor_ready, 1)
                for t in range(TT):
                    act.wait_ge(turned, min(t // 2 * 2 + 2, TT))
                    act.activation(y[:, t, :], bank[t // 2 % 4][:, t % 2 * HID:(t % 2 + 1) * HID], ACT.Copy,
                                   scale=factor[:, t:t + 1]).then_inc(y_ready, 1)


def allocate(nc, keep, c):
    keep.x = c.sb("x", [P, TT, HID])
    keep.xT_hi = c.sb("xT_hi", [P, KT, TOK], F32R)
    keep.xT_lo = c.sb("xT_lo", [P, KT, TOK], F32R)
    keep.ident = c.sb("ident", [P, P])


def load_x(nc, keep, x):
    with Scope(nc, "load") as c:
        loaded = c.sem("x")
        with nc.Block() as block:
            @block.sync
            def _(sp):
                sp.dma_start(keep.x[:], x.rearrange("b (t p) f -> p (b t) f", p=P)).then_inc(loaded, DMA)
                sp.wait_ge(loaded, DMA)


def lay_out_linear(w_qkv, w_gate, w_out, norm_w):
    qkv = w_qkv.reshape(PAIRS, 2, 3, HD, KT, P)
    gate = w_gate.reshape(PAIRS, 2, HD, KT, P)
    blocks = [qkv[:, 0, 0], qkv[:, 0, 1], qkv[:, 1, 0], qkv[:, 1, 1], gate[:, 0], gate[:, 1], qkv[:, 0, 2], qkv[:, 1, 2]]
    w = np.stack(blocks, 1)
    w = w.transpose(0, 4, 3, 1, 2).reshape(PAIRS, P, KT, 8 * HD)
    wo = w_out.reshape(HID, PAIRS, 2, HD).transpose(1, 3, 2, 0)
    return {"wp": np.ascontiguousarray(w), "wop": np.ascontiguousarray(wo), "nw": np.ascontiguousarray(norm_w.reshape(NH, HD).T)}


def swiglu(nc, keep, name, y, w_up, w_down, widths):
    J, W = len(widths), sum(widths)
    starts = [sum(widths[:j]) for j in range(J)]
    with Scope(nc, name) as c:
        raw, w_hi, w_lo = c.sb("raw", [P, KT, 2 * W]), c.sb("w_hi", [P, KT, 2 * W], F32R), c.sb("w_lo", [P, KT, 2 * W], F32R)
        raw_d, d_hi, d_lo = c.sb("raw_d", [P, J, HID]), c.sb("d_hi", [P, J, HID], F32R), c.sb("d_lo", [P, J, HID], F32R)
        silu, h = c.sb("silu", [P, 2, SEG]), c.sb("h", [P, 2, SEG])
        h_hi, h_lo = c.sb("h_hi", [P, 2, SEG], F32R), c.sb("h_lo", [P, 2, SEG], F32R)
        bank = c.banks(8)
        up_in, down_in, up_hi, down_hi, up_lo, down_lo = (c.sem(n) for n in ("up_in", "down_in", "up_hi", "down_hi", "up_lo", "down_lo"))
        g_mm, u_mm, down_mm, silu_sb, h_own, h_sb, y_sb = (c.sem(n) for n in ("g_mm", "u_mm", "down_mm", "silu", "h_own", "h", "y"))
        steps = [(s, j) for s in range(2) for j in range(J)]

        with nc.Block() as block:
            @block.sync
            def _(sp):
                for f in range(KT):
                    sp.dma_start(raw[:, f, :], w_up[f * P:(f + 1) * P, :]).then_inc(up_in, DMA)
                for j in range(J):
                    sp.dma_start(raw_d[0:widths[j], j, :], w_down[starts[j]:starts[j] + widths[j], :]).then_inc(down_in, DMA)

            def columns(j):
                return [slice(b + starts[j], b + starts[j] + widths[j]) for b in (0, W)]

            @block.scalar
            def _(act):
                act.wait_ge(up_in, KT * DMA)
                for j in range(J):
                    for cols in columns(j):
                        act.activation(w_hi[:, :, cols], raw[:, :, cols], ACT.Copy).then_inc(up_hi, 1)
                act.wait_ge(down_in, J * DMA)
                for j in range(J):
                    act.activation(d_hi[0:widths[j], j, :], raw_d[0:widths[j], j, :], ACT.Copy).then_inc(down_hi, 1)
                with act.Fori(0, SEGS // 2) as half:
                    for s, j in steps:
                        n, b, w = (2 * half + s) * J + j, (s * J + j) % 2, widths[j]
                        act.wait_ge(g_mm, n + 1)
                        if s or j > 1:
                            act.wait_ge(h_sb, n - 1)
                        act.activation(silu[0:w, b, :], bank[b][0:w, :], ACT.Silu).then_inc(silu_sb, 1)
                        if j == J - 1:
                            seg = 2 * half + s
                            act.wait_ge(down_mm, seg * J + J)
                            for i in range(2):
                                act.activation(y[:, bass.ds(seg * TPS + 2 * i, 2), :].rearrange("p t f -> p (t f)"), bank[4 + 2 * s + i][:],
                                               ACT.Copy).then_inc(y_sb, 1)

            @block.vector
            def _(dve):
                for j in range(J):
                    for i, cols in enumerate(columns(j)):
                        dve.wait_ge(up_hi, 2 * j + i + 1)
                        dve.tensor_tensor(w_lo[:, :, cols], raw[:, :, cols], w_hi[:, :, cols].bitcast(F32), ALU.subtract).then_inc(up_lo, 1)
                for j in range(J):
                    w = widths[j]
                    dve.wait_ge(down_hi, j + 1)
                    dve.tensor_tensor(d_lo[0:w, j, :], raw_d[0:w, j, :], d_hi[0:w, j, :].bitcast(F32), ALU.subtract).then_inc(down_lo, 1)
                with dve.Fori(0, SEGS // 2) as half:
                    for s, j in steps:
                        n, b, w = (2 * half + s) * J + j, (s * J + j) % 2, widths[j]
                        chain = Chain(dve, h_own, 2 * n)
                        dve.wait_ge(silu_sb, n + 1)
                        dve.wait_ge(u_mm, n + 1)
                        chain.link(dve.tensor_tensor(h[0:w, b, :], silu[0:w, b, :], bank[2 + b][0:w, :], ALU.mult))
                        if s or j > 1:
                            dve.wait_ge(down_mm, n - 1)
                        chain.link(dve.tensor_copy(h_hi[0:w, b, :], h[0:w, b, :]))
                        dve.tensor_tensor(h_lo[0:w, b, :], h[0:w, b, :], h_hi[0:w, b, :].bitcast(F32), ALU.subtract).then_inc(h_sb, 1)

            @block.tensor
            def _(pe):
                def down(half, s, j):
                    n, b, w = (2 * half + s) * J + j, (s * J + j) % 2, widths[j]
                    pe.wait_ge(h_sb, n + 1)
                    for t in range(TPS):
                        to = bank[4 + 2 * s + t // 2][:, t % 2 * HID:(t % 2 + 1) * HID]
                        toks = slice(t * P, (t + 1) * P)
                        last = three_passes(nc, to, (h_hi[0:w, b, toks], h_lo[0:w, b, toks]), (d_hi[0:w, j, :], d_lo[0:w, j, :]),
                                            j == 0 and t % 2 == 0, j == J - 1, skip=True)
                    last.then_inc(down_mm, 1)

                pe.wait_ge(up_lo, 2 * J)
                pe.wait_ge(down_lo, J)
                with pe.Fori(0, SEGS // 2) as half:
                    for s, j in steps:
                        n, b, w = (2 * half + s) * J + j, (s * J + j) % 2, widths[j]
                        toks = bass.ds((2 * half + s) * SEG, SEG)
                        if s or j > 1:
                            pe.wait_ge(h_sb, n - 1)
                        for cols, to, sem in zip(columns(j), (bank[b], bank[2 + b]), (g_mm, u_mm)):
                            for f in range(KT):
                                last = three_passes(nc, to[0:w, :], (w_hi[:, f, cols], w_lo[:, f, cols]),
                                                    (keep.xT_hi[:, f, toks], keep.xT_lo[:, f, toks]), f == 0, f == KT - 1)
                            last.then_inc(sem, 1)
                        if j:
                            down(half, s, j - 1)
                        if j == J - 1:
                            down(half, s, j)


def ident(nc, keep):
    with Scope(nc, "ident") as c:
        done = c.sem("done")
        with nc.Block() as block:
            @block.gpsimd
            def _(pool):
                pool.memset(keep.ident[:], 0.0).then_inc(done, 1)
                pool.wait_ge(done, 1)
                pool.affine_select(out=keep.ident[:], in_=keep.ident[:], compare_op=ALU.not_equal, fill=1.0,
                                   base=0, pattern=[[-1, P]], channel_multiplier=1)


NE, TOP, INNER = 16, 2, 176
IH = INNER // 2
SLOT_TILES = (TOP * TOK + NE * (P - 1)) // P
SLOT_TILES += SLOT_TILES % 2
SLOTS = SLOT_TILES * P


def route(nc, keep, gate_w, sorted_x, normed):
    with Scope(nc, "route") as c:
        gate, g_hi, g_lo = c.sb("gate", [P, KT, P]), c.sb("g_hi", [P, KT, P], F32R), c.sb("g_lo", [P, KT, P], F32R)
        logits_T = c.sb("logits_T", [NE, TOK])
        full = lambda n, dt=F32: c.sb(n, [P, TT, NE], dt)
        score, key, rest, one1, one2 = (full(n) for n in ("score", "key", "rest", "one1", "one2"))
        per_token = lambda n: c.sb(n, [P, TT])
        top, total, best = (per_token(n) for n in ("top", "total", "best"))
        where = c.sb("where", [P, TT])
        chosen = full("chosen", BF16)
        before, every = c.sb("before", [P, P], BF16), c.sb("every", [P, P], BF16)
        rank_first, thresholds = c.sb("rank_first", [P, NE]), c.sb("thresholds", [P, NE])
        upto = c.sb("upto", [P, NE, NE])
        counts_over, tiles, tiles_to, base = c.sb("counts_over", [P, NE, NE]), c.sb("tiles", [P, NE]), c.sb("tiles_to", [P, NE]), c.sb("base", [P, NE])
        tile_no, passed, expert_f = c.sb("tile_no", [1, SLOT_TILES]), c.sb("passed", [1, SLOT_TILES, NE]), c.sb("expert_f", [1, SLOT_TILES])
        bank = c.banks(7)
        zeroed, gate_in, gate_hi, gate_lo, made, logits_mm, logits_sb, logits_T_mm = (
            c.sem(n) for n in ("zeroed", "gate_in", "gate_hi", "gate_lo", "made", "logits_mm", "logits_sb", "logits_T_mm"))
        own, shifted, exps, chosen_ready, ranks, scattered, slots_ready = (
            c.sem(n) for n in ("own", "shifted", "exps", "chosen_ready", "ranks", "scattered", "slots"))
        over_e = lambda a: a.rearrange("p (t o) -> p t o", o=1).broadcast_to([P, TT, NE])
        over_t = lambda a: a.rearrange("p (o e) -> p o e", o=1).broadcast_to([P, TT, NE])
        with nc.Block() as block:
            @block.sync
            def _(sp):
                sp.wait_ge(zeroed, 1)
                sp.dma_start(gate[:, :, 0:NE], gate_w).then_inc(gate_in, DMA)

            @block.gpsimd
            def _(pool):
                iota = lambda out, pattern, base, mult: pool.iota(out, pattern=pattern, base=base, channel_multiplier=mult,
                                                                  allow_small_or_imprecise_dtypes=True).then_inc(made, 1)
                iota(rank_first[:], [[-1, NE]], NE, 0)
                iota(thresholds[:], [[P, NE]], 0, 0)
                iota(tile_no[:], [[1, SLOT_TILES]], 0, 0)
                pool.memset(upto[:], 1.0).then_inc(made, 1)
                pool.memset(before[:], 1.0).then_inc(made, 1)
                pool.memset(every[:], 1.0).then_inc(made, 1)
                pool.wait_ge(made, 6)
                pool.affine_select(out=upto[:], in_=upto[:], compare_op=ALU.is_ge, fill=0.0, base=0,
                                   pattern=[[1, NE], [-1, NE]], channel_multiplier=0).then_inc(made, 1)
                pool.affine_select(out=before[:], in_=before[:], compare_op=ALU.is_gt, fill=0.0, base=0,
                                   pattern=[[1, P]], channel_multiplier=-1).then_inc(made, 1)
                pool.wait_ge(slots_ready, 1)
                for t in range(TT):
                    for slot in (keep.slot1, keep.slot2):
                        pool.indirect_dma_start(out=sorted_x, out_offset=bass.IndirectOffsetOnAxis(ap=slot[:, t:t + 1], axis=0),
                                                in_=normed[:, t, :], in_offset=None).then_inc(scattered, DMA)
                pool.wait_ge(scattered, 2 * TT * DMA)

            @block.tensor
            def _(pe):
                pe.wait_ge(gate_lo, 1)
                for seg in range(SEGS):
                    toks = slice(seg * SEG, (seg + 1) * SEG)
                    for f in range(KT):
                        last = three_passes(nc, bank[seg][:], (g_hi[:, f, :], g_lo[:, f, :]),
                                            (keep.xT_hi[:, f, toks], keep.xT_lo[:, f, toks]), f == 0, f == KT - 1)
                    last.then_inc(logits_mm, 1)
                for t in range(TT):
                    pe.wait_ge(logits_sb, t // TPS + 1)
                    last = pe.transpose(bank[4][:, t * NE:(t + 1) * NE], logits_T[:, t * P:(t + 1) * P], keep.ident[0:NE, 0:NE])
                last.then_inc(logits_T_mm, 1)
                pe.wait_ge(chosen_ready, 1)
                pe.wait_ge(made, 8)
                pe.matmul(bank[5][:, 0:TT * NE], before[:], chosen[:].rearrange("p t e -> p (t e)"), start=True, stop=False, skip_group_check=True)
                for t in range(TT - 1):
                    later = TT - 1 - t
                    pe.matmul(bank[5][:, (t + 1) * NE:TT * NE].rearrange("p (t e) -> p t e", e=NE), every[:],
                              chosen[:, t:t + 1, :].broadcast_to([P, later, NE]), start=False, stop=t == TT - 2, skip_group_check=True)
                for t in range(TT):
                    last = pe.matmul(bank[6][:, 0:NE], every[:], chosen[:, t, :], start=t == 0, stop=t == TT - 1)
                last.then_inc(ranks, 1)

            @block.scalar
            def _(act):
                act.wait_ge(gate_in, DMA)
                act.activation(g_hi[:], gate[:], ACT.Copy).then_inc(gate_hi, 1)
                for seg in range(SEGS):
                    act.wait_ge(logits_mm, seg + 1)
                    act.activation(logits_T[:, seg * SEG:(seg + 1) * SEG], bank[seg][0:NE, :], ACT.Copy).then_inc(logits_sb, 1)
                act.wait_ge(shifted, 1)
                act.activation(score[:], score[:], ACT.Exp).then_inc(exps, 1)

            @block.vector
            def _(dve):
                chain = Chain(dve, own)
                dve.memset(gate[:], 0.0).then_inc(zeroed, 1)
                dve.wait_ge(gate_hi, 1)
                dve.tensor_tensor(g_lo[:], gate[:], g_hi[:].bitcast(F32), ALU.subtract).then_inc(gate_lo, 1)
                logits = bank[4][:, 0:TT * NE].rearrange("p (t e) -> p t e", e=NE)
                dve.wait_ge(logits_T_mm, 1)
                chain.link(dve.tensor_reduce(top[:], logits, AX.X, ALU.max))
                dve.tensor_tensor(score[:], logits, over_e(top[:]), ALU.subtract).then_inc(shifted, 1)
                dve.wait_ge(exps, 1)
                chain.link(dve.tensor_reduce(total[:], score[:], AX.X, ALU.add))
                chain.link(dve.reciprocal(top[:], total[:]))
                chain.link(dve.tensor_tensor(score[:], score[:], over_e(top[:]), ALU.mult))
                dve.wait_ge(made, 8)
                for left, one, weight in ((score, one1, keep.weight1), (rest, one2, keep.weight2)):
                    chain.link(dve.tensor_reduce(weight[:], left[:], AX.X, ALU.max))
                    chain.link(dve.tensor_tensor(key[:], left[:], over_e(weight[:]), ALU.is_equal))
                    chain.link(dve.tensor_tensor(key[:], key[:], over_t(rank_first[:]), ALU.mult))
                    chain.link(dve.tensor_reduce(best[:], key[:], AX.X, ALU.max))
                    chain.link(dve.tensor_tensor(one[:], key[:], over_e(best[:]), ALU.is_equal))
                    if one is one1:
                        chain.link(dve.scalar_tensor_tensor(rest[:], one[:], -2.0, score[:], ALU.mult, ALU.add))
                dve.tensor_tensor(chosen[:], one1[:], one2[:], ALU.add).then_inc(chosen_ready, 1)
                dve.wait_ge(ranks, 1)
                per = lambda a: a.rearrange("p (e o) -> p e o", o=1).broadcast_to([P, NE, NE])
                along = lambda a: a.rearrange("p (o e) -> p o e", o=1).broadcast_to([P, NE, NE])
                chain.link(dve.tensor_copy(base[:], bank[6][:, 0:NE]))
                chain.link(dve.tensor_tensor(counts_over[:], per(base[:]), along(thresholds[:]), ALU.is_gt))
                chain.link(dve.tensor_reduce(tiles[:], counts_over[:], AX.X, ALU.add))
                chain.link(dve.tensor_tensor(counts_over[:], upto[:], along(tiles[:]), ALU.mult))
                chain.link(dve.tensor_reduce(tiles_to[:], counts_over[:], AX.X, ALU.add))
                chain.link(dve.tensor_tensor(base[:], tiles_to[:], tiles[:], ALU.subtract))
                chain.link(dve.tensor_scalar(base[:], base[:], float(P), None, ALU.mult))
                chain.link(dve.tensor_tensor(rest[:], bank[5][:, 0:TT * NE].rearrange("p (t e) -> p t e", e=NE), over_t(base[:]), ALU.add))
                for one, slot in ((one1, keep.slot1), (one2, keep.slot2)):
                    chain.link(dve.tensor_tensor(key[:], rest[:], one[:], ALU.mult))
                    chain.link(dve.tensor_reduce(where[:], key[:], AX.X, ALU.add))
                    chain.link(dve.tensor_copy(slot[:], where[:]))
                dve.tensor_copy(best[:], top[:]).then_inc(slots_ready, 1)
                ends = tiles_to[0:1, :].rearrange("p (o e) -> p o e", o=1).broadcast_to([1, SLOT_TILES, NE])
                numbers = tile_no[:].rearrange("p (i o) -> p i o", o=1).broadcast_to([1, SLOT_TILES, NE])
                chain.link(dve.tensor_tensor(passed[:], numbers, ends, ALU.is_ge))
                chain.link(dve.tensor_reduce(expert_f[:], passed[:], AX.X, ALU.add))
                chain.link(dve.tensor_scalar(expert_f[:], expert_f[:], float(NE - 1), None, ALU.min))
                chain.link(dve.tensor_copy(keep.expert_of[:], expert_f[:]))


def experts(nc, keep, w_up, w_down, sorted_x, sorted_y):
    with Scope(nc, "experts") as c:
        up, down_w = c.sb("up", [P, NE, KT, 2 * INNER]), c.sb("down", [IH, NE, 2, HID])
        two = lambda n, *shape: [c.sb(f"{n}{b}", list(shape)) for b in range(2)]
        xs, xT, silu, h, hT, ys = two("xs", P, HID), two("xT", P, KT, P), two("silu", P, INNER), two("h", P, INNER), two("hT", IH, 2, P), two("ys", P, HID)
        bank = c.banks(8)
        up_in, down_in = c.sem("up_in"), c.sem("down_in")
        xs_in = [c.sem("xs_in0"), c.sem("xs_in1")]
        stored = [c.sem("stored0"), c.sem("stored1")]
        x_turned, xT_sb, gu_mm, silu_sb, h_sb, h_turned, hT_sb, y_mm, ys_sb = (
            c.sem(n) for n in ("x_turned", "xT", "gu_mm", "silu", "h", "h_turned", "hT", "y_mm", "ys"))
        N = SLOT_TILES
        row = lambda a, i: a[bass.ds(i * P, P), :]
        assert N % 2 == 0

        def tiles(eng, body):
            body(0, 0, True)
            body(1, 1, False)
            body(2, 0, False)
            with eng.Fori(0, (N - 4) // 2) as i:
                body(2 * i + 3, 1, False)
                body(2 * i + 4, 0, False)
            body(N - 1, 1, False)

        with nc.Block() as block:
            @block.sync
            def _(sp):
                for e in range(NE):
                    sp.dma_start(up[:, e], w_up[e]).then_inc(up_in, DMA)
                    sp.dma_start(down_w[:, e], w_down[e]).then_inc(down_in, DMA)

                def store(i, b, first):
                    sp.wait_ge(ys_sb, i + 1)
                    sp.dma_start(row(sorted_y, i), ys[b][:]).then_inc(stored[b], DMA)
                tiles(sp, store)
                for b in range(2):
                    sp.wait_ge(stored[b], N // 2 * DMA)

            @block.gpsimd
            def _(pool):
                def load(i, b, first):
                    if not (isinstance(i, int) and i < 2):
                        pool.wait_ge(x_turned, i - 1)
                    pool.dma_start(xs[b][:], row(sorted_x, i)).then_inc(xs_in[b], DMA)
                tiles(pool, load)

            @block.tensor
            def _(pe):
                pe.wait_ge(up_in, NE * DMA)
                pe.wait_ge(down_in, NE * DMA)

                def turn_h(i, b):
                    pe.wait_ge(h_sb, i + 1)
                    for k in range(2):
                        last = pe.transpose(bank[4 + b][0:IH, k * P:(k + 1) * P], h[b][:, k * IH:(k + 1) * IH], keep.ident[:])
                    last.then_inc(h_turned, 1)

                def down(i, b):
                    e = pe.value_load(keep.expert_of[0:1, bass.ds(i, 1)], min_val=0, max_val=NE - 1)
                    if not (isinstance(i, int) and i < 2):
                        pe.wait_ge(ys_sb, i - 1)
                    pe.wait_ge(hT_sb, i + 1)
                    for k in range(2):
                        last = pe.matmul(bank[6 + b][:, 0:HID], hT[b][:, k, :], down_w[:, bass.ds(e, 1), k, :].rearrange("p a f -> p (a f)"),
                                         start=k == 0, stop=k == 1)
                    last.then_inc(y_mm, 1)

                def tile(i, b, first):
                    pe.wait_ge(xs_in[b], loads(i, b))
                    if not first:
                        pe.wait_ge(xT_sb, i)
                    for f in range(KT):
                        last = pe.transpose(bank[b][:, f * P:(f + 1) * P], xs[b][:, f * P:(f + 1) * P], keep.ident[:])
                    last.then_inc(x_turned, 1)
                    if not first:
                        turn_h(i - 1, 1 - b)
                    e = pe.value_load(keep.expert_of[0:1, bass.ds(i, 1)], min_val=0, max_val=NE - 1)
                    pe.wait_ge(xT_sb, i + 1)
                    if not first:
                        pe.wait_ge(h_sb, i)
                    for f in range(KT):
                        last = pe.matmul(bank[2 + b][:, 0:2 * INNER], xT[b][:, f, :], up[:, bass.ds(e, 1), f, :].rearrange("p a f -> p (a f)"),
                                         start=f == 0, stop=f == KT - 1)
                    last.then_inc(gu_mm, 1)
                    if not first:
                        down(i - 1, 1 - b)

                tiles(pe, tile)
                turn_h(N - 1, 1)
                down(N - 1, 1)

            @block.scalar
            def _(act):
                def tile(i, b, first):
                    act.wait_ge(x_turned, i + 1)
                    act.activation(xT[b][:].rearrange("p k t -> p (k t)"), bank[b][:, 0:HID], ACT.Copy).then_inc(xT_sb, 1)
                    act.wait_ge(gu_mm, i + 1)
                    if not first:
                        act.wait_ge(h_sb, i)
                    act.activation(silu[b][:], bank[2 + b][:, 0:INNER], ACT.Silu).then_inc(silu_sb, 1)
                tiles(act, tile)

            @block.vector
            def _(dve):
                def late(i, b, first):
                    dve.wait_ge(h_turned, i + 1)
                    dve.tensor_copy(hT[b][:].rearrange("p k t -> p (k t)"), bank[4 + b][0:IH, 0:HID]).then_inc(hT_sb, 1)

                def output(i, b, stores):
                    dve.wait_ge(y_mm, i + 1)
                    if not (isinstance(stores, int) and stores == 0):
                        dve.wait_ge(stored[b], stores)
                    dve.tensor_copy(ys[b][:], bank[6 + b][:, 0:HID]).then_inc(ys_sb, 1)

                def tile(i, b, first):
                    if not first:
                        late(i - 1, 1 - b, False)
                    dve.wait_ge(silu_sb, i + 1)
                    dve.tensor_tensor(h[b][:], silu[b][:], bank[2 + b][:, INNER:2 * INNER], ALU.mult).then_inc(h_sb, 1)
                    if not first:
                        output(i - 1, 1 - b, stores_before(i - 1, 1 - b))
                tiles(dve, tile)
                late(N - 1, 1, False)
                output(N - 1, 1, stores_before(N - 1, 1))


def loads(i, b):
    return (i - b) * (DMA // 2) + DMA


def stores_before(i, b):
    return (i - b) * (DMA // 2)


def combine(nc, keep, sorted_y, y):
    with Scope(nc, "combine") as c:
        got = [c.sb(f"got{b}", [P, TT, HID]) for b in range(2)]
        arrived = [c.sem(f"arrived{t}") for t in range(TT)]
        added = c.sem("added")
        with nc.Block() as block:
            @block.gpsimd
            def _(pool):
                for t in range(TT):
                    for b, slot in enumerate((keep.slot1, keep.slot2)):
                        pool.indirect_dma_start(out=got[b][:, t, :], out_offset=None, in_=sorted_y,
                                                in_offset=bass.IndirectOffsetOnAxis(ap=slot[:, t:t + 1], axis=0)).then_inc(arrived[t], DMA)

            @block.vector
            def _(dve):
                for t in range(TT):
                    dve.wait_ge(arrived[t], 2 * DMA)
                    for b, weight in enumerate((keep.weight1, keep.weight2)):
                        dve.scalar_tensor_tensor(y[:, t, :], got[b][:, t, :], weight[:, t:t + 1], y[:, t, :], ALU.mult, ALU.add).then_inc(added, 1)
                        if b == 0:
                            dve.wait_ge(added, 2 * t + 1)


def zero_slots(nc, sorted_x):
    with Scope(nc, "zero") as c:
        zeros, made, done = c.sb("zeros", [P, 2048]), c.sem("made"), c.sem("done")
        rows = sorted_x.rearrange("(n p r) f -> n p (r f)", p=P, r=8)
        with nc.Block() as block:
            @block.gpsimd
            def _(pool):
                pool.memset(zeros[:], 0.0).then_inc(made, 1)

            @block.sync
            def _(sp):
                sp.wait_ge(made, 1)
                for n in range(rows.shape[0]):
                    sp.dma_start(rows[n], zeros[:]).then_inc(done, DMA)
                sp.wait_ge(done, rows.shape[0] * DMA)


def moe_keep(keep, c):
    keep.weight1, keep.weight2 = c.sb("weight1", [P, TT]), c.sb("weight2", [P, TT])
    keep.slot1, keep.slot2 = c.sb("slot1", [P, TT], I32), c.sb("slot2", [P, TT], I32)
    keep.expert_of = c.sb("expert_of", [1, SLOT_TILES], I32)


def lay_out_moe(gate_w, w_gate_up, w_down):
    return {"gw": np.ascontiguousarray(gate_w.reshape(NE, KT, P).transpose(2, 1, 0)),
            "wgu": np.ascontiguousarray(w_gate_up.reshape(NE, KT, P, 2 * INNER).transpose(0, 2, 1, 3)),
            "wdn": np.ascontiguousarray(w_down.reshape(NE, 2, IH, HID).transpose(0, 2, 1, 3))}


WH, WD, WG, WIN = 16, 16, 2, 32
REP = WH // WG
STEP = WIN // 2
USED = SEQ // WIN * STEP + STEP
WPAIRS = SEQ // WIN // 2
GD = WG * WD
RR = REP // 4


def window_attention(nc, keep, y, w):
    with Scope(nc, "win") as c:
        sb = c.sb
        wq, wq_hi, wq_lo = sb("wq", [P, KT, HID]), sb("wq_hi", [P, KT, HID], F32R), sb("wq_lo", [P, KT, HID], F32R)
        wkv, wkv_hi, wkv_lo = sb("wkv", [P, KT, P]), sb("wkv_hi", [P, KT, P], F32R), sb("wkv_lo", [P, KT, P], F32R)
        wo, bo = sb("wo", [P, RR, HID]), sb("bo", [P, HID])
        bq, bkv = sb("bq", [P, RR]), sb("bkv", [2 * GD, 1])
        qT, kvT = sb("qT", [P, BATCH, RR, USED]), sb("kvT", [2 * GD, BATCH, USED])
        q2 = sb("q2", [P, REP, WPAIRS * WIN])
        q3 = sb("q3", [P, RR, WPAIRS, 4, WIN])
        k2 = sb("k2", [P, 2, WG, WPAIRS * WIN])
        vdup = sb("vdup", [2 * GD, BATCH, WPAIRS, 2, WG, WIN])
        v2 = sb("v2", [P, BATCH, WPAIRS, 2 * GD])
        less, prob, norm = ([sb(f"{n}{b}", [P, SEG]) for b in range(2)] for n in ("less", "prob", "norm"))
        pT = [sb(f"pT{b}", [P, SEG]) for b in range(2)]
        most, total, inv = ([sb(f"{n}{b}", [P, SEG // WIN]) for b in range(2)] for n in ("most", "total", "inv"))
        o2 = sb("o2", [2 * GD, BATCH, RR, 4, WPAIRS, WIN])
        oT = q2[:].rearrange("p r n -> p (r n)").rearrange("p (b r h m q) -> p b r h m q", b=BATCH, r=RR, h=2, m=WPAIRS)
        oP = q3[:].rearrange("p r m a q -> p (r m a q)").rearrange("p (b r m h q) -> p b r m h q", b=BATCH, r=RR, m=WPAIRS, h=2)
        q3_sb, oP_sb = c.sem("q3"), c.sem("oP")
        bank = c.banks(8)
        (wq_in, wkv_in, kv_zero, k_zero, v_zero, rest_in, bias_in, split_hi, split_lo, q_mm, kv_mm, q_sb, kv_sb) = (
            c.sem(n) for n in ("wq_in", "wkv_in", "kv_zero", "k_zero", "v_zero", "rest_in", "bias_in", "split_hi", "split_lo", "q_mm", "kv_mm", "q_sb", "kv_sb"))
        (v_mm, v_sb, s_mm, most_sb, less_sb, prob_sb, total_sb, inv_sb, norm_sb, t_mm, pT_sb, o_mm, o_sb, y_mm, y_sb) = (
            c.sem(n) for n in ("v_mm", "v_sb", "s_mm", "most", "less", "prob", "total", "inv", "norm", "t_mm", "pT", "o_mm", "o", "y_mm", "y"))
        vdup_sb = c.sem("vdup")
        k_moved = [c.sem(f"k_moved{b}") for b in range(BATCH)]
        q_moved = [c.sem(f"q_moved{n}") for n in range(BATCH * RR)]
        o_moved = [c.sem(f"o_moved{b}") for b in range(BATCH)]
        HALF = USED // 2
        JOBS = [(b, rr, mq) for b in range(BATCH) for rr in range(RR) for mq in range(4)]
        NJ = len(JOBS)
        rows = lambda b, half, n=1: slice(b * 2 * GD + half * GD, b * 2 * GD + (half + n) * GD)
        by_window = lambda a: a.rearrange("p (w k) -> p w k", k=WIN)
        spread_w = lambda a: a.rearrange("p (w o) -> p w o", o=1).broadcast_to([P, SEG // WIN, WIN])

        with nc.Block() as block:
            @block.sync
            def _(sp):
                sp.dma_start(wq[:], w["Wq"].rearrange("(k p) n -> p k n", p=P)).then_inc(wq_in, DMA)
                sp.wait_ge(kv_zero, 1)
                for n, name in enumerate(("Wk", "Wv")):
                    sp.dma_start(wkv[:, :, n * GD:(n + 1) * GD], w[name].rearrange("(k p) n -> p k n", p=P)).then_inc(wkv_in, DMA)
                for n, name in enumerate(("bk", "bv")):
                    sp.dma_start(bkv[n * GD:(n + 1) * GD, :], w[name]).then_inc(bias_in, DMA)
                sp.dma_start(bq[:], w["bq"]).then_inc(bias_in, DMA)
                sp.dma_start(wo[:], w["Wo"].rearrange("(r n) f -> n r f", n=P)).then_inc(rest_in, DMA)
                sp.dma_start(bo[:], w["bo"].rearrange("(o f) -> o f", o=1).broadcast_to([P, HID])).then_inc(rest_in, DMA)
                sp.wait_ge(k_zero, 1)
                for b in range(BATCH):
                    sp.wait_ge(kv_sb, 2 * b + 2)
                    for half in range(2):
                        for g in range(WG):
                            at = b * 2 * GD + half * GD + g * WD
                            sp.dma_start(k2[at:at + WD, half, g, :], kvT[g * WD:(g + 1) * WD, b, half * STEP:half * STEP + WPAIRS * WIN]).then_inc(k_moved[b], DMA)
                    for rr in range(RR):
                        sp.wait_ge(q_sb, 2 * (b * RR + rr) + 2)
                        for half in range(2):
                            for r in range(4):
                                sp.dma_start(q2[rows(b, half), rr * 4 + r, :],
                                             qT[r * GD:(r + 1) * GD, b, rr, half * STEP:half * STEP + WPAIRS * WIN]).then_inc(q_moved[b * RR + rr], DMA)
                for b in range(BATCH):
                    for rr in range(RR):
                        sp.wait_ge(o_sb, (b * RR + rr) * 4 + 4)
                        for half in range(2):
                            for r in range(4):
                                sp.dma_start(oT[r * GD:(r + 1) * GD, b, rr, half], o2[half * GD:(half + 1) * GD, b, rr, r]).then_inc(o_moved[b], DMA)

            @block.gpsimd
            def _(pool):
                pool.memset(k2[:], 0.0).then_inc(k_zero, 1)
                pool.memset(v2[:], 0.0).then_inc(v_zero, 1)
                for i in range(NJ):
                    pool.wait_ge(inv_sb, i + 1)
                    if i >= 2:
                        pool.wait_ge(t_mm, i - 1)
                    pool.tensor_tensor(by_window(norm[i % 2][:]), by_window(prob[i % 2][:]), spread_w(inv[i % 2][:]), ALU.mult).then_inc(norm_sb, 1)

            @block.scalar
            def _(act):
                act.wait_ge(wkv_in, 2 * DMA)
                act.activation(wkv_hi[:], wkv[:], ACT.Copy).then_inc(split_hi, 1)
                act.wait_ge(wq_in, DMA)
                act.activation(wq_hi[:], wq[:], ACT.Copy).then_inc(split_hi, 1)
                act.wait_ge(bias_in, 3 * DMA)
                for b in range(BATCH):
                    for n in range(2):
                        act.wait_ge(kv_mm, 2 * b + n + 1)
                        act.activation(kvT[:, b, n * HALF:(n + 1) * HALF], bank[n][0:2 * GD, 0:HALF], ACT.Identity, bias=bkv[:, 0:1]).then_inc(kv_sb, 1)
                    for rr in range(RR):
                        for n in range(2):
                            i = (b * RR + rr) * 2 + n
                            act.wait_ge(q_mm, i + 1)
                            act.activation(qT[:, b, rr, n * HALF:(n + 1) * HALF], bank[2 + i % 4][:, 0:HALF], ACT.Identity, bias=bq[:, rr:rr + 1]).then_inc(q_sb, 1)
                for i in range(NJ + 3):
                    if i < NJ:
                        act.wait_ge(less_sb, i + 1)
                        if i >= 2:
                            act.wait_ge(norm_sb, i - 1)
                        act.activation(prob[i % 2][:], less[i % 2][:], ACT.Exp, scale=float(WD) ** -0.5).then_inc(prob_sb, 1)
                    if 3 <= i:
                        n = i - 3
                        act.wait_ge(t_mm, n + 1)
                        act.activation(pT[n % 2][:], bank[2 + n % 2][:], ACT.Copy).then_inc(pT_sb, 1)

            @block.vector
            def _(dve):
                dve.memset(wkv[:], 0.0).then_inc(kv_zero, 1)
                dve.wait_ge(split_hi, 1)
                dve.tensor_tensor(wkv_lo[:], wkv[:], wkv_hi[:].bitcast(F32), ALU.subtract).then_inc(split_lo, 1)
                dve.wait_ge(split_hi, 2)
                dve.tensor_tensor(wq_lo[:], wq[:], wq_hi[:].bitcast(F32), ALU.subtract).then_inc(split_lo, 1)
                for b in range(BATCH):
                    dve.wait_ge(kv_sb, 2 * b + 2)
                    for half in range(2):
                        v = kvT[GD:2 * GD, b, half * STEP:half * STEP + WPAIRS * WIN].rearrange("p (m k) -> p m k", k=WIN)
                        for g in range(WG):
                            last = dve.tensor_copy(vdup[GD:2 * GD, b, :, half, g, :], v)
                    last.then_inc(vdup_sb, 1)
                for b in range(BATCH):
                    for rr in range(RR):
                        dve.wait_ge(q_moved[b * RR + rr], 8 * DMA)
                        dve.tensor_copy(q3[rows(b, 0, 2), rr].rearrange("p m r q -> p r m q"),
                                        q2[rows(b, 0, 2), rr * 4:rr * 4 + 4, :].rearrange("p r (m q) -> p r m q", q=WIN)).then_inc(q3_sb, 1)
                dve.wait_ge(v_zero, 1)
                for b in range(BATCH):
                    dve.wait_ge(v_mm, b + 1)
                    for half in range(2):
                        for g in range(WG):
                            at = (half * WG + g) * WIN
                            col = half * GD + g * WD
                            last = dve.tensor_copy(v2[at:at + WIN, b, :, col:col + WD],
                                                   bank[6 + b][at:at + WIN, :].rearrange("p (m n) -> p m n", n=GD)[:, :, g * WD:(g + 1) * WD])
                    last.then_inc(v_sb, 1)
                for i in range(NJ + 4):
                    if i < NJ:
                        x = i % 2
                        scores = by_window(bank[x][:])
                        dve.wait_ge(s_mm, i + 1)
                        dve.tensor_reduce(most[x][:], scores, AX.X, ALU.max).then_inc(most_sb, 1)
                        dve.wait_ge(most_sb, i + 1)
                        dve.tensor_tensor(by_window(less[x][:]), scores, spread_w(most[x][:]), ALU.subtract).then_inc(less_sb, 1)
                    if 1 <= i <= NJ:
                        n = i - 1
                        x = n % 2
                        dve.wait_ge(prob_sb, n + 1)
                        dve.tensor_reduce(total[x][:], by_window(prob[x][:]), AX.X, ALU.add).then_inc(total_sb, 1)
                        dve.wait_ge(total_sb, n + 1)
                        if n >= 2:
                            dve.wait_ge(norm_sb, n - 1)
                        dve.reciprocal(inv[x][:], total[x][:]).then_inc(inv_sb, 1)
                    if i >= 4:
                        n = i - 4
                        b, rr, mq = JOBS[n]
                        dve.wait_ge(o_mm, n + 1)
                        dve.tensor_copy(o2[:, b, rr, :, mq * 4:mq * 4 + 4, :].rearrange("p r m q -> p m r q"),
                                        bank[4 + n % 2][0:2 * GD, :].rearrange("p (m r q) -> p m r q", m=4, r=4)).then_inc(o_sb, 1)
                for b in range(BATCH):
                    dve.wait_ge(o_moved[b], 16 * DMA)
                    for rr in range(RR):
                        dve.tensor_copy(oP[:, b, rr].rearrange("p m h q -> p h m q"), oT[:, b, rr]).then_inc(oP_sb, 1)
                dve.wait_ge(rest_in, 2 * DMA)
                for t in range(TT // 2):
                    dve.wait_ge(y_mm, t + 1)
                    dve.tensor_tensor(y[:, 2 * t:2 * t + 2, :], bank[6 + t % 2][:].rearrange("p (a f) -> p a f", a=2),
                                      bo[:].rearrange("p (o f) -> p o f", o=1).broadcast_to([P, 2, HID]), ALU.add).then_inc(y_sb, 1)

            @block.tensor
            def _(pe):
                def project(to, w_hi, w_lo, cols, b, n):
                    toks = slice(b * SEQ + n * HALF, b * SEQ + (n + 1) * HALF)
                    for f in range(KT):
                        last = three_passes(nc, to[:, 0:HALF], (w_hi[:, f, cols], w_lo[:, f, cols]),
                                            (keep.xT_hi[:, f, toks], keep.xT_lo[:, f, toks]), f == 0, f == KT - 1)
                    return last

                pe.wait_ge(split_lo, 1)
                for b in range(BATCH):
                    for n in range(2):
                        if b:
                            pe.wait_ge(kv_sb, n + 1)
                        project(bank[n], wkv_hi, wkv_lo, slice(0, P), b, n).then_inc(kv_mm, 1)
                    pe.wait_ge(split_lo, 2)
                    for rr in range(RR):
                        for n in range(2):
                            i = (b * RR + rr) * 2 + n
                            if i >= 4:
                                pe.wait_ge(q_sb, i - 3)
                            project(bank[2 + i % 4], wq_hi, wq_lo, slice(rr * P, (rr + 1) * P), b, n).then_inc(q_mm, 1)
                for b in range(BATCH):
                    pe.wait_ge(vdup_sb, b + 1)
                    for m in range(WPAIRS):
                        last = pe.transpose(bank[6 + b][:, m * GD:(m + 1) * GD], vdup[GD:2 * GD, b, m, :, :, :].rearrange("p h g k -> p (h g k)"),
                                            keep.ident[GD:2 * GD, GD:2 * GD])
                    last.then_inc(v_mm, 1)
                pe.wait_ge(q_sb, 4 * RR)
                pe.wait_ge(kv_sb, 4)
                for i in range(NJ + 4):
                    if i < NJ:
                        b, rr, mq = JOBS[i]
                        if i % (NJ // BATCH) == 0:
                            pe.wait_ge(k_moved[b], 4 * DMA)
                        pe.wait_ge(q3_sb, b * RR + rr + 1)
                        if i >= 2:
                            pe.wait_ge(less_sb, i - 1)
                        for j in range(4):
                            at = slice((mq * 4 + j) * WIN, (mq * 4 + j + 1) * WIN)
                            last = pe.matmul(bank[i % 2][:, j * P:(j + 1) * P].rearrange("p (a k) -> p a k", k=WIN), q3[rows(b, 0, 2), rr, mq * 4 + j].rearrange("p r q -> p (r q)"),
                                             k2[rows(b, 0, 2), :, :, at].rearrange("p a g k -> p (a g) k"), start=True, stop=True)
                        last.then_inc(s_mm, 1)
                    if 2 <= i < NJ + 2:
                        n = i - 2
                        pe.wait_ge(norm_sb, n + 1)
                        if n >= 2:
                            pe.wait_ge(pT_sb, n - 1)
                        for j in range(4):
                            last = pe.transpose(bank[2 + n % 2][:, j * P:(j + 1) * P], norm[n % 2][:, j * P:(j + 1) * P], keep.ident[:])
                        last.then_inc(t_mm, 1)
                    if 3 <= i < NJ + 3:
                        n = i - 3
                        b, rr, mq = JOBS[n]
                        pe.wait_ge(pT_sb, n + 1)
                        pe.wait_ge(v_sb, 2)
                        if n >= 2:
                            pe.wait_ge(o_sb, n - 1)
                        for j in range(4):
                            last = pe.matmul(bank[4 + n % 2][0:2 * GD, j * P:(j + 1) * P], v2[:, b, mq * 4 + j, :], pT[n % 2][:, j * P:(j + 1) * P],
                                             start=True, stop=True)
                        last.then_inc(o_mm, 1)
                pe.wait_ge(rest_in, 2 * DMA)
                for t in range(TT):
                    b, tile = t // (TT // BATCH), t % (TT // BATCH)
                    if t % (TT // BATCH) == 0:
                        pe.wait_ge(oP_sb, (b + 1) * RR)
                    if t >= 4 and t % 2 == 0:
                        pe.wait_ge(y_sb, t // 2 - 1)
                    for rr in range(RR):
                        o = oP[:, b, rr, 2 * tile:2 * tile + 2].rearrange("p m h q -> p (m h q)")
                        last = pe.matmul(bank[6 + t // 2 % 2][:, t % 2 * HID:(t % 2 + 1) * HID], o, wo[:, rr, :], start=rr == 0, stop=rr == RR - 1)
                    if t % 2:
                        last.then_inc(y_mm, 1)


def lay_out_window(Wq, bq, Wk, bk, Wv, bv, Wo, bo):
    return {"Wq": Wq, "bq": np.ascontiguousarray(bq.reshape(RR, P).T), "Wk": Wk, "bk": bk.reshape(GD, 1),
            "Wv": Wv, "bv": bv.reshape(GD, 1), "Wo": Wo, "bo": bo}


def build_program(nc, a, out, sorted_x, sorted_y):
    keep = Keep()
    with Scope(nc, "keep") as whole:
        allocate(nc, keep, whole)
        moe_keep(keep, whole)
        load_x(nc, keep, a["x"])
        zero_slots(nc, sorted_x)
        with Scope(nc, "linear") as c:
            keep.decay_mask, keep.query_decay = c.sb("decay_mask", [P, NH, P]), c.sb("query_decay", [P, NH, P])
            keep.key_decay, keep.chunk_decay = c.sb("key_decay", [P, NH]), c.sb("chunk_decay", [P, NH])
            keep.acc, keep.squares = c.sb("acc", [P, KT, TOK]), c.sb("squares", [P, TOK])
            constants(nc, keep, a["slope"])
            norm_stage(nc, keep, "norm0")
            linear_attention(nc, keep, a["wp"], a["wop"], a["nw"])
            with Scope(nc, "linear_out") as c1:
                y = c1.sb("y", [P, TT, HID])
                rms_to_tokens(nc, keep, y)
                normed = c1.sb("normed", [P, TT, HID])
                norm_stage(nc, keep, "norm1", y=y, normed=normed)
                route(nc, keep, a["gw"], sorted_x, normed)
        y = whole.sb("y", [P, TT, HID])
        swiglu(nc, keep, "shared", y, a["shared_gate_up"], a["shared_down"], [P, P, 2 * INNER - 2 * P])
        experts(nc, keep, a["wgu"], a["wdn"], sorted_x, sorted_y)
        combine(nc, keep, sorted_y, y)
        norm_stage(nc, keep, "norm2", y=y)
        window_attention(nc, keep, y, a)
        norm_stage(nc, keep, "norm3", y=y)
        swiglu(nc, keep, "ffn", y, a["ffn_up"], a["ffn_down"], [P] * 8)
        norm_stage(nc, keep, "norm4", y=y, out=out.rearrange("b (t p) f -> p (b t) f", p=P))


def kernel(L0_attn_hidden_states, L0_attn_slope_rate, L0_attn_w_qkv, L0_attn_w_gate, L0_attn_w_out, L0_attn_norm_w,
           L0_ffn_gate_w, L0_ffn_w_gate_up, L0_ffn_w_down, L0_ffn_shared_gate_up, L0_ffn_shared_down,
           L1_attn_Wq, L1_attn_bq, L1_attn_Wk, L1_attn_bk, L1_attn_Wv, L1_attn_bv, L1_attn_Wo, L1_attn_bo,
           L1_ffn_w_gate_up, L1_ffn_w_down):
    import concourse.bacc as bacc
    from concourse.bass_utils import run_bass_kernel_spmd

    arrays = {
        "x": L0_attn_hidden_states, "slope": L0_attn_slope_rate,
        **lay_out_linear(L0_attn_w_qkv, L0_attn_w_gate, L0_attn_w_out, L0_attn_norm_w),
        **lay_out_moe(L0_ffn_gate_w, L0_ffn_w_gate_up, L0_ffn_w_down),
        "shared_gate_up": L0_ffn_shared_gate_up, "shared_down": L0_ffn_shared_down,
        **lay_out_window(L1_attn_Wq, L1_attn_bq, L1_attn_Wk, L1_attn_bk, L1_attn_Wv, L1_attn_bv, L1_attn_Wo, L1_attn_bo),
        "ffn_up": L1_ffn_w_gate_up.T, "ffn_down": L1_ffn_w_down.T,
    }
    arrays = {f"in_{n}": np.ascontiguousarray(v) for n, v in arrays.items()}
    nc = bacc.Bacc("TRN2", target_bir_lowering=False, num_devices=1)
    a = {n[3:]: nc.dram_tensor(n, v.shape, mybir.dt.from_np(v.dtype), kind="ExternalInput").ap() for n, v in arrays.items()}
    out = nc.dram_tensor("out", (BATCH, SEQ, HID), F32, kind="ExternalOutput").ap()
    sorted_x = nc.dram_tensor("sorted_x", (SLOTS, HID), F32).ap()
    sorted_y = nc.dram_tensor("sorted_y", (SLOTS, HID), F32).ap()
    build_program(nc, a, out, sorted_x, sorted_y)
    return run_bass_kernel_spmd(nc, [arrays], core_ids=[0]).results[0]["out"]
```

```python
import numpy as np
import concourse.bass as bass
from concourse import mybir
from concourse.alu_op_type import AluOpType as ALU
from contextlib import ExitStack

F32 = mybir.dt.float32
F32R = mybir.dt.float32r
BF16 = mybir.dt.bfloat16
I32 = mybir.dt.int32
ACT = mybir.ActivationFunctionType
AX = mybir.AxisListType

P = 128
BATCH, SEQ, HID = 2, 1024, 256
TOK = BATCH * SEQ
TT = TOK // P
KT = HID // P
SEG = 512
SEGS = TOK // SEG
TPS = SEG // P

NH, HD = 16, 128
BLK = 32
RMS_EPS, LN_EPS = 1e-6, 1e-5
PAIRS = NH // 2
DMA = 16


def three_passes(nc, out, lhs, rhs, first=True, last=True, skip=False):
    (lh, ll), (rh, rl) = lhs, rhs
    nc.tensor.matmul(out, lh, rh, start=first, stop=False, skip_group_check=skip)
    nc.tensor.matmul(out, lh, rl, start=False, stop=False, skip_group_check=skip)
    return nc.tensor.matmul(out, ll, rh, start=False, stop=last, skip_group_check=skip)


class Keep:
    pass


class Scope:

    def __init__(self, nc, name):
        self.nc, self.name, self.stack, self.sems = nc, name, ExitStack(), []

    def __enter__(self):
        self.stack.__enter__()
        return self

    def __exit__(self, *a):
        numbers = sorted(s.num for s in self.sems)
        while numbers:
            n = 1
            while n < len(numbers) and numbers[n] == numbers[0] + n:
                n += 1
            self.nc.gpsimd.sem_clear(range(numbers[0], numbers[0] + n))
            numbers = numbers[n:]
        return self.stack.__exit__(*a)

    def sb(self, name, shape, dt=F32):
        return self.stack.enter_context(self.nc.sbuf_tensor(f"{self.name}_{name}", shape, dt))

    def banks(self, n, first=0):
        return [self.stack.enter_context(self.nc.psum_tensor(f"{self.name}_bank{i}", [P, SEG], F32)) for i in range(n)]

    def sem(self, name):
        self.sems.append(self.stack.enter_context(self.nc.semaphore(f"{self.name}_{name}")))
        return self.sems[-1]


class Chain:

    def __init__(self, eng, sem, base=0):
        self.eng, self.sem, self.base, self.n = eng, sem, base, 0

    def step(self, ins):
        self.n += 1
        ins.then_inc(self.sem, 1)

    def link(self, ins):
        self.step(ins)
        self.wait()

    def wait(self):
        self.eng.wait_ge(self.sem, self.base + self.n)


class Decays:

    def __init__(self, c, keep):
        self.keep = keep
        self.slopes, self.neg, self.cols = c.sb("slopes", [P, NH]), c.sb("neg", [P, NH]), c.sb("cols", [P, 1])
        self.ages, self.rows = c.sb("ages", [P, P]), c.sb("rows", [P, P])
        self.mask, self.query = c.sb("decay_mask", [P, NH, P]), c.sb("query_decay", [P, NH, P])
        self.key, self.chunk = c.sb("key_decay", [P, NH]), c.sb("chunk_decay", [P, NH])
        self.slopes_in, self.numbered, self.ready, self.exps, self.masked = (c.sem(n) for n in ("slopes_in", "numbered", "ready", "exps", "masked"))

    def load(self, sp, slope):
        sp.dma_start(self.slopes[:], slope.rearrange("h a b -> (a b) h").broadcast_to([P, NH])).then_inc(self.slopes_in, DMA)

    def pool_start(self, pool):
        ident = self.keep.ident
        numbers = dict(allow_small_or_imprecise_dtypes=True)
        pool.memset(ident[:], 0.0).then_inc(self.numbered, 1)
        pool.iota(self.ages[:], pattern=[[1, P]], base=0, channel_multiplier=-1, **numbers).then_inc(self.numbered, 1)
        pool.iota(self.rows[:], pattern=[[1, P]], base=1, channel_multiplier=0, **numbers).then_inc(self.numbered, 1)
        pool.iota(self.cols[:], pattern=[[0, 1]], base=P - 1, channel_multiplier=-1, **numbers).then_inc(self.numbered, 1)
        pool.wait_ge(self.numbered, 4)
        pool.affine_select(out=ident[:], in_=ident[:], compare_op=ALU.not_equal, fill=1.0,
                           base=0, pattern=[[-1, P]], channel_multiplier=1).then_inc(self.numbered, 1)

    def dve_start(self, dve):
        dve.wait_ge(self.numbered, 4)
        dve.tensor_scalar(self.ages[:], self.ages[:], 0.0, None, ALU.max).then_inc(self.ready, 1)
        dve.wait_ge(self.slopes_in, DMA)
        dve.tensor_scalar(self.neg[:], self.slopes[:], -1.0, None, ALU.mult).then_inc(self.ready, 1)

    def act_start(self, act):
        act.wait_ge(self.ready, 2)
        act.activation(self.key[:], self.neg[:], ACT.Exp, scale=self.cols[:, 0:1])
        act.activation(self.chunk[:], self.neg[:], ACT.Exp, scale=float(P))
        self.act_heads(act, 0, 2)

    def act_heads(self, act, first, end):
        for h in range(first, end):
            s = self.neg[:, h:h + 1]
            act.activation(self.query[:, h, :], self.rows[:], ACT.Exp, scale=s)
            act.activation(self.mask[:, h, :], self.ages[:], ACT.Exp, scale=s).then_inc(self.exps, 1)

    def pool_heads(self, pool, first, end):
        pool.wait_ge(self.exps, end)
        for h in range(first, end):
            pool.affine_select(out=self.mask[:, h, :], in_=self.mask[:, h, :], compare_op=ALU.is_ge,
                               fill=0.0, base=0, pattern=[[1, P]], channel_multiplier=-1).then_inc(self.masked, 1)


class Norms:
    ROUNDS = SEGS + 2

    def __init__(self, c, keep, tag, y, banks, z_all=None):
        self.keep, self.y, self.banks, self.z_all = keep, y, banks, z_all
        sb = lambda n, shape, dt=F32: c.sb(f"{tag}_{n}", shape, dt)
        self.stats, self.mean_var = sb("stats", [P, 2 * TPS, 6]), sb("mean_var", [P, 2 * TPS, 2])
        self.spread, self.root, self.scale, self.shift = (sb(n, [P, 2 * TPS]) for n in ("spread", "root", "scale", "shift"))
        self.z_y = sb("z_y", [P, TPS, HID]) if y is not None else None
        self.z_one = sb("z_x", [P, TPS, HID]) if z_all is None else None
        self.spread_ready, self.root_ready, self.affine_ready, self.z_x_ready, self.turned, self.high, self.low = (
            c.sem(f"{tag}_{n}") for n in ("spread", "root", "affine", "z_x", "turned", "high", "low"))
        self.first = 0 if y is not None else 1

    def z_x(self, g):
        return self.z_one if self.z_all is None else self.z_all[:, g * TPS:(g + 1) * TPS, :]

    def tiles(self, a, g):
        return a[:, g * TPS:(g + 1) * TPS, :]

    def span(self, r):
        return slice(0 if r < SEGS and self.y is not None else TPS, 2 * TPS if r >= 1 else TPS)

    def dve_round(self, dve, chain, r, y_wait=None):
        n = r - self.first
        if r <= SEGS:
            if self.y is not None and r >= 1:
                xs = self.tiles(self.keep.x, r - 1)
                chain.link(dve.tensor_tensor(xs, xs, self.z_y[:], ALU.add))
            columns = []
            if self.y is not None and r < SEGS:
                columns += [(j, self.y[:, r * TPS + j, :]) for j in range(TPS)]
            if r >= 1:
                columns += [(TPS + j, self.keep.x[:, (r - 1) * TPS + j, :]) for j in range(TPS)]
            for i, (col, tile) in enumerate(columns):
                if y_wait is not None and i in (0, 2) and r < SEGS + (self.y is None):
                    y_wait(i // 2)
                chain.step(dve.bn_stats(self.stats[:, col, :], tile))
            chain.wait()
            for col, _ in columns:
                chain.step(dve.bn_aggr(self.mean_var[:, col, :], self.stats[:, col, :]))
            chain.wait()
            at = self.span(r)
            dve.tensor_scalar(self.spread[:, at], self.mean_var[:, at, 1], LN_EPS, None, ALU.add).then_inc(self.spread_ready, 1)
        if r >= 2:
            self.dve_low(dve, r - 2)
        if r <= SEGS:
            dve.wait_ge(self.root_ready, n + 1)
            chain.link(dve.reciprocal(self.scale[:, at], self.root[:, at]))
            dve.scalar_tensor_tensor(self.shift[:, at], self.mean_var[:, at, 0], -1.0, self.scale[:, at], ALU.mult, ALU.mult).then_inc(self.affine_ready, 1)
            if self.y is not None and r < SEGS:
                for j in range(TPS):
                    chain.step(dve.tensor_scalar(self.z_y[:, j, :], self.y[:, r * TPS + j, :], self.mean_var[:, j, 0:1], self.scale[:, j:j + 1],
                                                 ALU.subtract, ALU.mult))
                chain.wait()

    def dve_low(self, dve, g):
        for k in range(KT):
            dve.wait_ge(self.high, KT * g + k + 1)
            at = slice(g * SEG, (g + 1) * SEG)
            dve.tensor_tensor(self.keep.xT_lo[:, k, at], self.banks[k][:], self.keep.xT_hi[:, k, at].bitcast(F32),
                              ALU.subtract).then_inc(self.low, 1)

    def act_root(self, act, r):
        if r <= SEGS:
            act.wait_ge(self.spread_ready, r - self.first + 1)
            at = self.span(r)
            act.activation(self.root[:, at], self.spread[:, at], ACT.Sqrt).then_inc(self.root_ready, 1)
        if r >= 2:
            g = r - 2
            for k in range(KT):
                act.wait_ge(self.turned, KT * g + k + 1)
                act.activation(self.keep.xT_hi[:, k, g * SEG:(g + 1) * SEG], self.banks[k][:], ACT.Copy).then_inc(self.high, 1)

    def act_apply(self, act, r):
        if not 1 <= r <= SEGS:
            return
        act.wait_ge(self.affine_ready, r - self.first + 1)
        for j in range(TPS):
            last = act.activation(self.z_x(r - 1)[:, j, :], self.keep.x[:, (r - 1) * TPS + j, :], ACT.Identity,
                                  scale=self.scale[:, TPS + j:TPS + j + 1], bias=self.shift[:, TPS + j:TPS + j + 1])
        last.then_inc(self.z_x_ready, 1)

    def pe_turn(self, pe, g):
        pe.wait_ge(self.z_x_ready, g + 1)
        for k in range(KT):
            if g:
                pe.wait_ge(self.low, KT * (g - 1) + k + 1)
            for j in range(TPS):
                last = pe.transpose(self.banks[k][:, j * P:(j + 1) * P], self.z_x(g)[:, j, k * P:(k + 1) * P], self.keep.ident[:])
            last.then_inc(self.turned, 1)


def linear_attention(nc, keep, x, slope, w_pairs, wout_pairs, norm_w, sorted_x):
    with Scope(nc, "lin") as c:
        raw = c.sb("raw", [P, KT, 1024])
        w_hi, w_lo = c.sb("w_hi", [P, KT, 1024], F32R), c.sb("w_lo", [P, KT, 1024], F32R)
        raw_out = c.sb("raw_out", [P, 2, HID])
        wo_hi, wo_lo = c.sb("wo_hi", [P, 2, HID], F32R), c.sb("wo_lo", [P, 2, HID], F32R)
        norm_in = c.sb("norm_in", [P, NH])
        two = lambda n, dt=F32: c.sb(n, [P, 2, SEG], dt)
        q, k, kd, o, th, sq, qd, st, g = (two(n) for n in ("q", "k", "kd", "o", "th", "sq", "qd", "st", "g"))
        g_hi, g_lo = two("g_hi", F32R), two("g_lo", F32R)
        v = c.sb("v", [P, TPS, 2, HD])
        state = c.sb("state", [P, 2, TPS, HD])
        mask, q_dec = c.sb("mask", [P, 2, P]), c.sb("q_dec", [P, 2, P])
        k_dec, c_dec, half_norm = c.sb("k_dec", [P, 2]), c.sb("c_dec", [P, 2]), c.sb("half_norm", [P, 2])
        zeros = c.sb("zeros", [P, HID])
        bank = c.banks(8)
        sem = c.sem
        raw_in, raw_out_in, norm_sem = sem("raw_in"), sem("raw_out_in"), sem("norm_in")
        w_hi_done, w_lo_done, wo_done, wo_hi_done = sem("w_hi"), sem("w_lo"), sem("wo"), sem("wo_hi")
        q_mm, k_mm, v_mm, g_mm, t_mm, s_mm, d_mm, o_mm, w_mm = (sem(n + "_mm") for n in "qkvgtsdow")
        q_sb, k_sb, v_sb, th_sb, kd_sb, o_sb, sq_sb = (sem(n + "_sb") for n in ("q", "k", "v", "th", "kd", "o", "sq"))
        qd_sb, st_sb, state_sb, g_sb, acc_sb, squares_sb = (sem(n + "_sb") for n in ("qd", "st", "state", "g", "acc", "squares"))
        heads_sb, own, norms_own, zeroed = sem("heads"), sem("own"), sem("norms_own"), sem("zeroed")
        decays = Decays(c, keep)
        norms = Norms(c, keep, "norms", None, bank[2:4])
        x_in = [sem(f"x_in{g}") for g in range(SEGS)]
        C4 = lambda ap: ap.rearrange("p (c i) -> p c i", c=TPS)

        def states(t, seg, a, n):
            hp28 = (t - seg) // 4 * 28 if isinstance(t, int) else None
            base = hp28 if hp28 is not None else (t - seg) * 7
            return base + (0, 8, 14, 22)[seg] + a * (4 - seg % 2) + n

        def n_states(seg):
            return 4 - seg % 2

        COL = {("q", 0): 0, ("k", 0): 1, ("q", 1): 2, ("k", 1): 3, ("g", 0): 4, ("g", 1): 5}

        def pe_pass(pe, hp, first):
            def project(job, a, to, seg):
                cols = slice(COL[job, a] * P, (COL[job, a] + 1) * P)
                toks = slice(seg * SEG, (seg + 1) * SEG)
                for f in range(KT):
                    last = three_passes(nc, to[:], (w_hi[:, f, cols], w_lo[:, f, cols]),
                                        (keep.xT_hi[:, f, toks], keep.xT_lo[:, f, toks]), f == 0, f == KT - 1)
                return last

            pe.wait_ge(w_hi_done, 2 * hp + 2)
            pe.wait_ge(w_lo_done, 2 * hp + 2)
            for seg in range(SEGS):
                t = 4 * hp + seg
                start = first and seg == 0
                if first:
                    pe.wait_ge(norms.low, KT * (seg + 1))
                if not start:
                    pe.wait_ge(o_sb, 2 * t - 1)
                project("q", 0, bank[0], seg).then_inc(q_mm, 1)
                if not start:
                    pe.wait_ge(o_sb, 2 * t)
                project("k", 0, bank[1], seg).then_inc(k_mm, 1)
                if not start:
                    pe.wait_ge(st_sb, 2 * t - 1)
                project("q", 1, bank[2], seg).then_inc(q_mm, 1)
                if not start:
                    pe.wait_ge(st_sb, 2 * t)
                project("k", 1, bank[3], seg).then_inc(k_mm, 1)
                for b in range(2):
                    if not (first and seg <= 1):
                        pe.wait_ge(acc_sb, 2 * t - 3 + b)
                    for j in range(2):
                        toks = slice(seg * SEG + (2 * b + j) * P, seg * SEG + (2 * b + j + 1) * P)
                        for f in range(KT):
                            last = three_passes(nc, bank[4 + b][:, j * HID:(j + 1) * HID],
                                                (keep.xT_hi[:, f, toks], keep.xT_lo[:, f, toks]),
                                                (w_hi[:, f, 768:1024], w_lo[:, f, 768:1024]), f == 0, f == KT - 1)
                    last.then_inc(v_mm, 1)
                for a in range(2):
                    if not start:
                        s1 = (seg - 1) % SEGS
                        pe.wait_ge(state_sb, states(t - 1, s1, a, n_states(s1)))
                    project("g", a, bank[6 + a], seg).then_inc(g_mm, 1)
                for a in range(2):
                    pe.wait_ge(k_sb, 2 * t + 1 + a)
                    pe.wait_ge(q_sb, 2 * t + 1)
                    for j in range(TPS):
                        last = pe.transpose(bank[a][:, j * P:(j + 1) * P], k[:, a, j * P:(j + 1) * P], keep.ident[:])
                    last.then_inc(t_mm, 1)
                for a in range(2):
                    pe.wait_ge(q_sb, 2 * t + 2)
                    pe.wait_ge(k_sb, 2 * t + 2)
                    for j in range(TPS):
                        cols = slice(j * P, (j + 1) * P)
                        last = pe.matmul(bank[2 + a][:, cols], k[:, a, cols], q[:, a, cols], start=True, stop=True)
                    last.then_inc(s_mm, 1)
                if not start:
                    if seg == 1:
                        pe.wait_ge(wo_done, 2 * hp + 2)
                    out_projection(pe, t - 1, 2 * t + 2)
                for a in range(2):
                    pe.wait_ge(th_sb, 2 * t + 1 + a)
                    pe.wait_ge(kd_sb, 2 * t + 1 + a)
                    pe.wait_ge(v_sb, 2 * t + 2)
                    for j in range(TPS):
                        last = pe.matmul(bank[6 + a][:, j * P:(j + 1) * P], kd[:, a, j * P:(j + 1) * P], v[:, j, a, :], start=True, stop=True)
                    last.then_inc(d_mm, 1)
                if first and seg + 1 < SEGS:
                    pe.wait_ge(st_sb, 2 * t + 2)
                    norms.pe_turn(pe, seg + 1)
                for a in range(2):
                    pe.wait_ge(st_sb, 2 * t + 1 + a)
                    pe.wait_ge(qd_sb, 2 * t + 1 + a)
                    pe.wait_ge(kd_sb, 2 * t + 1 + a)
                    for j in range(TPS):
                        cols = slice(j * P, (j + 1) * P)
                        fresh = seg % 2 == 0 and j == 0
                        last = pe.matmul(bank[a][:, cols], v[:, j, a, :], st[:, a, cols], start=True, stop=fresh)
                        if not fresh:
                            if j:
                                pe.wait_ge(state_sb, states(t, seg, a, j))
                            last = pe.matmul(bank[a][:, cols], state[:, a, j, :], qd[:, a, cols], start=False, stop=True)
                    last.then_inc(o_mm, 1)

        def out_projection(pe, t, v_count):
            pe.wait_ge(v_sb, v_count)
            pe.wait_ge(g_sb, 2 * t + 2)
            for f in range(KT):
                for a in range(2):
                    last = three_passes(nc, bank[4 + f][:], (wo_hi[:, a, f * P:(f + 1) * P], wo_lo[:, a, f * P:(f + 1) * P]),
                                        (g_hi[:, a, :], g_lo[:, a, :]), a == 0, a == 1)
                last.then_inc(w_mm, 1)

        def act_split(act, hp):
            act.wait_ge(raw_in, DMA * (hp + 1))
            for f in range(KT):
                act.activation(w_hi[:, f, :], raw[:, f, :], ACT.Copy).then_inc(w_hi_done, 1)

        def act_pass(act, hp, first, last):
            for seg in range(SEGS):
                t = 4 * hp + seg
                start = first and seg == 0
                for a in range(2):
                    act.wait_ge(q_mm, 2 * t + 1 + a)
                    if not start:
                        act.wait_ge(qd_sb, 2 * t - 1 + a)
                    act.activation(q[:, a, :], bank[2 * a][:], ACT.Silu).then_inc(q_sb, 1)
                    act.wait_ge(k_mm, 2 * t + 1 + a)
                    act.activation(k[:, a, :], bank[2 * a + 1][:], ACT.Silu).then_inc(k_sb, 1)
                for b in range(2):
                    act.wait_ge(v_mm, 2 * t + 1 + b)
                    act.activation(v[:, 2 * b:2 * b + 2, :, :].rearrange("p c a e -> p (c a e)"), bank[4 + b][:], ACT.Silu).then_inc(v_sb, 1)
                for a in range(2):
                    act.wait_ge(g_mm, 2 * t + 1 + a)
                    if not start:
                        act.wait_ge(g_sb, 2 * t - 1 + a)
                    act.activation(th[:, a, :], bank[6 + a][:], ACT.Tanh, scale=0.5).then_inc(th_sb, 1)
                if seg == SEGS - 1 and not last:
                    act_split(act, hp + 1)
                if seg == 0:
                    act.wait_ge(heads_sb, hp + 1)
                for a in range(2):
                    act.wait_ge(t_mm, 2 * t + 1 + a)
                    act.activation(kd[:, a, :], bank[a][:], ACT.Copy, scale=k_dec[:, a:a + 1]).then_inc(kd_sb, 1)
                if first and seg + 1 < SEGS:
                    norms.act_root(act, seg + 3)
                    norms.act_apply(act, seg + 3)
                for a in range(2):
                    act.wait_ge(o_mm, 2 * t + 1 + a)
                    act.activation(o[:, a, :], bank[a][:], ACT.Copy).then_inc(o_sb, 1)
                    act.wait_ge(o_sb, 2 * t + 1 + a)
                    if not start:
                        act.wait_ge(squares_sb, 2 * t - 1 + a)
                    act.activation(sq[:, a, :], o[:, a, :], ACT.Square).then_inc(sq_sb, 1)
                if first and seg == 1:
                    decays.act_heads(act, 2, NH)

        def gate(dve, chain, t):
            for a in range(2):
                dve.wait_ge(o_sb, 2 * t + 1 + a)
                dve.wait_ge(th_sb, 2 * t + 1 + a)
                chain.link(dve.tensor_scalar(g[:, a, :], th[:, a, :], 1.0, half_norm[:, a:a + 1], ALU.add, ALU.mult))
                chain.link(dve.tensor_tensor(g[:, a, :], g[:, a, :], o[:, a, :], ALU.mult))
                chain.link(dve.tensor_copy(g_hi[:, a, :], g[:, a, :]))
                dve.tensor_tensor(g_lo[:, a, :], g[:, a, :], g_hi[:, a, :].bitcast(F32), ALU.subtract).then_inc(g_sb, 1)

        def dve_split(dve, hp):
            for f in range(KT):
                dve.wait_ge(w_hi_done, 2 * hp + 1 + f)
                dve.tensor_tensor(w_lo[:, f, :], raw[:, f, :], w_hi[:, f, :].bitcast(F32), ALU.subtract).then_inc(w_lo_done, 1)

        def accumulate(dve, t, seg):
            for f in range(KT):
                dve.wait_ge(w_mm, 2 * t + 1 + f)
                part = keep.acc[:, seg, f, :]
                dve.tensor_tensor(part, part, bank[4 + f][:], ALU.add).then_inc(acc_sb, 1)

        def dve_pass(dve, hp, first, last, chain, norms_chain=None):
            for seg in range(SEGS):
                t = 4 * hp + seg
                start = first and seg == 0
                if not start:
                    gate(dve, chain, t - 1)
                if seg == 0:
                    two = bass.ds(2 * hp, 2)
                    dve.wait_ge(decays.masked, 2 if first else NH)
                    chain.step(dve.tensor_copy(mask[:], decays.mask[:, two, :]))
                    chain.step(dve.tensor_copy(q_dec[:], decays.query[:, two, :]))
                    chain.step(dve.tensor_copy(k_dec[:], decays.key[:, two]))
                    chain.step(dve.tensor_copy(c_dec[:], decays.chunk[:, two]))
                    dve.tensor_scalar(half_norm[:], norm_in[:, two], 0.5, None, ALU.mult).then_inc(heads_sb, 1)
                    dve.wait_ge(heads_sb, hp + 1)
                for a in range(2):
                    dve.wait_ge(q_sb, 2 * t + 1 + a)
                    dve.tensor_tensor(C4(qd[:, a, :]), C4(q[:, a, :]), q_dec[:, a:a + 1, :].broadcast_to([P, TPS, P]),
                                      ALU.mult).then_inc(qd_sb, 1)
                for a in range(2):
                    dve.wait_ge(s_mm, 2 * t + 1 + a)
                    dve.tensor_tensor(C4(st[:, a, :]), C4(bank[2 + a][:]), mask[:, a:a + 1, :].broadcast_to([P, TPS, P]),
                                      ALU.mult).then_inc(st_sb, 1)
                if seg == SEGS - 1 and not last:
                    dve_split(dve, hp + 1)
                if not start:
                    accumulate(dve, t - 1, (seg - 1) % SEGS)
                if seg == 0:
                    dve.wait_ge(raw_out_in, DMA * (hp + 1))
                    dve.tensor_copy(wo_hi[:], raw_out[:]).then_inc(wo_done, 1)
                    dve.wait_ge(wo_done, 2 * hp + 1)
                    dve.tensor_tensor(wo_lo[:], raw_out[:], wo_hi[:].bitcast(F32), ALU.subtract).then_inc(wo_done, 1)
                for a in range(2):
                    dve.wait_ge(d_mm, 2 * t + 1 + a)
                    for j in range(n_states(seg)):
                        grown = bank[6 + a][:, j * P:(j + 1) * P]
                        new = state[:, a, (j + 1) % TPS, :]
                        if seg % 2 == 0 and j == 0:
                            dve.tensor_copy(new, grown).then_inc(state_sb, 1)
                        else:
                            dve.wait_ge(state_sb, states(t, seg, a, j) if j else states(t - 1, seg - 1, a, n_states(seg - 1)))
                            dve.scalar_tensor_tensor(new, state[:, a, j, :], c_dec[:, a:a + 1], grown, ALU.mult, ALU.add).then_inc(state_sb, 1)
                if first and seg + 1 < SEGS:
                    dve_norms(dve, norms_chain, seg + 3)

        def dve_norms(dve, chain, r):
            if r <= SEGS:
                dve.wait_ge(x_in[r - 1], DMA)
            norms.dve_round(dve, chain, r)

        def pool_pass(pool, hp, first):
            for seg in range(SEGS):
                part = keep.squares[:, seg * SEG:(seg + 1) * SEG]
                for a in range(2):
                    n = 2 * (4 * hp + seg) + a
                    pool.wait_ge(sq_sb, n + 1)
                    if a:
                        pool.wait_ge(squares_sb, n)
                    pool.tensor_tensor(part, part, sq[:, a, :], ALU.add).then_inc(squares_sb, 1)
                if first and seg == 1:
                    decays.pool_heads(pool, 2, NH)

        STEPS_FIRST, STEPS = 1 + 4 + 6 * (SEGS - 1), 4 + 6 * SEGS
        with nc.Block() as block:
            @block.sync
            def _(sp):
                decays.load(sp, slope)
                tiles = x.rearrange("b (t p) f -> p (b t) f", p=P)
                for g in range(SEGS):
                    at = slice(g * TPS, (g + 1) * TPS)
                    sp.dma_start(keep.x[:, at, :], tiles[:, at, :]).then_inc(x_in[g], DMA)
                    if g == 0:
                        sp.dma_start(raw[:], w_pairs[0]).then_inc(raw_in, DMA)
                        sp.dma_start(norm_in[:], norm_w).then_inc(norm_sem, DMA)
                sp.dma_start(raw_out[:], wout_pairs[0]).then_inc(raw_out_in, DMA)
                sp.wait_ge(zeroed, 2)
                for rows in zero_parts(sorted_x):
                    sp.dma_start(rows, zeros[:].rearrange("p (r f) -> p r f", r=1).broadcast_to([P, ZERO_ROWS, HID])).then_inc(keep.slots_zero, DMA)
                with sp.Fori(0, PAIRS - 1) as hp:
                    sp.wait_ge(w_lo_done, 2 * hp + 2)
                    sp.dma_start(raw[:], w_pairs[bass.ds(hp + 1, 1)].rearrange("a p k n -> (a p) k n")).then_inc(raw_in, DMA)
                    sp.wait_ge(wo_done, 2 * hp + 2)
                    sp.dma_start(raw_out[:], wout_pairs[bass.ds(hp + 1, 1)].rearrange("a p k n -> (a p) k n")).then_inc(raw_out_in, DMA)

            @block.gpsimd
            def _(pool):
                decays.pool_start(pool)
                pool.memset(zeros[:], 0.0).then_inc(zeroed, 1)
                pool.memset(keep.squares[:], 0.0).then_inc(zeroed, 1)
                pool.wait_ge(zeroed, 2)
                decays.pool_heads(pool, 0, 2)
                pool_pass(pool, 0, True)
                with pool.Fori(1, PAIRS) as hp:
                    pool_pass(pool, hp, False)

            @block.vector
            def _(dve):
                chain = Chain(dve, own)
                norms_chain = Chain(dve, norms_own)
                decays.dve_start(dve)
                dve_norms(dve, norms_chain, 1)
                dve_split(dve, 0)
                dve_norms(dve, norms_chain, 2)
                chain.link(dve.memset(keep.acc[:], 0.0))
                dve.wait_ge(norm_sem, DMA)
                dve_pass(dve, 0, True, False, chain, norms_chain)
                assert chain.n == STEPS_FIRST
                with dve.Fori(1, PAIRS - 1) as hp:
                    chain = Chain(dve, own, (hp - 1) * STEPS + STEPS_FIRST)
                    dve_pass(dve, hp, False, False, chain)
                    assert chain.n == STEPS
                chain = Chain(dve, own, (PAIRS - 2) * STEPS + STEPS_FIRST)
                dve_pass(dve, PAIRS - 1, False, True, chain)
                gate(dve, chain, 4 * PAIRS - 1)
                accumulate(dve, 4 * PAIRS - 1, SEGS - 1)

            @block.scalar
            def _(act):
                norms.act_root(act, 1)
                norms.act_apply(act, 1)
                act_split(act, 0)
                norms.act_root(act, 2)
                norms.act_apply(act, 2)
                decays.act_start(act)
                act_pass(act, 0, True, False)
                with act.Fori(1, PAIRS - 1) as hp:
                    act_pass(act, hp, False, False)
                act_pass(act, PAIRS - 1, False, True)

            @block.tensor
            def _(pe):
                pe.wait_ge(decays.numbered, 5)
                norms.pe_turn(pe, 0)
                pe_pass(pe, 0, True)
                with pe.Fori(1, PAIRS) as hp:
                    pe_pass(pe, hp, False)
                out_projection(pe, 4 * PAIRS - 1, 8 * PAIRS)


def allocate(nc, keep, c):
    keep.x = c.sb("x", [P, TT, HID])
    keep.xT_hi = c.sb("xT_hi", [P, KT, TOK], F32R)
    keep.xT_lo = c.sb("xT_lo", [P, KT, TOK], F32R)
    keep.ident = c.sb("ident", [P, P])


def lay_out_linear(w_qkv, w_gate, w_out, norm_w):
    qkv = w_qkv.reshape(PAIRS, 2, 3, HD, KT, P)
    gate = w_gate.reshape(PAIRS, 2, HD, KT, P)
    blocks = [qkv[:, 0, 0], qkv[:, 0, 1], qkv[:, 1, 0], qkv[:, 1, 1], gate[:, 0], gate[:, 1], qkv[:, 0, 2], qkv[:, 1, 2]]
    w = np.stack(blocks, 1)
    w = w.transpose(0, 4, 3, 1, 2).reshape(PAIRS, P, KT, 8 * HD)
    wo = w_out.reshape(HID, PAIRS, 2, HD).transpose(1, 3, 2, 0)
    return {"wp": np.ascontiguousarray(w), "wop": np.ascontiguousarray(wo), "nw": np.ascontiguousarray(norm_w.reshape(NH, HD).T)}


RSQRT_SEED = 0x5f3759df


class Affine:

    def __init__(self, c, tag, used):
        sb = lambda n, shape, dt=F32: c.sb(f"{tag}_{n}", shape, dt)
        self.stats, self.mean_var = sb("stats", [P, TPS, 6]), sb("mean_var", [P, TPS, 2])
        self.var, self.scale, self.shift, self.t = (sb(n, [P, TPS]) for n in ("var", "scale", "shift", "t"))
        self.stats_ready, self.ready = c.sem(f"{tag}_stats"), c.sem(f"{tag}_affine")
        self.used = used

    def statistics(self, dve, chain, tiles, g, half):
        js = (2 * half, 2 * half + 1)
        for j in js:
            chain.step(dve.bn_stats(self.stats[:, j, :], tiles[:, j, :]))
        chain.wait()
        for j in js:
            if g and j == 0:
                dve.wait_ge(self.ready, g)
            dve.bn_aggr(self.mean_var[:, j, :], self.stats[:, j, :]).then_inc(self.stats_ready, 1)

    def scale_and_shift(self, eng, chain, g):
        eng.wait_ge(self.stats_ready, TPS * (g + 1))
        chain.link(eng.tensor_scalar(self.var[:], self.mean_var[:, :, 1], LN_EPS, None, ALU.add))
        if g:
            eng.wait_ge(self.used, g)
        inverse_root(eng, chain, self.var, self.scale, self.t)
        chain.link(eng.tensor_scalar(self.t[:], self.mean_var[:, :, 0], -1.0, None, ALU.mult))
        eng.tensor_tensor(self.shift[:], self.t[:], self.scale[:], ALU.mult).then_inc(self.ready, 1)


def inverse_root(eng, chain, v, r, t):
    chain.link(eng.tensor_scalar(r[:].bitcast(I32), v[:].bitcast(I32), -0.5, float(RSQRT_SEED), ALU.mult, ALU.add))
    for _ in range(3):
        chain.link(eng.tensor_tensor(t[:], r[:], r[:], ALU.mult))
        chain.link(eng.tensor_tensor(t[:], t[:], v[:], ALU.mult))
        chain.link(eng.tensor_scalar(t[:], t[:], -0.5, 1.5, ALU.mult, ALU.add))
        chain.link(eng.tensor_tensor(r[:], t[:], r[:], ALU.mult))


class AddNorm:

    def __init__(self, c, keep, tag, y):
        self.x, self.y = keep.x, y
        self.z = c.sb(f"{tag}_z", [P, TPS, HID])
        self.z_ready, self.added = c.sem(f"{tag}_z"), c.sem(f"{tag}_added")
        self.affine = Affine(c, tag, self.z_ready)

    def statistics(self, dve, chain, g, half):
        self.affine.statistics(dve, chain, self.y[:, g * TPS:(g + 1) * TPS, :], g, half)

    def act_apply(self, act, g):
        act.wait_ge(self.affine.ready, g + 1)
        if g:
            act.wait_ge(self.added, g)
        apply(act, self.z, self.y[:, g * TPS:(g + 1) * TPS, :], self.affine).then_inc(self.z_ready, 1)

    def add(self, eng, g):
        eng.wait_ge(self.z_ready, g + 1)
        xs = self.x[:, g * TPS:(g + 1) * TPS, :]
        eng.tensor_tensor(xs, xs, self.z[:], ALU.add).then_inc(self.added, 1)


def apply(act, z, tiles, affine):
    for j in range(TPS):
        last = act.activation(z[:, j, :], tiles[:, j, :], ACT.Identity, scale=affine.scale[:, j:j + 1], bias=affine.shift[:, j:j + 1])
    return last


class TurnNorm:

    def __init__(self, c, keep, tag, banks, z_all=None):
        self.keep, self.banks, self.z_all = keep, banks, z_all
        self.z_one = c.sb(f"{tag}_z", [P, TPS, HID]) if z_all is None else None
        self.z_ready, self.turned, self.high, self.low = (c.sem(f"{tag}_{n}") for n in ("z", "turned", "high", "low"))
        self.affine = Affine(c, tag, self.z_ready)

    def z(self, g):
        return self.z_one if self.z_all is None else self.z_all[:, g * TPS:(g + 1) * TPS, :]

    def statistics(self, dve, chain, g, half):
        self.affine.statistics(dve, chain, self.keep.x[:, g * TPS:(g + 1) * TPS, :], g, half)

    def act_apply(self, act, g):
        act.wait_ge(self.affine.ready, g + 1)
        if g:
            act.wait_ge(self.turned, KT * g)
        apply(act, self.z(g), self.keep.x[:, g * TPS:(g + 1) * TPS, :], self.affine).then_inc(self.z_ready, 1)

    def pe_turn(self, pe, g):
        pe.wait_ge(self.z_ready, g + 1)
        for k in range(KT):
            if g:
                pe.wait_ge(self.low, KT * (g - 1) + k + 1)
            for j in range(TPS):
                last = pe.transpose(self.banks[k][:, j * P:(j + 1) * P], self.z(g)[:, j, k * P:(k + 1) * P], self.keep.ident[:])
            last.then_inc(self.turned, 1)

    def act_high(self, act, g):
        for k in range(KT):
            act.wait_ge(self.turned, KT * g + k + 1)
            act.activation(self.keep.xT_hi[:, k, g * SEG:(g + 1) * SEG], self.banks[k][:], ACT.Copy).then_inc(self.high, 1)

    def dve_low(self, dve, g):
        for k in range(KT):
            dve.wait_ge(self.high, KT * g + k + 1)
            at = slice(g * SEG, (g + 1) * SEG)
            dve.tensor_tensor(self.keep.xT_lo[:, k, at], self.banks[k][:], self.keep.xT_hi[:, k, at].bitcast(F32),
                              ALU.subtract).then_inc(self.low, 1)


class Swiglu:

    def __init__(self, nc, c, keep, y, banks, widths):
        self.nc, self.keep, self.y, self.bank, self.widths = nc, keep, y, banks, widths
        self.J, self.W = len(widths), sum(widths)
        self.starts = [sum(widths[:j]) for j in range(self.J)]
        J, W = self.J, self.W
        self.raw, self.w_hi, self.w_lo = c.sb("raw", [P, KT, 2 * W]), c.sb("w_hi", [P, KT, 2 * W], F32R), c.sb("w_lo", [P, KT, 2 * W], F32R)
        self.raw_d, self.d_hi, self.d_lo = c.sb("raw_d", [P, J, HID]), c.sb("d_hi", [P, J, HID], F32R), c.sb("d_lo", [P, J, HID], F32R)
        self.silu, self.h = c.sb("silu", [P, 2, SEG]), c.sb("h", [P, 2, SEG])
        self.h_hi, self.h_lo = c.sb("h_hi", [P, 2, SEG], F32R), c.sb("h_lo", [P, 2, SEG], F32R)
        self.up_in, self.down_in, self.up_hi, self.down_hi, self.up_lo, self.down_lo = (
            c.sem(n) for n in ("up_in", "down_in", "up_hi", "down_hi", "up_lo", "down_lo"))
        self.g_mm, self.u_mm, self.down_mm, self.silu_sb, self.h_sb, self.y_sb = (
            c.sem(n) for n in ("g_mm", "u_mm", "down_mm", "silu", "h", "y"))

    def columns(self, j):
        return [slice(b + self.starts[j], b + self.starts[j] + self.widths[j]) for b in (0, self.W)]

    def load(self, sp, w_up, w_down):
        for f in range(KT):
            sp.dma_start(self.raw[:, f, :], w_up[f * P:(f + 1) * P, :]).then_inc(self.up_in, DMA)
        for j in range(self.J):
            w = self.widths[j]
            sp.dma_start(self.raw_d[0:w, j, :], w_down[self.starts[j]:self.starts[j] + w, :]).then_inc(self.down_in, DMA)

    def act_high(self, act, j):
        w = self.widths[j]
        act.wait_ge(self.up_in, KT * DMA)
        for cols in self.columns(j):
            act.activation(self.w_hi[:, :, cols], self.raw[:, :, cols], ACT.Copy).then_inc(self.up_hi, 1)
        act.wait_ge(self.down_in, self.J * DMA)
        act.activation(self.d_hi[0:w, j, :], self.raw_d[0:w, j, :], ACT.Copy).then_inc(self.down_hi, 1)

    def dve_low(self, dve, j):
        w = self.widths[j]
        for i, cols in enumerate(self.columns(j)):
            dve.wait_ge(self.up_hi, 2 * j + i + 1)
            dve.tensor_tensor(self.w_lo[:, :, cols], self.raw[:, :, cols], self.w_hi[:, :, cols].bitcast(F32), ALU.subtract).then_inc(self.up_lo, 1)
        dve.wait_ge(self.down_hi, j + 1)
        dve.tensor_tensor(self.d_lo[0:w, j, :], self.raw_d[0:w, j, :], self.d_hi[0:w, j, :].bitcast(F32), ALU.subtract).then_inc(self.down_lo, 1)

    def act_step(self, act, g, j):
        n, w = g * self.J + j, self.widths[j]
        b = n % 2
        act.wait_ge(self.g_mm, n + 1)
        if n >= 2:
            act.wait_ge(self.h_sb, n - 1)
        act.activation(self.silu[0:w, b, :], self.bank[b][0:w, :], ACT.Silu).then_inc(self.silu_sb, 1)

    def act_output(self, act, g):
        act.wait_ge(self.down_mm, (g + 1) * self.J)
        for i in range(2):
            t = g * TPS + 2 * i
            act.activation(self.y[:, t:t + 2, :].rearrange("p t f -> p (t f)"), self.bank[4 + i][:], ACT.Copy).then_inc(self.y_sb, 1)

    def dve_step(self, dve, chain, g, j):
        n, w = g * self.J + j, self.widths[j]
        b = n % 2
        h, h_hi, h_lo = (a[0:w, b, :] for a in (self.h, self.h_hi, self.h_lo))
        dve.wait_ge(self.silu_sb, n + 1)
        dve.wait_ge(self.u_mm, n + 1)
        chain.link(dve.tensor_tensor(h, self.silu[0:w, b, :], self.bank[2 + b][0:w, :], ALU.mult))
        if n >= 2:
            dve.wait_ge(self.down_mm, n - 1)
        chain.link(dve.tensor_copy(h_hi, h))
        dve.tensor_tensor(h_lo, h, h_hi.bitcast(F32), ALU.subtract).then_inc(self.h_sb, 1)

    def pe_up(self, pe, g, j):
        n, w = g * self.J + j, self.widths[j]
        b = n % 2
        toks = slice(g * SEG, (g + 1) * SEG)
        if g == 0:
            pe.wait_ge(self.up_lo, 2 * j + 2)
        if n >= 2:
            pe.wait_ge(self.h_sb, n - 1)
        for cols, to, sem in zip(self.columns(j), (self.bank[b], self.bank[2 + b]), (self.g_mm, self.u_mm)):
            for f in range(KT):
                last = three_passes(self.nc, to[0:w, :], (self.w_hi[:, f, cols], self.w_lo[:, f, cols]),
                                    (self.keep.xT_hi[:, f, toks], self.keep.xT_lo[:, f, toks]), f == 0, f == KT - 1)
            last.then_inc(sem, 1)

    def pe_down(self, pe, g, j):
        n, w = g * self.J + j, self.widths[j]
        b = n % 2
        pe.wait_ge(self.h_sb, n + 1)
        if g == 0:
            pe.wait_ge(self.down_lo, j + 1)
        if g and j == 0:
            pe.wait_ge(self.y_sb, 2 * g)
        for t in range(TPS):
            to = self.bank[4 + t // 2][:, t % 2 * HID:(t % 2 + 1) * HID]
            toks = slice(t * P, (t + 1) * P)
            last = three_passes(self.nc, to, (self.h_hi[0:w, b, toks], self.h_lo[0:w, b, toks]), (self.d_hi[0:w, j, :], self.d_lo[0:w, j, :]),
                                j == 0 and t % 2 == 0, j == self.J - 1, skip=True)
        last.then_inc(self.down_mm, 1)


def feed_forward(nc, keep, y, w_up, w_down, out):
    with Scope(nc, "ffn") as c:
        bank = c.banks(8)
        net = Swiglu(nc, c, keep, y, bank, [P] * 8)
        before = AddNorm(c, keep, "before", y)
        turn = TurnNorm(c, keep, "turn", bank[6:8])
        after = AddNorm(c, keep, "after", y)
        own, pool_own, stored = c.sem("own"), c.sem("pool_own"), c.sem("stored")
        J = net.J
        with nc.Block() as block:
            @block.sync
            def _(sp):
                net.load(sp, w_up, w_down)
                for g in range(SEGS):
                    sp.wait_ge(after.added, g + 1)
                    at = slice(g * TPS, (g + 1) * TPS)
                    sp.dma_start(out[:, at, :], keep.x[:, at, :]).then_inc(stored, DMA)
                sp.wait_ge(stored, SEGS * DMA)

            @block.gpsimd
            def _(pool):
                chain = Chain(pool, pool_own)
                before.affine.scale_and_shift(pool, chain, 1)
                before.add(pool, 1)
                for g in range(SEGS):
                    if g + 1 < SEGS:
                        turn.affine.scale_and_shift(pool, chain, g + 1)
                    if g:
                        after.affine.scale_and_shift(pool, chain, g - 1)
                        after.add(pool, g - 1)
                    if g + 2 < SEGS:
                        before.affine.scale_and_shift(pool, chain, g + 2)
                        before.add(pool, g + 2)

            @block.vector
            def _(dve):
                chain = Chain(dve, own)
                for half in range(2):
                    before.statistics(dve, chain, 0, half)
                before.affine.scale_and_shift(dve, chain, 0)
                net.dve_low(dve, 0)
                before.add(dve, 0)
                dve.wait_ge(before.added, 1)
                for half in range(2):
                    turn.statistics(dve, chain, 0, half)
                turn.affine.scale_and_shift(dve, chain, 0)
                for half in range(2):
                    before.statistics(dve, chain, 1, half)
                turn.dve_low(dve, 0)
                net.dve_low(dve, 1)
                for g in range(SEGS):
                    for j in range(J):
                        if g == 0 and j + 2 < J:
                            net.dve_low(dve, j + 2)
                        net.dve_step(dve, chain, g, j)
                        if j < 2 and g + 1 < SEGS:
                            dve.wait_ge(before.added, g + 2)
                            turn.statistics(dve, chain, g + 1, j)
                        if 2 <= j < 4 and g:
                            dve.wait_ge(net.y_sb, 2 * g)
                            after.statistics(dve, chain, g - 1, j - 2)
                        if j == 4 and g + 1 < SEGS:
                            turn.dve_low(dve, g + 1)
                        if 5 <= j < 7 and g + 2 < SEGS:
                            before.statistics(dve, chain, g + 2, j - 5)
                for half in range(2):
                    dve.wait_ge(net.y_sb, 2 * SEGS - 1 + half)
                    after.statistics(dve, chain, SEGS - 1, half)
                after.affine.scale_and_shift(dve, chain, SEGS - 1)
                after.add(dve, SEGS - 1)

            @block.scalar
            def _(act):
                net.act_high(act, 0)
                before.act_apply(act, 0)
                net.act_high(act, 1)
                turn.act_apply(act, 0)
                turn.act_high(act, 0)
                before.act_apply(act, 1)
                for g in range(SEGS):
                    for j in range(J):
                        if g == 0 and j + 2 < J:
                            net.act_high(act, j + 2)
                        net.act_step(act, g, j)
                        if g + 1 < SEGS:
                            if j == 2:
                                turn.act_apply(act, g + 1)
                            if j == 3:
                                turn.act_high(act, g + 1)
                        if j == 4 and g:
                            after.act_apply(act, g - 1)
                        if j == 1 and g:
                            net.act_output(act, g - 1)
                        if j == 7 and g + 2 < SEGS:
                            before.act_apply(act, g + 2)
                net.act_output(act, SEGS - 1)
                after.act_apply(act, SEGS - 1)

            @block.tensor
            def _(pe):
                turn.pe_turn(pe, 0)
                for g in range(SEGS):
                    pe.wait_ge(turn.low, KT * (g + 1))
                    for j in range(J):
                        net.pe_up(pe, g, j)
                        if j >= 2 or g:
                            n = g * J + j - 2
                            net.pe_down(pe, n // J, n % J)
                        if j == 3 and g + 1 < SEGS:
                            turn.pe_turn(pe, g + 1)
                for j in (J - 2, J - 1):
                    net.pe_down(pe, SEGS - 1, j)


NE, TOP, INNER = 16, 2, 176
IH = INNER // 2
SLOT_TILES = (TOP * TOK + NE * (P - 1)) // P
SLOT_TILES += SLOT_TILES % 2
SLOTS = SLOT_TILES * P
ZERO_ROWS = 8


def zero_parts(sorted_x):
    parts = sorted_x.rearrange("(n p r) f -> n p r f", p=P, r=ZERO_ROWS)
    return [parts[n] for n in range(parts.shape[0])]


class Router:

    def __init__(self, nc, c, keep, normed, banks):
        self.nc, self.keep, self.normed = nc, keep, normed
        self.logits_bank, self.turned_bank, self.ranks_bank = banks
        self.gate = c.sb("gate", [P, KT, P])
        self.g_hi, self.g_lo = c.sb("g_hi", [P, KT, P], F32R), c.sb("g_lo", [P, KT, P], F32R)
        self.logits_T = c.sb("logits_T", [NE, TPS, P])
        full = lambda n, dt=F32: c.sb(n, [P, TT, NE], dt)
        self.score, self.key, self.rest, self.one1, self.one2 = (full(n) for n in ("score", "key", "rest", "one1", "one2"))
        self.top, self.total, self.best, self.where = (c.sb(n, [P, TT]) for n in ("top", "total", "best", "where"))
        self.chosen = full("chosen", BF16)
        self.before, self.every = c.sb("before", [P, P], BF16), c.sb("every", [P, P], BF16)
        self.rank_first, self.thresholds = c.sb("rank_first", [P, NE]), c.sb("thresholds", [P, NE])
        self.upto, self.counts_over = c.sb("upto", [P, NE, NE]), c.sb("counts_over", [P, NE, NE])
        self.tiles, self.tiles_to, self.base = (c.sb(n, [P, NE]) for n in ("tiles", "tiles_to", "base"))
        self.tile_no, self.expert_f = c.sb("tile_no", [1, SLOT_TILES]), c.sb("expert_f", [1, SLOT_TILES])
        self.passed = c.sb("passed", [1, SLOT_TILES, NE])
        self.zeroed, self.gate_in, self.gate_hi, self.gate_lo, self.made, self.logits_mm, self.logits_sb, self.logits_T_mm = (
            c.sem(n) for n in ("zeroed", "gate_in", "gate_hi", "gate_lo", "made", "logits_mm", "logits_sb", "logits_T_mm"))
        self.score_in, self.shifted, self.exps, self.chosen_ready, self.ranks, self.scattered, self.slots_ready = (
            c.sem(n) for n in ("score_in", "shifted", "exps", "chosen_ready", "ranks", "scattered", "slots"))
        self.over_e = lambda a: a.rearrange("p (t o) -> p t o", o=1).broadcast_to([P, TT, NE])
        self.over_t = lambda a: a.rearrange("p (o e) -> p o e", o=1).broadcast_to([P, TT, NE])

    def load(self, sp, gate_w):
        sp.wait_ge(self.zeroed, 1)
        sp.dma_start(self.gate[:, :, 0:NE], gate_w).then_inc(self.gate_in, DMA)

    def pool_constants(self, pool):
        made, upto, before = self.made, self.upto, self.before
        iota = lambda out, pattern, base, mult: pool.iota(out, pattern=pattern, base=base, channel_multiplier=mult,
                                                          allow_small_or_imprecise_dtypes=True).then_inc(made, 1)
        iota(self.rank_first[:], [[-1, NE]], NE, 0)
        iota(self.thresholds[:], [[P, NE]], 0, 0)
        iota(self.tile_no[:], [[1, SLOT_TILES]], 0, 0)
        pool.memset(upto[:], 1.0).then_inc(made, 1)
        pool.memset(before[:], 1.0).then_inc(made, 1)
        pool.memset(self.every[:], 1.0).then_inc(made, 1)
        pool.wait_ge(made, 6)
        pool.affine_select(out=upto[:], in_=upto[:], compare_op=ALU.is_ge, fill=0.0, base=0,
                           pattern=[[1, NE], [-1, NE]], channel_multiplier=0).then_inc(made, 1)
        pool.affine_select(out=before[:], in_=before[:], compare_op=ALU.is_gt, fill=0.0, base=0,
                           pattern=[[1, P]], channel_multiplier=-1).then_inc(made, 1)

    def pool_scatter(self, pool, sorted_x):
        pool.wait_ge(self.keep.slots_zero, SLOT_TILES // ZERO_ROWS * DMA)
        pool.wait_ge(self.slots_ready, 1)
        for t in range(TT):
            for slot in (self.keep.slot1, self.keep.slot2):
                pool.indirect_dma_start(out=sorted_x, out_offset=bass.IndirectOffsetOnAxis(ap=slot[:, t:t + 1], axis=0),
                                        in_=self.normed[:, t, :], in_offset=None).then_inc(self.scattered, DMA)
        pool.wait_ge(self.scattered, 2 * TT * DMA)

    def act_gate(self, act):
        act.wait_ge(self.gate_in, DMA)
        act.activation(self.g_hi[:], self.gate[:], ACT.Copy).then_inc(self.gate_hi, 1)

    def dve_gate(self, dve):
        dve.wait_ge(self.gate_hi, 1)
        dve.tensor_tensor(self.g_lo[:], self.gate[:], self.g_hi[:].bitcast(F32), ALU.subtract).then_inc(self.gate_lo, 1)

    def pe_logits(self, pe, g):
        toks = slice(g * SEG, (g + 1) * SEG)
        if g == 0:
            pe.wait_ge(self.gate_lo, 1)
        else:
            pe.wait_ge(self.logits_sb, g)
        for f in range(KT):
            last = three_passes(self.nc, self.logits_bank[:], (self.g_hi[:, f, :], self.g_lo[:, f, :]),
                                (self.keep.xT_hi[:, f, toks], self.keep.xT_lo[:, f, toks]), f == 0, f == KT - 1)
        last.then_inc(self.logits_mm, 1)

    def act_logits(self, act, g):
        act.wait_ge(self.logits_mm, g + 1)
        if g:
            act.wait_ge(self.logits_T_mm, g)
        act.activation(self.logits_T[:].rearrange("e t p -> e (t p)"), self.logits_bank[0:NE, :], ACT.Copy).then_inc(self.logits_sb, 1)

    def pe_turn(self, pe, g):
        pe.wait_ge(self.logits_sb, g + 1)
        if g:
            pe.wait_ge(self.score_in, g)
        for t in range(TPS):
            last = pe.transpose(self.turned_bank[:, t * NE:(t + 1) * NE], self.logits_T[:, t, :], self.keep.ident[0:NE, 0:NE])
        last.then_inc(self.logits_T_mm, 1)

    def act_score(self, act, g):
        act.wait_ge(self.logits_T_mm, g + 1)
        act.activation(self.score[:, g * TPS:(g + 1) * TPS, :].rearrange("p t e -> p (t e)"), self.turned_bank[:, 0:TPS * NE],
                       ACT.Copy).then_inc(self.score_in, 1)

    def dve_shift(self, dve, chain):
        score, top = self.score, self.top
        dve.wait_ge(self.score_in, SEGS)
        chain.link(dve.tensor_reduce(top[:], score[:], AX.X, ALU.max))
        dve.tensor_tensor(score[:], score[:], self.over_e(top[:]), ALU.subtract).then_inc(self.shifted, 1)

    def act_exp(self, act):
        act.wait_ge(self.shifted, 1)
        act.activation(self.score[:], self.score[:], ACT.Exp).then_inc(self.exps, 1)

    def dve_scores(self, dve, chain):
        score, top, total = self.score, self.top, self.total
        dve.wait_ge(self.exps, 1)
        chain.link(dve.tensor_reduce(total[:], score[:], AX.X, ALU.add))
        chain.link(dve.reciprocal(top[:], total[:]))
        chain.link(dve.tensor_tensor(score[:], score[:], self.over_e(top[:]), ALU.mult))

    def dve_choose(self, dve, chain, n):
        key, best = self.key, self.best
        left, one, weight = ((self.score, self.one1, self.keep.weight1), (self.rest, self.one2, self.keep.weight2))[n]
        chain.link(dve.tensor_reduce(weight[:], left[:], AX.X, ALU.max))
        chain.link(dve.tensor_tensor(key[:], left[:], self.over_e(weight[:]), ALU.is_equal))
        dve.wait_ge(self.made, 8)
        chain.link(dve.tensor_tensor(key[:], key[:], self.over_t(self.rank_first[:]), ALU.mult))
        chain.link(dve.tensor_reduce(best[:], key[:], AX.X, ALU.max))
        chain.link(dve.tensor_tensor(one[:], key[:], self.over_e(best[:]), ALU.is_equal))
        if n == 0:
            chain.link(dve.scalar_tensor_tensor(self.rest[:], one[:], -2.0, self.score[:], ALU.mult, ALU.add))
        else:
            dve.tensor_tensor(self.chosen[:], self.one1[:], self.one2[:], ALU.add).then_inc(self.chosen_ready, 1)

    def pe_ranks(self, pe):
        chosen, every, bank = self.chosen, self.every, self.ranks_bank
        pe.wait_ge(self.chosen_ready, 1)
        pe.wait_ge(self.made, 8)
        for t in range(TT):
            pe.matmul(bank[:, TT * NE:TT * NE + NE], every[:], chosen[:, t, :], start=t == 0, stop=t == TT - 1, skip_group_check=True)
        pe.matmul(bank[:, 0:TT * NE], self.before[:], chosen[:].rearrange("p t e -> p (t e)"), start=False, stop=False, skip_group_check=True)
        for t in range(TT - 1):
            later = TT - 1 - t
            last = pe.matmul(bank[:, (t + 1) * NE:TT * NE].rearrange("p (t e) -> p t e", e=NE), every[:],
                             chosen[:, t:t + 1, :].broadcast_to([P, later, NE]), start=False, stop=t == TT - 2, skip_group_check=True)
        last.then_inc(self.ranks, 1)

    def dve_slots(self, dve, chain):
        counts_over, tiles, tiles_to, base, rest, key, where = (
            self.counts_over, self.tiles, self.tiles_to, self.base, self.rest, self.key, self.where)
        dve.wait_ge(self.ranks, 1)
        per = lambda a: a.rearrange("p (e o) -> p e o", o=1).broadcast_to([P, NE, NE])
        along = lambda a: a.rearrange("p (o e) -> p o e", o=1).broadcast_to([P, NE, NE])
        chain.link(dve.tensor_copy(base[:], self.ranks_bank[:, TT * NE:TT * NE + NE]))
        chain.link(dve.tensor_tensor(counts_over[:], per(base[:]), along(self.thresholds[:]), ALU.is_gt))
        chain.link(dve.tensor_reduce(tiles[:], counts_over[:], AX.X, ALU.add))
        chain.link(dve.tensor_tensor(counts_over[:], self.upto[:], along(tiles[:]), ALU.mult))
        chain.link(dve.tensor_reduce(tiles_to[:], counts_over[:], AX.X, ALU.add))
        chain.link(dve.tensor_tensor(base[:], tiles_to[:], tiles[:], ALU.subtract))
        chain.link(dve.tensor_scalar(base[:], base[:], float(P), None, ALU.mult))
        chain.link(dve.tensor_tensor(rest[:], self.ranks_bank[:, 0:TT * NE].rearrange("p (t e) -> p t e", e=NE), self.over_t(base[:]), ALU.add))
        for one, slot in ((self.one1, self.keep.slot1), (self.one2, self.keep.slot2)):
            chain.link(dve.tensor_tensor(key[:], rest[:], one[:], ALU.mult))
            chain.link(dve.tensor_reduce(where[:], key[:], AX.X, ALU.add))
            last = dve.tensor_copy(slot[:], where[:])
            if one is self.one1:
                chain.link(last)
        last.then_inc(self.slots_ready, 1)

    def dve_tiles(self, dve, chain):
        ends = self.tiles_to[0:1, :].rearrange("p (o e) -> p o e", o=1).broadcast_to([1, SLOT_TILES, NE])
        numbers = self.tile_no[:].rearrange("p (i o) -> p i o", o=1).broadcast_to([1, SLOT_TILES, NE])
        chain.link(dve.tensor_tensor(self.passed[:], numbers, ends, ALU.is_ge))
        chain.link(dve.tensor_reduce(self.expert_f[:], self.passed[:], AX.X, ALU.add))
        chain.link(dve.tensor_scalar(self.expert_f[:], self.expert_f[:], float(NE - 1), None, ALU.min))
        chain.link(dve.tensor_copy(self.keep.expert_of[:], self.expert_f[:]))


def close_attention_and_route(nc, keep, y, w_up, w_down, gate_w, sorted_x):
    with Scope(nc, "route") as c:
        bank = c.banks(8)
        normed = keep.acc[:].rearrange("p s k t -> p (s k t)").rearrange("p (t f) -> p t f", f=HID)
        net = Swiglu(nc, c, keep, y, bank, [P, P, 2 * INNER - 2 * P])
        norms = Norms(c, keep, "norms", y, bank[6:8], normed)
        router = Router(nc, c, keep, normed, (bank[4], bank[5], bank[6]))
        ones = c.sb("ones", [P, 2])
        spread, root, factor = (c.sb(n, [P, TT]) for n in ("spread", "root", "factor"))
        own, ones_ready, sums, spread_ready, root_ready, factor_ready, back, y_ready = (
            c.sem(n) for n in ("own", "ones", "sums", "spread", "root", "factor", "back", "y_ready"))
        J = net.J
        STEPS = [(g, j) for g in range(SEGS) for j in range(J)]
        with nc.Block() as block:
            @block.sync
            def _(sp):
                router.load(sp, gate_w)
                net.load(sp, w_up, w_down)

            @block.gpsimd
            def _(pool):
                router.pool_constants(pool)
                router.pool_scatter(pool, sorted_x)

            @block.vector
            def _(dve):
                chain = Chain(dve, own)
                dve.memset(router.gate[:], 0.0).then_inc(router.zeroed, 1)
                dve.memset(ones[:], 1.0).then_inc(ones_ready, 1)
                dve.wait_ge(sums, 1)
                dve.tensor_scalar(spread[:], bank[5][:, 0:2 * TT].rearrange("p (t a) -> p t a", a=2)[:, :, 0],
                                  1.0 / (NH * HD), RMS_EPS, ALU.mult, ALU.add).then_inc(spread_ready, 1)
                dve.wait_ge(root_ready, 1)
                dve.reciprocal(factor[:], root[:]).then_inc(factor_ready, 1)
                router.dve_gate(dve)
                for r in range(norms.ROUNDS):
                    norms.dve_round(dve, chain, r, lambda half: dve.wait_ge(y_ready, 2 * r + half + 1))
                    if r < J:
                        net.dve_low(dve, r)
                router.dve_shift(dve, chain)
                for n, (g, j) in enumerate(STEPS):
                    net.dve_step(dve, chain, g, j)
                    if n == 0:
                        router.dve_scores(dve, chain)
                        router.dve_choose(dve, chain, 0)
                    if n == 1:
                        router.dve_choose(dve, chain, 1)
                    if n == 2:
                        router.dve_slots(dve, chain)
                    if n == 4:
                        router.dve_tiles(dve, chain)

            @block.scalar
            def _(act):
                def take_back(g):
                    for half in range(2):
                        act.wait_ge(back, 2 * g + half + 1)
                        for i in range(2):
                            t = g * TPS + 2 * half + i
                            last = act.activation(y[:, t, :], bank[2 * (g % 2) + half][:, i * HID:(i + 1) * HID], ACT.Copy, scale=factor[:, t:t + 1])
                        last.then_inc(y_ready, 1)

                act.wait_ge(spread_ready, 1)
                act.activation(root[:], spread[:], ACT.Sqrt).then_inc(root_ready, 1)
                router.act_gate(act)
                act.wait_ge(factor_ready, 1)
                take_back(0)
                for r in range(norms.ROUNDS):
                    norms.act_root(act, r)
                    if r + 1 < SEGS:
                        take_back(r + 1)
                    if r >= 3:
                        router.act_logits(act, r - 3)
                        router.act_score(act, r - 3)
                    norms.act_apply(act, r)
                    if r < J:
                        net.act_high(act, r)
                router.act_logits(act, SEGS - 1)
                router.act_score(act, SEGS - 1)
                router.act_exp(act)
                for n, (g, j) in enumerate(STEPS):
                    net.act_step(act, g, j)
                    if j == 1 and g:
                        net.act_output(act, g - 1)
                net.act_output(act, SEGS - 1)

            @block.tensor
            def _(pe):
                pe.wait_ge(ones_ready, 1)
                for t in range(TT):
                    last = pe.matmul(bank[5][:, 2 * t:2 * t + 2], keep.squares[:, t * P:(t + 1) * P], ones[:], start=True, stop=True)
                last.then_inc(sums, 1)

                def turn_back(g):
                    for half in range(2):
                        if g >= 2:
                            pe.wait_ge(y_ready, 2 * (g - 2) + half + 1)
                        for i in range(2):
                            for f in range(KT):
                                at = slice((2 * half + i) * P, (2 * half + i + 1) * P)
                                last = pe.transpose(bank[2 * (g % 2) + half][:, i * HID + f * P:i * HID + (f + 1) * P], keep.acc[:, g, f, at], keep.ident[:])
                        last.then_inc(back, 1)

                turn_back(0)
                for r in range(norms.ROUNDS):
                    if r + 1 < SEGS:
                        turn_back(r + 1)
                    if r >= 3:
                        router.pe_turn(pe, r - 3)
                    if r >= 2:
                        pe.wait_ge(norms.low, KT * (r - 1))
                        router.pe_logits(pe, r - 2)
                    if 1 <= r <= SEGS:
                        norms.pe_turn(pe, r - 1)
                router.pe_turn(pe, SEGS - 1)
                for n, (g, j) in enumerate(STEPS):
                    net.pe_up(pe, g, j)
                    if n >= 2:
                        net.pe_down(pe, *STEPS[n - 2])
                    if n == 2:
                        router.pe_ranks(pe)
                net.pe_down(pe, *STEPS[-2])
                net.pe_down(pe, *STEPS[-1])


def experts(nc, keep, w_up, w_down, sorted_x, sorted_y):
    with Scope(nc, "experts") as c:
        up, down_w = c.sb("up", [P, NE, KT, 2 * INNER]), c.sb("down", [IH, NE, 2, HID])
        two = lambda n, *shape: [c.sb(f"{n}{b}", list(shape)) for b in range(2)]
        xs, xT, silu, h, hT, ys = two("xs", P, HID), two("xT", P, KT, P), two("silu", P, INNER), two("h", P, INNER), two("hT", IH, 2, P), two("ys", P, HID)
        bank = c.banks(8)
        up_in, down_in = c.sem("up_in"), c.sem("down_in")
        xs_in = [c.sem("xs_in0"), c.sem("xs_in1")]
        stored = [c.sem("stored0"), c.sem("stored1")]
        x_turned, xT_sb, gu_mm, silu_sb, h_sb, h_turned, hT_sb, y_mm, ys_sb = (
            c.sem(n) for n in ("x_turned", "xT", "gu_mm", "silu", "h", "h_turned", "hT", "y_mm", "ys"))
        N = SLOT_TILES
        row = lambda a, i: a[bass.ds(i * P, P), :]
        assert N % 2 == 0

        def tiles(eng, body):
            body(0, 0, True)
            body(1, 1, False)
            body(2, 0, False)
            with eng.Fori(0, (N - 4) // 2) as i:
                body(2 * i + 3, 1, False)
                body(2 * i + 4, 0, False)
            body(N - 1, 1, False)

        with nc.Block() as block:
            @block.sync
            def _(sp):
                for e in range(NE):
                    sp.dma_start(up[:, e], w_up[e]).then_inc(up_in, DMA)
                    sp.dma_start(down_w[:, e], w_down[e]).then_inc(down_in, DMA)

                def store(i, b, first):
                    sp.wait_ge(ys_sb, i + 1)
                    sp.dma_start(row(sorted_y, i), ys[b][:]).then_inc(stored[b], DMA)
                tiles(sp, store)
                for b in range(2):
                    sp.wait_ge(stored[b], N // 2 * DMA)

            @block.gpsimd
            def _(pool):
                def load(i, b, first):
                    if not (isinstance(i, int) and i < 2):
                        pool.wait_ge(x_turned, i - 1)
                    pool.dma_start(xs[b][:], row(sorted_x, i)).then_inc(xs_in[b], DMA)
                tiles(pool, load)

            @block.tensor
            def _(pe):
                pe.wait_ge(up_in, NE * DMA)
                pe.wait_ge(down_in, NE * DMA)

                def turn_h(i, b):
                    pe.wait_ge(h_sb, i + 1)
                    for k in range(2):
                        last = pe.transpose(bank[4 + b][0:IH, k * P:(k + 1) * P], h[b][:, k * IH:(k + 1) * IH], keep.ident[:])
                    last.then_inc(h_turned, 1)

                def down(i, b):
                    e = pe.value_load(keep.expert_of[0:1, bass.ds(i, 1)], min_val=0, max_val=NE - 1)
                    if not (isinstance(i, int) and i < 2):
                        pe.wait_ge(ys_sb, i - 1)
                    pe.wait_ge(hT_sb, i + 1)
                    for k in range(2):
                        last = pe.matmul(bank[6 + b][:, 0:HID], hT[b][:, k, :], down_w[:, bass.ds(e, 1), k, :].rearrange("p a f -> p (a f)"),
                                         start=k == 0, stop=k == 1)
                    last.then_inc(y_mm, 1)

                def tile(i, b, first):
                    pe.wait_ge(xs_in[b], loads(i, b))
                    if not first:
                        pe.wait_ge(xT_sb, i)
                    for f in range(KT):
                        last = pe.transpose(bank[b][:, f * P:(f + 1) * P], xs[b][:, f * P:(f + 1) * P], keep.ident[:])
                    last.then_inc(x_turned, 1)
                    if not first:
                        turn_h(i - 1, 1 - b)
                    e = pe.value_load(keep.expert_of[0:1, bass.ds(i, 1)], min_val=0, max_val=NE - 1)
                    pe.wait_ge(xT_sb, i + 1)
                    if not first:
                        pe.wait_ge(h_sb, i)
                    for f in range(KT):
                        last = pe.matmul(bank[2 + b][:, 0:2 * INNER], xT[b][:, f, :], up[:, bass.ds(e, 1), f, :].rearrange("p a f -> p (a f)"),
                                         start=f == 0, stop=f == KT - 1)
                    last.then_inc(gu_mm, 1)
                    if not first:
                        down(i - 1, 1 - b)

                tiles(pe, tile)
                turn_h(N - 1, 1)
                down(N - 1, 1)

            @block.scalar
            def _(act):
                def tile(i, b, first):
                    act.wait_ge(x_turned, i + 1)
                    act.activation(xT[b][:].rearrange("p k t -> p (k t)"), bank[b][:, 0:HID], ACT.Copy).then_inc(xT_sb, 1)
                    act.wait_ge(gu_mm, i + 1)
                    if not first:
                        act.wait_ge(h_sb, i)
                    act.activation(silu[b][:], bank[2 + b][:, 0:INNER], ACT.Silu).then_inc(silu_sb, 1)
                tiles(act, tile)

            @block.vector
            def _(dve):
                def late(i, b, first):
                    dve.wait_ge(h_turned, i + 1)
                    dve.tensor_copy(hT[b][:].rearrange("p k t -> p (k t)"), bank[4 + b][0:IH, 0:HID]).then_inc(hT_sb, 1)

                def output(i, b, stores):
                    dve.wait_ge(y_mm, i + 1)
                    if not (isinstance(stores, int) and stores == 0):
                        dve.wait_ge(stored[b], stores)
                    dve.tensor_copy(ys[b][:], bank[6 + b][:, 0:HID]).then_inc(ys_sb, 1)

                def tile(i, b, first):
                    if not first:
                        late(i - 1, 1 - b, False)
                    dve.wait_ge(silu_sb, i + 1)
                    dve.tensor_tensor(h[b][:], silu[b][:], bank[2 + b][:, INNER:2 * INNER], ALU.mult).then_inc(h_sb, 1)
                    if not first:
                        output(i - 1, 1 - b, stores_before(i - 1, 1 - b))
                tiles(dve, tile)
                late(N - 1, 1, False)
                output(N - 1, 1, stores_before(N - 1, 1))


def loads(i, b):
    return (i - b) * (DMA // 2) + DMA


def stores_before(i, b):
    return (i - b) * (DMA // 2)


def combine_and_norm(nc, keep, sorted_y, y):
    with Scope(nc, "combine") as c:
        got = [c.sb(f"got{b}", [P, TT, HID]) for b in range(2)]
        norms = Norms(c, keep, "norms", y, c.banks(KT))
        arrived = [c.sem(f"arrived{t}") for t in range(TT)]
        own = c.sem("own")
        with nc.Block() as block:
            @block.gpsimd
            def _(pool):
                for t in range(TT):
                    for b, slot in enumerate((keep.slot1, keep.slot2)):
                        pool.indirect_dma_start(out=got[b][:, t, :], out_offset=None, in_=sorted_y,
                                                in_offset=bass.IndirectOffsetOnAxis(ap=slot[:, t:t + 1], axis=0)).then_inc(arrived[t], DMA)

            @block.vector
            def _(dve):
                chain = Chain(dve, own)
                for r in range(norms.ROUNDS):
                    if r < SEGS:
                        for b, weight in enumerate((keep.weight1, keep.weight2)):
                            for t in range(r * TPS, (r + 1) * TPS):
                                dve.wait_ge(arrived[t], 2 * DMA)
                                chain.step(dve.scalar_tensor_tensor(y[:, t, :], got[b][:, t, :], weight[:, t:t + 1], y[:, t, :], ALU.mult, ALU.add))
                            chain.wait()
                    norms.dve_round(dve, chain, r)

            @block.scalar
            def _(act):
                for r in range(norms.ROUNDS):
                    norms.act_root(act, r)
                    norms.act_apply(act, r)

            @block.tensor
            def _(pe):
                for g in range(SEGS):
                    norms.pe_turn(pe, g)


def moe_keep(keep, c):
    keep.weight1, keep.weight2 = c.sb("weight1", [P, TT]), c.sb("weight2", [P, TT])
    keep.slot1, keep.slot2 = c.sb("slot1", [P, TT], I32), c.sb("slot2", [P, TT], I32)
    keep.expert_of = c.sb("expert_of", [1, SLOT_TILES], I32)
    keep.slots_zero = c.sem("slots_zero")


def lay_out_moe(gate_w, w_gate_up, w_down):
    return {"gw": np.ascontiguousarray(gate_w.reshape(NE, KT, P).transpose(2, 1, 0)),
            "wgu": np.ascontiguousarray(w_gate_up.reshape(NE, KT, P, 2 * INNER).transpose(0, 2, 1, 3)),
            "wdn": np.ascontiguousarray(w_down.reshape(NE, 2, IH, HID).transpose(0, 2, 1, 3))}


WH, WD, WG, WIN = 16, 16, 2, 32
REP = WH // WG
STEP = WIN // 2
USED = SEQ // WIN * STEP + STEP
WPAIRS = SEQ // WIN // 2
GD = WG * WD
RR = REP // 4


def window_attention(nc, keep, y, w):
    with Scope(nc, "win") as c:
        sb = c.sb
        wq, wq_hi, wq_lo = sb("wq", [P, KT, HID]), sb("wq_hi", [P, KT, HID], F32R), sb("wq_lo", [P, KT, HID], F32R)
        wkv, wkv_hi, wkv_lo = sb("wkv", [P, KT, P]), sb("wkv_hi", [P, KT, P], F32R), sb("wkv_lo", [P, KT, P], F32R)
        wo, bo = sb("wo", [P, RR, HID]), sb("bo", [P, HID])
        bq, bkv = sb("bq", [P, RR]), sb("bkv", [2 * GD, 1])
        qT, kvT = sb("qT", [P, BATCH, RR, USED]), sb("kvT", [2 * GD, BATCH, USED])
        q2 = sb("q2", [P, REP, WPAIRS * WIN])
        q3 = sb("q3", [P, RR, WPAIRS, 4, WIN])
        k2 = sb("k2", [P, 2, WG, WPAIRS * WIN])
        vdup = sb("vdup", [2 * GD, BATCH, WPAIRS, 2, WG, WIN])
        v2 = sb("v2", [P, BATCH, WPAIRS, 2 * GD])
        less, prob, norm = ([sb(f"{n}{b}", [P, SEG]) for b in range(2)] for n in ("less", "prob", "norm"))
        pT = [sb(f"pT{b}", [P, SEG]) for b in range(2)]
        most, total, inv = ([sb(f"{n}{b}", [P, SEG // WIN]) for b in range(2)] for n in ("most", "total", "inv"))
        o2 = sb("o2", [2 * GD, BATCH, RR, 4, WPAIRS, WIN])
        oT = q2[:].rearrange("p r n -> p (r n)").rearrange("p (b r h m q) -> p b r h m q", b=BATCH, r=RR, h=2, m=WPAIRS)
        oP = q3[:].rearrange("p r m a q -> p (r m a q)").rearrange("p (b r m h q) -> p b r m h q", b=BATCH, r=RR, m=WPAIRS, h=2)
        q3_sb, oP_sb = c.sem("q3"), c.sem("oP")
        bank = c.banks(8)
        (wq_in, wkv_in, kv_zero, k_zero, v_zero, rest_in, bias_in, split_hi, split_lo, q_mm, kv_mm, q_sb, kv_sb) = (
            c.sem(n) for n in ("wq_in", "wkv_in", "kv_zero", "k_zero", "v_zero", "rest_in", "bias_in", "split_hi", "split_lo", "q_mm", "kv_mm", "q_sb", "kv_sb"))
        (v_mm, v_sb, s_mm, most_sb, less_sb, prob_sb, total_sb, inv_sb, norm_sb, t_mm, pT_sb, o_mm, o_sb, y_mm, y_sb) = (
            c.sem(n) for n in ("v_mm", "v_sb", "s_mm", "most", "less", "prob", "total", "inv", "norm", "t_mm", "pT", "o_mm", "o", "y_mm", "y"))
        vdup_sb = c.sem("vdup")
        k_moved = [c.sem(f"k_moved{b}") for b in range(BATCH)]
        q_moved = [c.sem(f"q_moved{n}") for n in range(BATCH * RR)]
        o_moved = [c.sem(f"o_moved{b}") for b in range(BATCH)]
        HALF = USED // 2
        JOBS = [(b, rr, mq) for b in range(BATCH) for rr in range(RR) for mq in range(4)]
        NJ = len(JOBS)
        rows = lambda b, half, n=1: slice(b * 2 * GD + half * GD, b * 2 * GD + (half + n) * GD)
        by_window = lambda a: a.rearrange("p (w k) -> p w k", k=WIN)
        spread_w = lambda a: a.rearrange("p (w o) -> p w o", o=1).broadcast_to([P, SEG // WIN, WIN])

        with nc.Block() as block:
            @block.sync
            def _(sp):
                sp.dma_start(wq[:], w["Wq"].rearrange("(k p) n -> p k n", p=P)).then_inc(wq_in, DMA)
                sp.wait_ge(kv_zero, 1)
                for n, name in enumerate(("Wk", "Wv")):
                    sp.dma_start(wkv[:, :, n * GD:(n + 1) * GD], w[name].rearrange("(k p) n -> p k n", p=P)).then_inc(wkv_in, DMA)
                for n, name in enumerate(("bk", "bv")):
                    sp.dma_start(bkv[n * GD:(n + 1) * GD, :], w[name]).then_inc(bias_in, DMA)
                sp.dma_start(bq[:], w["bq"]).then_inc(bias_in, DMA)
                sp.dma_start(wo[:], w["Wo"].rearrange("(r n) f -> n r f", n=P)).then_inc(rest_in, DMA)
                sp.dma_start(bo[:], w["bo"].rearrange("(o f) -> o f", o=1).broadcast_to([P, HID])).then_inc(rest_in, DMA)
                for b in range(BATCH):
                    for rr in range(RR):
                        sp.wait_ge(q_sb, 2 * (b * RR + rr) + 2)
                        for half in range(2):
                            for r in range(4):
                                sp.dma_start(q2[rows(b, half), rr * 4 + r, :],
                                             qT[r * GD:(r + 1) * GD, b, rr, half * STEP:half * STEP + WPAIRS * WIN]).then_inc(q_moved[b * RR + rr], DMA)
                for b in range(BATCH):
                    for rr in range(RR):
                        sp.wait_ge(o_sb, (b * RR + rr) * 4 + 4)
                        for half in range(2):
                            for r in range(4):
                                sp.dma_start(oT[r * GD:(r + 1) * GD, b, rr, half], o2[half * GD:(half + 1) * GD, b, rr, r]).then_inc(o_moved[b], DMA)

            @block.gpsimd
            def _(pool):
                pool.memset(k2[:], 0.0).then_inc(k_zero, 1)
                pool.memset(v2[:], 0.0).then_inc(v_zero, 1)
                pool.wait_ge(k_zero, 1)
                for b in range(BATCH):
                    pool.wait_ge(kv_sb, 2 * b + 2)
                    for half in range(2):
                        for g in range(WG):
                            at = b * 2 * GD + half * GD + g * WD
                            pool.dma_start(k2[at:at + WD, half, g, :], kvT[g * WD:(g + 1) * WD, b, half * STEP:half * STEP + WPAIRS * WIN]).then_inc(k_moved[b], DMA)
                for i in range(NJ):
                    pool.wait_ge(inv_sb, i + 1)
                    if i >= 2:
                        pool.wait_ge(t_mm, i - 1)
                    pool.tensor_tensor(by_window(norm[i % 2][:]), by_window(prob[i % 2][:]), spread_w(inv[i % 2][:]), ALU.mult).then_inc(norm_sb, 1)

            @block.scalar
            def _(act):
                act.wait_ge(wkv_in, 2 * DMA)
                act.activation(wkv_hi[:], wkv[:], ACT.Copy).then_inc(split_hi, 1)
                act.wait_ge(wq_in, DMA)
                act.activation(wq_hi[:], wq[:], ACT.Copy).then_inc(split_hi, 1)
                act.wait_ge(bias_in, 3 * DMA)
                for b in range(BATCH):
                    for n in range(2):
                        act.wait_ge(kv_mm, 2 * b + n + 1)
                        act.activation(kvT[:, b, n * HALF:(n + 1) * HALF], bank[n][0:2 * GD, 0:HALF], ACT.Identity, bias=bkv[:, 0:1]).then_inc(kv_sb, 1)
                    for rr in range(RR):
                        for n in range(2):
                            i = (b * RR + rr) * 2 + n
                            act.wait_ge(q_mm, i + 1)
                            act.activation(qT[:, b, rr, n * HALF:(n + 1) * HALF], bank[2 + i % 4][:, 0:HALF], ACT.Identity, bias=bq[:, rr:rr + 1]).then_inc(q_sb, 1)
                for i in range(NJ + 3):
                    if 3 <= i:
                        n = i - 3
                        act.wait_ge(t_mm, n + 1)
                        if n >= 2:
                            act.wait_ge(o_mm, n - 1)
                        act.activation(pT[n % 2][:], bank[2 + n % 2][:], ACT.Copy).then_inc(pT_sb, 1)
                    if i < NJ:
                        act.wait_ge(less_sb, i + 1)
                        if i >= 2:
                            act.wait_ge(norm_sb, i - 1)
                        act.activation(prob[i % 2][:], less[i % 2][:], ACT.Exp, scale=float(WD) ** -0.5).then_inc(prob_sb, 1)

            @block.vector
            def _(dve):
                dve.memset(wkv[:], 0.0).then_inc(kv_zero, 1)
                dve.wait_ge(split_hi, 1)
                dve.tensor_tensor(wkv_lo[:], wkv[:], wkv_hi[:].bitcast(F32), ALU.subtract).then_inc(split_lo, 1)
                dve.wait_ge(split_hi, 2)
                dve.tensor_tensor(wq_lo[:], wq[:], wq_hi[:].bitcast(F32), ALU.subtract).then_inc(split_lo, 1)
                for b in range(BATCH):
                    dve.wait_ge(kv_sb, 2 * b + 2)
                    for half in range(2):
                        v = kvT[GD:2 * GD, b, half * STEP:half * STEP + WPAIRS * WIN].rearrange("p (m k) -> p m k", k=WIN)
                        for g in range(WG):
                            last = dve.tensor_copy(vdup[GD:2 * GD, b, :, half, g, :], v)
                    last.then_inc(vdup_sb, 1)
                def arrange(n):
                    b, rr = n // RR, n % RR
                    dve.wait_ge(q_moved[n], 8 * DMA)
                    dve.tensor_copy(q3[rows(b, 0, 2), rr].rearrange("p m r q -> p r m q"),
                                    q2[rows(b, 0, 2), rr * 4:rr * 4 + 4, :].rearrange("p r (m q) -> p r m q", q=WIN)).then_inc(q3_sb, 1)

                dve.wait_ge(v_zero, 1)
                for b in range(BATCH):
                    dve.wait_ge(v_mm, b + 1)
                    for half in range(2):
                        for g in range(WG):
                            at = (half * WG + g) * WIN
                            col = half * GD + g * WD
                            last = dve.tensor_copy(v2[at:at + WIN, b, :, col:col + WD],
                                                   bank[6 + b][at:at + WIN, :].rearrange("p (m n) -> p m n", n=GD)[:, :, g * WD:(g + 1) * WD])
                    last.then_inc(v_sb, 1)
                arrange(0)
                for i in range(NJ + 4):
                    if i % 4 == 2 and i // 4 + 1 < BATCH * RR:
                        arrange(i // 4 + 1)
                    if i < NJ:
                        x = i % 2
                        scores = by_window(bank[x][:])
                        dve.wait_ge(s_mm, i + 1)
                        dve.tensor_reduce(most[x][:], scores, AX.X, ALU.max).then_inc(most_sb, 1)
                        dve.wait_ge(most_sb, i + 1)
                        dve.tensor_tensor(by_window(less[x][:]), scores, spread_w(most[x][:]), ALU.subtract).then_inc(less_sb, 1)
                    if 1 <= i <= NJ:
                        n = i - 1
                        x = n % 2
                        dve.wait_ge(prob_sb, n + 1)
                        dve.tensor_reduce(total[x][:], by_window(prob[x][:]), AX.X, ALU.add).then_inc(total_sb, 1)
                        dve.wait_ge(total_sb, n + 1)
                        if n >= 2:
                            dve.wait_ge(norm_sb, n - 1)
                        dve.reciprocal(inv[x][:], total[x][:]).then_inc(inv_sb, 1)
                    if i >= 4:
                        n = i - 4
                        b, rr, mq = JOBS[n]
                        dve.wait_ge(o_mm, n + 1)
                        dve.tensor_copy(o2[:, b, rr, :, mq * 4:mq * 4 + 4, :].rearrange("p r m q -> p m r q"),
                                        bank[4 + n % 2][0:2 * GD, :].rearrange("p (m r q) -> p m r q", m=4, r=4)).then_inc(o_sb, 1)
                for b in range(BATCH):
                    dve.wait_ge(o_moved[b], 16 * DMA)
                    for rr in range(RR):
                        dve.tensor_copy(oP[:, b, rr].rearrange("p m h q -> p h m q"), oT[:, b, rr]).then_inc(oP_sb, 1)
                dve.wait_ge(rest_in, 2 * DMA)
                for t in range(TT // 2):
                    dve.wait_ge(y_mm, t + 1)
                    dve.tensor_tensor(y[:, 2 * t:2 * t + 2, :], bank[6 + t % 2][:].rearrange("p (a f) -> p a f", a=2),
                                      bo[:].rearrange("p (o f) -> p o f", o=1).broadcast_to([P, 2, HID]), ALU.add).then_inc(y_sb, 1)

            @block.tensor
            def _(pe):
                def project(to, w_hi, w_lo, cols, b, n):
                    toks = slice(b * SEQ + n * HALF, b * SEQ + (n + 1) * HALF)
                    for f in range(KT):
                        last = three_passes(nc, to[:, 0:HALF], (w_hi[:, f, cols], w_lo[:, f, cols]),
                                            (keep.xT_hi[:, f, toks], keep.xT_lo[:, f, toks]), f == 0, f == KT - 1)
                    return last

                pe.wait_ge(split_lo, 1)
                for b in range(BATCH):
                    for n in range(2):
                        if b:
                            pe.wait_ge(kv_sb, n + 1)
                        project(bank[n], wkv_hi, wkv_lo, slice(0, P), b, n).then_inc(kv_mm, 1)
                    pe.wait_ge(split_lo, 2)
                    for rr in range(RR):
                        for n in range(2):
                            i = (b * RR + rr) * 2 + n
                            if i >= 4:
                                pe.wait_ge(q_sb, i - 3)
                            project(bank[2 + i % 4], wq_hi, wq_lo, slice(rr * P, (rr + 1) * P), b, n).then_inc(q_mm, 1)
                for b in range(BATCH):
                    pe.wait_ge(vdup_sb, b + 1)
                    for m in range(WPAIRS):
                        last = pe.transpose(bank[6 + b][:, m * GD:(m + 1) * GD], vdup[GD:2 * GD, b, m, :, :, :].rearrange("p h g k -> p (h g k)"),
                                            keep.ident[GD:2 * GD, GD:2 * GD])
                    last.then_inc(v_mm, 1)
                pe.wait_ge(q_sb, 4 * RR)
                pe.wait_ge(kv_sb, 4)
                for i in range(NJ + 4):
                    if i < NJ:
                        b, rr, mq = JOBS[i]
                        if i % (NJ // BATCH) == 0:
                            pe.wait_ge(k_moved[b], 4 * DMA)
                        pe.wait_ge(q3_sb, b * RR + rr + 1)
                        if i >= 2:
                            pe.wait_ge(less_sb, i - 1)
                        for j in range(4):
                            at = slice((mq * 4 + j) * WIN, (mq * 4 + j + 1) * WIN)
                            last = pe.matmul(bank[i % 2][:, j * P:(j + 1) * P].rearrange("p (a k) -> p a k", k=WIN), q3[rows(b, 0, 2), rr, mq * 4 + j].rearrange("p r q -> p (r q)"),
                                             k2[rows(b, 0, 2), :, :, at].rearrange("p a g k -> p (a g) k"), start=True, stop=True)
                        last.then_inc(s_mm, 1)
                    if 2 <= i < NJ + 2:
                        n = i - 2
                        pe.wait_ge(norm_sb, n + 1)
                        if n >= 2:
                            pe.wait_ge(pT_sb, n - 1)
                        for j in range(4):
                            last = pe.transpose(bank[2 + n % 2][:, j * P:(j + 1) * P], norm[n % 2][:, j * P:(j + 1) * P], keep.ident[:])
                        last.then_inc(t_mm, 1)
                    if 3 <= i < NJ + 3:
                        n = i - 3
                        b, rr, mq = JOBS[n]
                        pe.wait_ge(pT_sb, n + 1)
                        pe.wait_ge(v_sb, 2)
                        if n >= 2:
                            pe.wait_ge(o_sb, n - 1)
                        for j in range(4):
                            last = pe.matmul(bank[4 + n % 2][0:2 * GD, j * P:(j + 1) * P], v2[:, b, mq * 4 + j, :], pT[n % 2][:, j * P:(j + 1) * P],
                                             start=True, stop=True)
                        last.then_inc(o_mm, 1)
                pe.wait_ge(rest_in, 2 * DMA)
                for t in range(TT):
                    b, tile = t // (TT // BATCH), t % (TT // BATCH)
                    if t % (TT // BATCH) == 0:
                        pe.wait_ge(oP_sb, (b + 1) * RR)
                    if t >= 4 and t % 2 == 0:
                        pe.wait_ge(y_sb, t // 2 - 1)
                    for rr in range(RR):
                        o = oP[:, b, rr, 2 * tile:2 * tile + 2].rearrange("p m h q -> p (m h q)")
                        last = pe.matmul(bank[6 + t // 2 % 2][:, t % 2 * HID:(t % 2 + 1) * HID], o, wo[:, rr, :], start=rr == 0, stop=rr == RR - 1)
                    if t % 2:
                        last.then_inc(y_mm, 1)


def lay_out_window(Wq, bq, Wk, bk, Wv, bv, Wo, bo):
    return {"Wq": Wq, "bq": np.ascontiguousarray(bq.reshape(RR, P).T), "Wk": Wk, "bk": bk.reshape(GD, 1),
            "Wv": Wv, "bv": bv.reshape(GD, 1), "Wo": Wo, "bo": bo}


def build_program(nc, a, out, sorted_x, sorted_y):
    keep = Keep()
    with Scope(nc, "keep") as whole:
        allocate(nc, keep, whole)
        moe_keep(keep, whole)
        y = whole.sb("y", [P, TT, HID])
        with Scope(nc, "linear_out") as c:
            keep.acc, keep.squares = c.sb("acc", [P, SEGS, KT, SEG]), c.sb("squares", [P, TOK])
            linear_attention(nc, keep, a["x"], a["slope"], a["wp"], a["wop"], a["nw"], sorted_x)
            close_attention_and_route(nc, keep, y, a["shared_gate_up"], a["shared_down"], a["gw"], sorted_x)
        experts(nc, keep, a["wgu"], a["wdn"], sorted_x, sorted_y)
        combine_and_norm(nc, keep, sorted_y, y)
        window_attention(nc, keep, y, a)
        feed_forward(nc, keep, y, a["ffn_up"], a["ffn_down"], out.rearrange("b (t p) f -> p (b t) f", p=P))


def kernel(L0_attn_hidden_states, L0_attn_slope_rate, L0_attn_w_qkv, L0_attn_w_gate, L0_attn_w_out, L0_attn_norm_w,
           L0_ffn_gate_w, L0_ffn_w_gate_up, L0_ffn_w_down, L0_ffn_shared_gate_up, L0_ffn_shared_down,
           L1_attn_Wq, L1_attn_bq, L1_attn_Wk, L1_attn_bk, L1_attn_Wv, L1_attn_bv, L1_attn_Wo, L1_attn_bo,
           L1_ffn_w_gate_up, L1_ffn_w_down):
    import concourse.bacc as bacc
    from concourse.bass_utils import run_bass_kernel_spmd

    arrays = {
        "x": L0_attn_hidden_states, "slope": L0_attn_slope_rate,
        **lay_out_linear(L0_attn_w_qkv, L0_attn_w_gate, L0_attn_w_out, L0_attn_norm_w),
        **lay_out_moe(L0_ffn_gate_w, L0_ffn_w_gate_up, L0_ffn_w_down),
        "shared_gate_up": L0_ffn_shared_gate_up, "shared_down": L0_ffn_shared_down,
        **lay_out_window(L1_attn_Wq, L1_attn_bq, L1_attn_Wk, L1_attn_bk, L1_attn_Wv, L1_attn_bv, L1_attn_Wo, L1_attn_bo),
        "ffn_up": L1_ffn_w_gate_up.T, "ffn_down": L1_ffn_w_down.T,
    }
    arrays = {f"in_{n}": np.ascontiguousarray(v) for n, v in arrays.items()}
    nc = bacc.Bacc("TRN2", target_bir_lowering=False, num_devices=1)
    a = {n[3:]: nc.dram_tensor(n, v.shape, mybir.dt.from_np(v.dtype), kind="ExternalInput").ap() for n, v in arrays.items()}
    out = nc.dram_tensor("out", (BATCH, SEQ, HID), F32, kind="ExternalOutput").ap()
    sorted_x = nc.dram_tensor("sorted_x", (SLOTS, HID), F32).ap()
    sorted_y = nc.dram_tensor("sorted_y", (SLOTS, HID), F32).ap()
    build_program(nc, a, out, sorted_x, sorted_y)
    return run_bass_kernel_spmd(nc, [arrays], core_ids=[0]).results[0]["out"]
```

```python
import numpy as np
import concourse.bass as bass
from concourse import mybir
from concourse.alu_op_type import AluOpType as ALU
from contextlib import ExitStack

F32 = mybir.dt.float32
F32R = mybir.dt.float32r
BF16 = mybir.dt.bfloat16
I32 = mybir.dt.int32
ACT = mybir.ActivationFunctionType
AX = mybir.AxisListType

P = 128
BATCH, SEQ, HID = 2, 1024, 256
TOK = BATCH * SEQ
TT = TOK // P
KT = HID // P
SEG = 512
SEGS = TOK // SEG
TPS = SEG // P

NH, HD = 16, 128
BLK = 32
RMS_EPS, LN_EPS = 1e-6, 1e-5
PAIRS = NH // 2
DMA = 16


def three_passes(nc, out, lhs, rhs, first=True, last=True, skip=False):
    (lh, ll), (rh, rl) = lhs, rhs
    nc.tensor.matmul(out, lh, rh, start=first, stop=False, skip_group_check=skip)
    nc.tensor.matmul(out, lh, rl, start=False, stop=False, skip_group_check=skip)
    return nc.tensor.matmul(out, ll, rh, start=False, stop=last, skip_group_check=skip)


class Keep:
    pass


class Scope:

    def __init__(self, nc, name):
        self.nc, self.name, self.stack, self.sems = nc, name, ExitStack(), []

    def __enter__(self):
        self.stack.__enter__()
        return self

    def __exit__(self, *a):
        numbers = sorted(s.num for s in self.sems)
        while numbers:
            n = 1
            while n < len(numbers) and numbers[n] == numbers[0] + n:
                n += 1
            self.nc.gpsimd.sem_clear(range(numbers[0], numbers[0] + n))
            numbers = numbers[n:]
        return self.stack.__exit__(*a)

    def sb(self, name, shape, dt=F32):
        return self.stack.enter_context(self.nc.sbuf_tensor(f"{self.name}_{name}", shape, dt))

    def banks(self, n, first=0):
        return [self.stack.enter_context(self.nc.psum_tensor(f"{self.name}_bank{i}", [P, SEG], F32)) for i in range(n)]

    def sem(self, name):
        self.sems.append(self.stack.enter_context(self.nc.semaphore(f"{self.name}_{name}")))
        return self.sems[-1]


class Chain:

    def __init__(self, eng, sem, base=0):
        self.eng, self.sem, self.base, self.n = eng, sem, base, 0

    def step(self, ins):
        self.n += 1
        ins.then_inc(self.sem, 1)

    def link(self, ins):
        self.step(ins)
        self.wait()

    def wait(self):
        self.eng.wait_ge(self.sem, self.base + self.n)


class Decays:

    def __init__(self, c, keep):
        self.keep = keep
        self.slopes, self.neg, self.cols = c.sb("slopes", [P, NH]), c.sb("neg", [P, NH]), c.sb("cols", [P, 1])
        self.ages, self.rows = c.sb("ages", [P, P]), c.sb("rows", [P, P])
        self.mask, self.query = c.sb("decay_mask", [P, NH, P]), c.sb("query_decay", [P, NH, P])
        self.key, self.chunk = c.sb("key_decay", [P, NH]), c.sb("chunk_decay", [P, NH])
        self.slopes_in, self.numbered, self.ready, self.exps, self.masked = (c.sem(n) for n in ("slopes_in", "numbered", "ready", "exps", "masked"))

    def load(self, sp, slope):
        sp.dma_start(self.slopes[:], slope.rearrange("h a b -> (a b) h").broadcast_to([P, NH])).then_inc(self.slopes_in, DMA)

    def pool_start(self, pool):
        ident = self.keep.ident
        numbers = dict(allow_small_or_imprecise_dtypes=True)
        pool.memset(ident[:], 0.0).then_inc(self.numbered, 1)
        pool.iota(self.ages[:], pattern=[[1, P]], base=0, channel_multiplier=-1, **numbers).then_inc(self.numbered, 1)
        pool.iota(self.rows[:], pattern=[[1, P]], base=1, channel_multiplier=0, **numbers).then_inc(self.numbered, 1)
        pool.iota(self.cols[:], pattern=[[0, 1]], base=P - 1, channel_multiplier=-1, **numbers).then_inc(self.numbered, 1)
        pool.wait_ge(self.numbered, 4)
        pool.affine_select(out=ident[:], in_=ident[:], compare_op=ALU.not_equal, fill=1.0,
                           base=0, pattern=[[-1, P]], channel_multiplier=1).then_inc(self.numbered, 1)

    def dve_start(self, dve):
        dve.wait_ge(self.numbered, 4)
        dve.tensor_scalar(self.ages[:], self.ages[:], 0.0, None, ALU.max).then_inc(self.ready, 1)
        dve.wait_ge(self.slopes_in, DMA)
        dve.tensor_scalar(self.neg[:], self.slopes[:], -1.0, None, ALU.mult).then_inc(self.ready, 1)

    def act_start(self, act):
        act.wait_ge(self.ready, 2)
        act.activation(self.key[:], self.neg[:], ACT.Exp, scale=self.cols[:, 0:1])
        act.activation(self.chunk[:], self.neg[:], ACT.Exp, scale=float(P))
        self.act_heads(act, 0, 2)

    def act_heads(self, act, first, end):
        for h in range(first, end):
            s = self.neg[:, h:h + 1]
            act.activation(self.query[:, h, :], self.rows[:], ACT.Exp, scale=s)
            act.activation(self.mask[:, h, :], self.ages[:], ACT.Exp, scale=s).then_inc(self.exps, 1)

    def pool_heads(self, pool, first, end):
        pool.wait_ge(self.exps, end)
        for h in range(first, end):
            pool.affine_select(out=self.mask[:, h, :], in_=self.mask[:, h, :], compare_op=ALU.is_ge,
                               fill=0.0, base=0, pattern=[[1, P]], channel_multiplier=-1).then_inc(self.masked, 1)


class Norms:
    ROUNDS = SEGS + 2

    def __init__(self, c, keep, tag, y, banks, z_all=None, pool_from=SEGS + 1):
        self.pool_from, self.added, self.z_y_ready = pool_from, c.sem(f"{tag}_added"), c.sem(f"{tag}_z_y")
        self.keep, self.y, self.banks, self.z_all = keep, y, banks, z_all
        sb = lambda n, shape, dt=F32: c.sb(f"{tag}_{n}", shape, dt)
        self.stats, self.mean_var = sb("stats", [P, 2 * TPS, 6]), sb("mean_var", [P, 2 * TPS, 2])
        self.spread, self.root, self.scale, self.shift = (sb(n, [P, 2 * TPS]) for n in ("spread", "root", "scale", "shift"))
        self.z_y = sb("z_y", [P, TPS, HID]) if y is not None else None
        self.z_one = sb("z_x", [P, TPS, HID]) if z_all is None else None
        self.spread_ready, self.root_ready, self.affine_ready, self.z_x_ready, self.turned, self.high, self.low = (
            c.sem(f"{tag}_{n}") for n in ("spread", "root", "affine", "z_x", "turned", "high", "low"))
        self.first = 0 if y is not None else 1

    def z_x(self, g):
        return self.z_one if self.z_all is None else self.z_all[:, g * TPS:(g + 1) * TPS, :]

    def tiles(self, a, g):
        return a[:, g * TPS:(g + 1) * TPS, :]

    def span(self, r):
        return slice(0 if r < SEGS and self.y is not None else TPS, 2 * TPS if r >= 1 else TPS)

    def dve_round(self, dve, chain, r, y_wait=None, split=True):
        n = r - self.first
        if r <= SEGS:
            if self.y is not None and 1 <= r < self.pool_from:
                xs = self.tiles(self.keep.x, r - 1)
                chain.link(dve.tensor_tensor(xs, xs, self.z_y[:], ALU.add))
            columns = []
            if self.y is not None and r < SEGS:
                columns += [(j, self.y[:, r * TPS + j, :]) for j in range(TPS)]
            if r >= 1:
                columns += [(TPS + j, self.keep.x[:, (r - 1) * TPS + j, :]) for j in range(TPS)]
            for i, (col, tile) in enumerate(columns):
                if y_wait is not None and i in (0, 2) and r < SEGS + (self.y is None):
                    y_wait(i // 2)
                if self.pool_from <= r and col == TPS:
                    dve.wait_ge(self.added, r - self.pool_from + 1)
                chain.step(dve.bn_stats(self.stats[:, col, :], tile))
            chain.wait()
            for col, _ in columns:
                chain.step(dve.bn_aggr(self.mean_var[:, col, :], self.stats[:, col, :]))
            chain.wait()
            at = self.span(r)
            dve.tensor_scalar(self.spread[:, at], self.mean_var[:, at, 1], LN_EPS, None, ALU.add).then_inc(self.spread_ready, 1)
        if r >= 2 and split:
            self.dve_low(dve, r - 2)
        if r <= SEGS:
            dve.wait_ge(self.root_ready, n + 1)
            chain.link(dve.reciprocal(self.scale[:, at], self.root[:, at]))
            dve.scalar_tensor_tensor(self.shift[:, at], self.mean_var[:, at, 0], -1.0, self.scale[:, at], ALU.mult, ALU.mult).then_inc(self.affine_ready, 1)
            if self.y is not None and r < SEGS:
                for j in range(TPS):
                    z = dve.tensor_scalar(self.z_y[:, j, :], self.y[:, r * TPS + j, :], self.mean_var[:, j, 0:1], self.scale[:, j:j + 1],
                                          ALU.subtract, ALU.mult)
                    if r + 1 < self.pool_from:
                        chain.step(z)
                    else:
                        z.then_inc(self.z_y_ready, 1)
                chain.wait()

    def dve_low(self, dve, g):
        for k in range(KT):
            dve.wait_ge(self.high, KT * g + k + 1)
            at = slice(g * SEG, (g + 1) * SEG)
            dve.tensor_tensor(self.keep.xT_lo[:, k, at], self.banks[k][:], self.keep.xT_hi[:, k, at].bitcast(F32),
                              ALU.subtract).then_inc(self.low, 1)

    def pool_add(self, pool, r):
        pool.wait_ge(self.z_y_ready, (r - self.pool_from + 1) * TPS)
        xs = self.tiles(self.keep.x, r - 1)
        pool.tensor_tensor(xs, xs, self.z_y[:], ALU.add).then_inc(self.added, 1)

    def act_root(self, act, r, split=True):
        if r <= SEGS:
            act.wait_ge(self.spread_ready, r - self.first + 1)
            at = self.span(r)
            act.activation(self.root[:, at], self.spread[:, at], ACT.Sqrt).then_inc(self.root_ready, 1)
        if r >= 2 and split:
            self.act_high(act, r - 2)

    def act_high(self, act, g):
        for k in range(KT):
            act.wait_ge(self.turned, KT * g + k + 1)
            act.activation(self.keep.xT_hi[:, k, g * SEG:(g + 1) * SEG], self.banks[k][:], ACT.Copy).then_inc(self.high, 1)

    def act_apply(self, act, r):
        if not 1 <= r <= SEGS:
            return
        act.wait_ge(self.affine_ready, r - self.first + 1)
        for j in range(TPS):
            last = act.activation(self.z_x(r - 1)[:, j, :], self.keep.x[:, (r - 1) * TPS + j, :], ACT.Identity,
                                  scale=self.scale[:, TPS + j:TPS + j + 1], bias=self.shift[:, TPS + j:TPS + j + 1])
        last.then_inc(self.z_x_ready, 1)

    def pe_turn(self, pe, g):
        pe.wait_ge(self.z_x_ready, g + 1)
        for k in range(KT):
            if g:
                pe.wait_ge(self.low, KT * (g - 1) + k + 1)
            for j in range(TPS):
                last = pe.transpose(self.banks[k][:, j * P:(j + 1) * P], self.z_x(g)[:, j, k * P:(k + 1) * P], self.keep.ident[:])
            last.then_inc(self.turned, 1)


class AttentionOutput:

    def __init__(self, c, keep, y):
        self.keep, self.y = keep, y
        self.ones = c.sb("ones", [P, 2])
        self.spread, self.root, self.factor = (c.sb(n, [P, TT]) for n in ("spread", "root", "factor"))
        self.ones_ready, self.sums, self.spread_ready, self.root_ready, self.factor_ready, self.back, self.y_ready = (
            c.sem(n) for n in ("ones", "sums", "spread", "root", "factor", "back", "y_ready"))

    def columns(self, g):
        return slice(g * TPS, (g + 1) * TPS)

    def pe_sums(self, pe, g, banks):
        pe.wait_ge(self.ones_ready, 1)
        for j in range(TPS):
            toks = slice((g * TPS + j) * P, (g * TPS + j + 1) * P)
            last = pe.matmul(banks[0][:, 2 * j:2 * j + 2], self.keep.squares[:, toks], self.ones[:], start=True, stop=True)
        last.then_inc(self.sums, 1)

    def dve_factor(self, dve, g, banks):
        at = self.columns(g)
        dve.wait_ge(self.sums, g + 1)
        dve.tensor_scalar(self.spread[:, at], banks[0][:, 0:2 * TPS].rearrange("p (t a) -> p t a", a=2)[:, :, 0],
                          1.0 / (NH * HD), RMS_EPS, ALU.mult, ALU.add).then_inc(self.spread_ready, 1)
        dve.wait_ge(self.root_ready, g + 1)
        dve.reciprocal(self.factor[:, at], self.root[:, at]).then_inc(self.factor_ready, 1)

    def act_root(self, act, g):
        at = self.columns(g)
        act.wait_ge(self.spread_ready, g + 1)
        act.activation(self.root[:, at], self.spread[:, at], ACT.Sqrt).then_inc(self.root_ready, 1)

    def pe_turn(self, pe, g, banks):
        pe.wait_ge(self.spread_ready, g + 1)
        for half in range(2):
            for i in range(2):
                for f in range(KT):
                    at = slice((2 * half + i) * P, (2 * half + i + 1) * P)
                    last = pe.transpose(banks[half][:, i * HID + f * P:i * HID + (f + 1) * P], self.keep.acc[:, g, f, at], self.keep.ident[:])
            last.then_inc(self.back, 1)

    def act_take(self, act, g, banks):
        act.wait_ge(self.factor_ready, g + 1)
        for half in range(2):
            act.wait_ge(self.back, 2 * g + half + 1)
            for i in range(2):
                t = g * TPS + 2 * half + i
                last = act.activation(self.y[:, t, :], banks[half][:, i * HID:(i + 1) * HID], ACT.Copy, scale=self.factor[:, t:t + 1])
            last.then_inc(self.y_ready, 1)


def linear_attention(nc, keep, x, slope, w_pairs, wout_pairs, norm_w, output, after):
    with Scope(nc, "lin") as c:
        raw = c.sb("raw", [P, KT, 1024])
        w_hi, w_lo = c.sb("w_hi", [P, KT, 1024], F32R), c.sb("w_lo", [P, KT, 1024], F32R)
        raw_out = c.sb("raw_out", [P, 2, HID])
        wo_hi, wo_lo = c.sb("wo_hi", [P, 2, HID], F32R), c.sb("wo_lo", [P, 2, HID], F32R)
        norm_in = c.sb("norm_in", [P, NH])
        two = lambda n, dt=F32: c.sb(n, [P, 2, SEG], dt)
        q, k, kd, o, th, sq, qd, st, g = (two(n) for n in ("q", "k", "kd", "o", "th", "sq", "qd", "st", "g"))
        g_hi, g_lo = two("g_hi", F32R), two("g_lo", F32R)
        v = c.sb("v", [P, TPS, 2, HD])
        state = c.sb("state", [P, 2, TPS, HD])
        mask, q_dec = c.sb("mask", [P, 2, P]), c.sb("q_dec", [P, 2, P])
        k_dec, c_dec, half_norm = c.sb("k_dec", [P, 2]), c.sb("c_dec", [P, 2]), c.sb("half_norm", [P, 2])
        bank = c.banks(8)
        sem = c.sem
        raw_in, raw_out_in, norm_sem = sem("raw_in"), sem("raw_out_in"), sem("norm_in")
        w_hi_done, w_lo_done, wo_done, wo_hi_done = sem("w_hi"), sem("w_lo"), sem("wo"), sem("wo_hi")
        q_mm, k_mm, v_mm, g_mm, t_mm, s_mm, d_mm, o_mm, w_mm = (sem(n + "_mm") for n in "qkvgtsdow")
        q_sb, k_sb, v_sb, th_sb, kd_sb, o_sb, sq_sb = (sem(n + "_sb") for n in ("q", "k", "v", "th", "kd", "o", "sq"))
        qd_sb, st_sb, state_sb, g_sb, acc_sb, squares_sb = (sem(n + "_sb") for n in ("qd", "st", "state", "g", "acc", "squares"))
        heads_sb, own, norms_own, zeroed = sem("heads"), sem("own"), sem("norms_own"), sem("zeroed")
        decays = Decays(c, keep)
        norms = Norms(c, keep, "norms", None, bank[2:4])
        x_in = [sem(f"x_in{g}") for g in range(SEGS)]
        C4 = lambda ap: ap.rearrange("p (c i) -> p c i", c=TPS)

        def states(t, seg, a, n):
            hp28 = (t - seg) // 4 * 28 if isinstance(t, int) else None
            base = hp28 if hp28 is not None else (t - seg) * 7
            return base + (0, 8, 14, 22)[seg] + a * (4 - seg % 2) + n

        def n_states(seg):
            return 4 - seg % 2

        COL = {("q", 0): 0, ("k", 0): 1, ("q", 1): 2, ("k", 1): 3, ("g", 0): 4, ("g", 1): 5}

        def pe_pass(pe, hp, first, last_pass=False):
            def project(job, a, to, seg):
                cols = slice(COL[job, a] * P, (COL[job, a] + 1) * P)
                toks = slice(seg * SEG, (seg + 1) * SEG)
                for f in range(KT):
                    last = three_passes(nc, to[:], (w_hi[:, f, cols], w_lo[:, f, cols]),
                                        (keep.xT_hi[:, f, toks], keep.xT_lo[:, f, toks]), f == 0, f == KT - 1)
                return last

            pe.wait_ge(w_hi_done, 2 * hp + 2)
            pe.wait_ge(w_lo_done, 2 * hp + 2)
            for seg in range(SEGS):
                t = 4 * hp + seg
                start = first and seg == 0
                if first:
                    pe.wait_ge(norms.low, KT * (seg + 1))
                if not start:
                    pe.wait_ge(o_sb, 2 * t - 1)
                project("q", 0, bank[0], seg).then_inc(q_mm, 1)
                if not start:
                    pe.wait_ge(o_sb, 2 * t)
                project("k", 0, bank[1], seg).then_inc(k_mm, 1)
                if last_pass and seg >= 2:
                    pe.wait_ge(output.y_ready, 2 * seg - 2)
                if not start:
                    pe.wait_ge(st_sb, 2 * t - 1)
                project("q", 1, bank[2], seg).then_inc(q_mm, 1)
                if not start:
                    pe.wait_ge(st_sb, 2 * t)
                project("k", 1, bank[3], seg).then_inc(k_mm, 1)
                for b in range(2):
                    if not (first and seg <= 1):
                        pe.wait_ge(acc_sb, 2 * t - 3 + b)
                    for j in range(2):
                        toks = slice(seg * SEG + (2 * b + j) * P, seg * SEG + (2 * b + j + 1) * P)
                        for f in range(KT):
                            last = three_passes(nc, bank[4 + b][:, j * HID:(j + 1) * HID],
                                                (keep.xT_hi[:, f, toks], keep.xT_lo[:, f, toks]),
                                                (w_hi[:, f, 768:1024], w_lo[:, f, 768:1024]), f == 0, f == KT - 1)
                    last.then_inc(v_mm, 1)
                for a in range(2):
                    if not start:
                        s1 = (seg - 1) % SEGS
                        pe.wait_ge(state_sb, states(t - 1, s1, a, n_states(s1)))
                    project("g", a, bank[6 + a], seg).then_inc(g_mm, 1)
                for a in range(2):
                    pe.wait_ge(k_sb, 2 * t + 1 + a)
                    pe.wait_ge(q_sb, 2 * t + 1)
                    for j in range(TPS):
                        last = pe.transpose(bank[a][:, j * P:(j + 1) * P], k[:, a, j * P:(j + 1) * P], keep.ident[:])
                    last.then_inc(t_mm, 1)
                for a in range(2):
                    pe.wait_ge(q_sb, 2 * t + 2)
                    pe.wait_ge(k_sb, 2 * t + 2)
                    for j in range(TPS):
                        cols = slice(j * P, (j + 1) * P)
                        last = pe.matmul(bank[2 + a][:, cols], k[:, a, cols], q[:, a, cols], start=True, stop=True)
                    last.then_inc(s_mm, 1)
                if not start:
                    if seg == 1:
                        pe.wait_ge(wo_done, 2 * hp + 2)
                    out_projection(pe, t - 1, 2 * t + 2)
                for a in range(2):
                    pe.wait_ge(th_sb, 2 * t + 1 + a)
                    pe.wait_ge(kd_sb, 2 * t + 1 + a)
                    pe.wait_ge(v_sb, 2 * t + 2)
                    for j in range(TPS):
                        last = pe.matmul(bank[6 + a][:, j * P:(j + 1) * P], kd[:, a, j * P:(j + 1) * P], v[:, j, a, :], start=True, stop=True)
                    last.then_inc(d_mm, 1)
                if first and seg + 1 < SEGS:
                    pe.wait_ge(st_sb, 2 * t + 2)
                    norms.pe_turn(pe, seg + 1)
                if last_pass and seg:
                    pe.wait_ge(st_sb, 2 * t + 2)
                    pe.wait_ge(squares_sb, 2 * t)
                    output.pe_sums(pe, seg - 1, bank[2:4])
                for a in range(2):
                    pe.wait_ge(st_sb, 2 * t + 1 + a)
                    pe.wait_ge(qd_sb, 2 * t + 1 + a)
                    pe.wait_ge(kd_sb, 2 * t + 1 + a)
                    for j in range(TPS):
                        cols = slice(j * P, (j + 1) * P)
                        fresh = seg % 2 == 0 and j == 0
                        last = pe.matmul(bank[a][:, cols], v[:, j, a, :], st[:, a, cols], start=True, stop=fresh)
                        if not fresh:
                            if j:
                                pe.wait_ge(state_sb, states(t, seg, a, j))
                            last = pe.matmul(bank[a][:, cols], state[:, a, j, :], qd[:, a, cols], start=False, stop=True)
                    last.then_inc(o_mm, 1)
                if last_pass and seg:
                    pe.wait_ge(acc_sb, 2 * t)
                    output.pe_turn(pe, seg - 1, bank[2:4])

        def out_projection(pe, t, v_count):
            pe.wait_ge(v_sb, v_count)
            pe.wait_ge(g_sb, 2 * t + 2)
            for f in range(KT):
                for a in range(2):
                    last = three_passes(nc, bank[4 + f][:], (wo_hi[:, a, f * P:(f + 1) * P], wo_lo[:, a, f * P:(f + 1) * P]),
                                        (g_hi[:, a, :], g_lo[:, a, :]), a == 0, a == 1)
                last.then_inc(w_mm, 1)

        def act_split(act, hp):
            act.wait_ge(raw_in, DMA * (hp + 1))
            for f in range(KT):
                act.activation(w_hi[:, f, :], raw[:, f, :], ACT.Copy).then_inc(w_hi_done, 1)

        def act_pass(act, hp, first, last):
            for seg in range(SEGS):
                t = 4 * hp + seg
                start = first and seg == 0
                for a in range(2):
                    act.wait_ge(q_mm, 2 * t + 1 + a)
                    if not start:
                        act.wait_ge(qd_sb, 2 * t - 1 + a)
                    act.activation(q[:, a, :], bank[2 * a][:], ACT.Silu).then_inc(q_sb, 1)
                    act.wait_ge(k_mm, 2 * t + 1 + a)
                    act.activation(k[:, a, :], bank[2 * a + 1][:], ACT.Silu).then_inc(k_sb, 1)
                for b in range(2):
                    act.wait_ge(v_mm, 2 * t + 1 + b)
                    act.activation(v[:, 2 * b:2 * b + 2, :, :].rearrange("p c a e -> p (c a e)"), bank[4 + b][:], ACT.Silu).then_inc(v_sb, 1)
                for a in range(2):
                    act.wait_ge(g_mm, 2 * t + 1 + a)
                    if not start:
                        act.wait_ge(g_sb, 2 * t - 1 + a)
                    act.activation(th[:, a, :], bank[6 + a][:], ACT.Tanh, scale=0.5).then_inc(th_sb, 1)
                if seg == SEGS - 1 and not last:
                    act_split(act, hp + 1)
                if seg == 0:
                    act.wait_ge(heads_sb, hp + 1)
                for a in range(2):
                    act.wait_ge(t_mm, 2 * t + 1 + a)
                    act.activation(kd[:, a, :], bank[a][:], ACT.Copy, scale=k_dec[:, a:a + 1]).then_inc(kd_sb, 1)
                if first and seg + 1 < SEGS:
                    norms.act_high(act, seg + 1)
                if last and seg:
                    output.act_root(act, seg - 1)
                for a in range(2):
                    act.wait_ge(o_mm, 2 * t + 1 + a)
                    act.activation(o[:, a, :], bank[a][:], ACT.Copy).then_inc(o_sb, 1)
                    act.wait_ge(o_sb, 2 * t + 1 + a)
                    if not start:
                        act.wait_ge(squares_sb, 2 * t - 1 + a)
                    act.activation(sq[:, a, :], o[:, a, :], ACT.Square).then_inc(sq_sb, 1)
                if first and seg + 3 <= SEGS:
                    norms.act_root(act, seg + 3, split=False)
                    norms.act_apply(act, seg + 3)
                if last and seg:
                    output.act_take(act, seg - 1, bank[2:4])
                    after.act_root(act, seg - 1, split=False)
                    after.act_apply(act, seg - 1)
                if first and seg == 2:
                    decays.act_heads(act, 2, NH)

        def gate(dve, chain, t):
            for a in range(2):
                dve.wait_ge(o_sb, 2 * t + 1 + a)
                dve.wait_ge(th_sb, 2 * t + 1 + a)
                chain.link(dve.tensor_scalar(g[:, a, :], th[:, a, :], 1.0, half_norm[:, a:a + 1], ALU.add, ALU.mult))
                chain.link(dve.tensor_tensor(g[:, a, :], g[:, a, :], o[:, a, :], ALU.mult))
                chain.link(dve.tensor_copy(g_hi[:, a, :], g[:, a, :]))
                dve.tensor_tensor(g_lo[:, a, :], g[:, a, :], g_hi[:, a, :].bitcast(F32), ALU.subtract).then_inc(g_sb, 1)

        def dve_split(dve, hp):
            for f in range(KT):
                dve.wait_ge(w_hi_done, 2 * hp + 1 + f)
                dve.tensor_tensor(w_lo[:, f, :], raw[:, f, :], w_hi[:, f, :].bitcast(F32), ALU.subtract).then_inc(w_lo_done, 1)

        def accumulate(dve, t, seg):
            for f in range(KT):
                dve.wait_ge(w_mm, 2 * t + 1 + f)
                part = keep.acc[:, seg, f, :]
                dve.tensor_tensor(part, part, bank[4 + f][:], ALU.add).then_inc(acc_sb, 1)

        def dve_pass(dve, hp, first, last, chain, norms_chain=None):
            for seg in range(SEGS):
                t = 4 * hp + seg
                start = first and seg == 0
                if not start:
                    gate(dve, chain, t - 1)
                if seg == 0:
                    two = bass.ds(2 * hp, 2)
                    dve.wait_ge(decays.masked, 2 if first else NH)
                    chain.step(dve.tensor_copy(mask[:], decays.mask[:, two, :]))
                    chain.step(dve.tensor_copy(q_dec[:], decays.query[:, two, :]))
                    chain.step(dve.tensor_copy(k_dec[:], decays.key[:, two]))
                    chain.step(dve.tensor_copy(c_dec[:], decays.chunk[:, two]))
                    dve.tensor_scalar(half_norm[:], norm_in[:, two], 0.5, None, ALU.mult).then_inc(heads_sb, 1)
                    dve.wait_ge(heads_sb, hp + 1)
                for a in range(2):
                    dve.wait_ge(q_sb, 2 * t + 1 + a)
                    dve.tensor_tensor(C4(qd[:, a, :]), C4(q[:, a, :]), q_dec[:, a:a + 1, :].broadcast_to([P, TPS, P]),
                                      ALU.mult).then_inc(qd_sb, 1)
                for a in range(2):
                    dve.wait_ge(s_mm, 2 * t + 1 + a)
                    dve.tensor_tensor(C4(st[:, a, :]), C4(bank[2 + a][:]), mask[:, a:a + 1, :].broadcast_to([P, TPS, P]),
                                      ALU.mult).then_inc(st_sb, 1)
                if seg == SEGS - 1 and not last:
                    dve_split(dve, hp + 1)
                if not start:
                    accumulate(dve, t - 1, (seg - 1) % SEGS)
                if seg == 0:
                    dve.wait_ge(raw_out_in, DMA * (hp + 1))
                    dve.tensor_copy(wo_hi[:], raw_out[:]).then_inc(wo_done, 1)
                    dve.wait_ge(wo_done, 2 * hp + 1)
                    dve.tensor_tensor(wo_lo[:], raw_out[:], wo_hi[:].bitcast(F32), ALU.subtract).then_inc(wo_done, 1)
                for a in range(2):
                    dve.wait_ge(d_mm, 2 * t + 1 + a)
                    for j in range(n_states(seg)):
                        grown = bank[6 + a][:, j * P:(j + 1) * P]
                        new = state[:, a, (j + 1) % TPS, :]
                        if seg % 2 == 0 and j == 0:
                            dve.tensor_copy(new, grown).then_inc(state_sb, 1)
                        else:
                            dve.wait_ge(state_sb, states(t, seg, a, j) if j else states(t - 1, seg - 1, a, n_states(seg - 1)))
                            dve.scalar_tensor_tensor(new, state[:, a, j, :], c_dec[:, a:a + 1], grown, ALU.mult, ALU.add).then_inc(state_sb, 1)
                if last and seg:
                    output.dve_factor(dve, seg - 1, bank[2:4])
                    if seg == SEGS - 1:
                        gate(dve, chain, t)
                    after.dve_round(dve, norms_chain, seg - 1, lambda half: dve.wait_ge(output.y_ready, 2 * seg - 1 + half), split=False)
                if first and seg + 1 < SEGS:
                    norms.dve_low(dve, seg + 1)
                if first and seg + 3 <= SEGS:
                    dve_norms(dve, norms_chain, seg + 3)

        def dve_norms(dve, chain, r):
            dve.wait_ge(x_in[r - 1], DMA)
            norms.dve_round(dve, chain, r, split=False)

        def pool_pass(pool, hp, first):
            for seg in range(SEGS):
                part = keep.squares[:, seg * SEG:(seg + 1) * SEG]
                for a in range(2):
                    n = 2 * (4 * hp + seg) + a
                    pool.wait_ge(sq_sb, n + 1)
                    if a:
                        pool.wait_ge(squares_sb, n)
                    pool.tensor_tensor(part, part, sq[:, a, :], ALU.add).then_inc(squares_sb, 1)
                if first and seg == 2:
                    decays.pool_heads(pool, 2, NH)

        STEPS_FIRST, STEPS = 1 + 4 + 6 * (SEGS - 1), 4 + 6 * SEGS
        with nc.Block() as block:
            @block.sync
            def _(sp):
                decays.load(sp, slope)
                tiles = x.rearrange("b (t p) f -> p (b t) f", p=P)
                for g in range(SEGS):
                    at = slice(g * TPS, (g + 1) * TPS)
                    sp.dma_start(keep.x[:, at, :], tiles[:, at, :]).then_inc(x_in[g], DMA)
                    if g == 0:
                        sp.dma_start(raw[:], w_pairs[0]).then_inc(raw_in, DMA)
                        sp.dma_start(norm_in[:], norm_w).then_inc(norm_sem, DMA)
                sp.dma_start(raw_out[:], wout_pairs[0]).then_inc(raw_out_in, DMA)
                with sp.Fori(0, PAIRS - 1) as hp:
                    sp.wait_ge(w_lo_done, 2 * hp + 2)
                    sp.dma_start(raw[:], w_pairs[bass.ds(hp + 1, 1)].rearrange("a p k n -> (a p) k n")).then_inc(raw_in, DMA)
                    sp.wait_ge(wo_done, 2 * hp + 2)
                    sp.dma_start(raw_out[:], wout_pairs[bass.ds(hp + 1, 1)].rearrange("a p k n -> (a p) k n")).then_inc(raw_out_in, DMA)

            @block.gpsimd
            def _(pool):
                decays.pool_start(pool)
                pool.memset(keep.squares[:], 0.0).then_inc(zeroed, 1)
                pool.wait_ge(zeroed, 1)
                decays.pool_heads(pool, 0, 2)
                pool_pass(pool, 0, True)
                with pool.Fori(1, PAIRS) as hp:
                    pool_pass(pool, hp, False)

            @block.vector
            def _(dve):
                chain = Chain(dve, own)
                norms_chain = Chain(dve, norms_own)
                decays.dve_start(dve)
                dve_norms(dve, norms_chain, 1)
                dve_split(dve, 0)
                norms.dve_low(dve, 0)
                dve_norms(dve, norms_chain, 2)
                dve.memset(output.ones[:], 1.0).then_inc(output.ones_ready, 1)
                chain.link(dve.memset(keep.acc[:], 0.0))
                dve.wait_ge(norm_sem, DMA)
                dve_pass(dve, 0, True, False, chain, norms_chain)
                assert chain.n == STEPS_FIRST
                with dve.Fori(1, PAIRS - 1) as hp:
                    chain = Chain(dve, own, (hp - 1) * STEPS + STEPS_FIRST)
                    dve_pass(dve, hp, False, False, chain)
                    assert chain.n == STEPS
                chain = Chain(dve, own, (PAIRS - 2) * STEPS + STEPS_FIRST)
                dve_pass(dve, PAIRS - 1, False, True, chain, norms_chain)
                accumulate(dve, 4 * PAIRS - 1, SEGS - 1)

            @block.scalar
            def _(act):
                norms.act_root(act, 1)
                norms.act_apply(act, 1)
                act_split(act, 0)
                norms.act_high(act, 0)
                norms.act_root(act, 2, split=False)
                norms.act_apply(act, 2)
                decays.act_start(act)
                act_pass(act, 0, True, False)
                with act.Fori(1, PAIRS - 1) as hp:
                    act_pass(act, hp, False, False)
                act_pass(act, PAIRS - 1, False, True)

            @block.tensor
            def _(pe):
                pe.wait_ge(decays.numbered, 5)
                norms.pe_turn(pe, 0)
                pe_pass(pe, 0, True)
                with pe.Fori(1, PAIRS - 1) as hp:
                    pe_pass(pe, hp, False)
                pe_pass(pe, PAIRS - 1, False, True)
                out_projection(pe, 4 * PAIRS - 1, 8 * PAIRS)


def allocate(nc, keep, c):
    keep.x = c.sb("x", [P, TT, HID])
    keep.xT_hi = c.sb("xT_hi", [P, KT, TOK], F32R)
    keep.xT_lo = c.sb("xT_lo", [P, KT, TOK], F32R)
    keep.ident = c.sb("ident", [P, P])


def lay_out_linear(w_qkv, w_gate, w_out, norm_w):
    qkv = w_qkv.reshape(PAIRS, 2, 3, HD, KT, P)
    gate = w_gate.reshape(PAIRS, 2, HD, KT, P)
    blocks = [qkv[:, 0, 0], qkv[:, 0, 1], qkv[:, 1, 0], qkv[:, 1, 1], gate[:, 0], gate[:, 1], qkv[:, 0, 2], qkv[:, 1, 2]]
    w = np.stack(blocks, 1)
    w = w.transpose(0, 4, 3, 1, 2).reshape(PAIRS, P, KT, 8 * HD)
    wo = w_out.reshape(HID, PAIRS, 2, HD).transpose(1, 3, 2, 0)
    return {"wp": np.ascontiguousarray(w), "wop": np.ascontiguousarray(wo), "nw": np.ascontiguousarray(norm_w.reshape(NH, HD).T)}


RSQRT_SEED = 0x5f3759df


class Affine:

    def __init__(self, c, tag, used):
        sb = lambda n, shape, dt=F32: c.sb(f"{tag}_{n}", shape, dt)
        self.stats, self.mean_var = sb("stats", [P, TPS, 6]), sb("mean_var", [P, TPS, 2])
        self.var, self.scale, self.shift, self.t = (sb(n, [P, TPS]) for n in ("var", "scale", "shift", "t"))
        self.stats_ready, self.ready, self.spread_ready, self.root_ready = (c.sem(f"{tag}_{n}") for n in ("stats", "affine", "spread", "root"))
        self.used = used

    def statistics(self, dve, chain, tiles, g, half):
        js = (2 * half, 2 * half + 1)
        for j in js:
            chain.step(dve.bn_stats(self.stats[:, j, :], tiles[:, j, :]))
        chain.wait()
        for j in js:
            if g and j == 0:
                dve.wait_ge(self.ready, g)
            dve.bn_aggr(self.mean_var[:, j, :], self.stats[:, j, :]).then_inc(self.stats_ready, 1)

    def dve_quick_scale(self, dve, chain, g):
        dve.wait_ge(self.stats_ready, TPS * (g + 1))
        dve.tensor_scalar(self.var[:], self.mean_var[:, :, 1], LN_EPS, None, ALU.add).then_inc(self.spread_ready, 1)
        dve.wait_ge(self.root_ready, 1)
        chain.link(dve.reciprocal(self.scale[:], self.t[:]))
        dve.scalar_tensor_tensor(self.shift[:], self.mean_var[:, :, 0], -1.0, self.scale[:], ALU.mult, ALU.mult).then_inc(self.ready, 1)

    def act_root(self, act):
        act.wait_ge(self.spread_ready, 1)
        act.activation(self.t[:], self.var[:], ACT.Sqrt).then_inc(self.root_ready, 1)

    def scale_and_shift(self, eng, chain, g):
        eng.wait_ge(self.stats_ready, TPS * (g + 1))
        chain.link(eng.tensor_scalar(self.var[:], self.mean_var[:, :, 1], LN_EPS, None, ALU.add))
        if g:
            eng.wait_ge(self.used, g)
        inverse_root(eng, chain, self.var, self.scale, self.t)
        chain.link(eng.tensor_scalar(self.t[:], self.mean_var[:, :, 0], -1.0, None, ALU.mult))
        eng.tensor_tensor(self.shift[:], self.t[:], self.scale[:], ALU.mult).then_inc(self.ready, 1)


def inverse_root(eng, chain, v, r, t):
    chain.link(eng.tensor_scalar(r[:].bitcast(I32), v[:].bitcast(I32), -0.5, float(RSQRT_SEED), ALU.mult, ALU.add))
    for _ in range(3):
        chain.link(eng.tensor_tensor(t[:], r[:], r[:], ALU.mult))
        chain.link(eng.tensor_tensor(t[:], t[:], v[:], ALU.mult))
        chain.link(eng.tensor_scalar(t[:], t[:], -0.5, 1.5, ALU.mult, ALU.add))
        chain.link(eng.tensor_tensor(r[:], t[:], r[:], ALU.mult))


class AddNorm:

    def __init__(self, c, keep, tag, y, z=None):
        self.x, self.y = keep.x, y
        self.z = c.sb(f"{tag}_z", [P, TPS, HID])[:] if z is None else z
        self.z_ready, self.added = c.sem(f"{tag}_z"), c.sem(f"{tag}_added")
        self.affine = Affine(c, tag, self.z_ready)

    def statistics(self, dve, chain, g, half):
        self.affine.statistics(dve, chain, self.y[:, g * TPS:(g + 1) * TPS, :], g, half)

    def dve_apply(self, dve, chain, g):
        if g:
            dve.wait_ge(self.added, g)
        for j in range(TPS):
            last = dve.tensor_scalar(self.z[:, j, :], self.y[:, g * TPS + j, :], self.affine.mean_var[:, j, 0:1], self.affine.scale[:, j:j + 1],
                                     ALU.subtract, ALU.mult)
            chain.step(last) if j + 1 < TPS else last.then_inc(self.z_ready, 1)
        chain.wait()

    def act_apply(self, act, g):
        act.wait_ge(self.affine.ready, g + 1)
        if g:
            act.wait_ge(self.added, g)
        apply(act, self.z, self.y[:, g * TPS:(g + 1) * TPS, :], self.affine).then_inc(self.z_ready, 1)

    def add(self, eng, g):
        eng.wait_ge(self.z_ready, g + 1)
        xs = self.x[:, g * TPS:(g + 1) * TPS, :]
        eng.tensor_tensor(xs, xs, self.z, ALU.add).then_inc(self.added, 1)


def apply(act, z, tiles, affine):
    for j in range(TPS):
        last = act.activation(z[:, j, :], tiles[:, j, :], ACT.Identity, scale=affine.scale[:, j:j + 1], bias=affine.shift[:, j:j + 1])
    return last


class TurnNorm:

    def __init__(self, c, keep, tag, z):
        self.keep, self.banks, self.z = keep, None, z
        self.z_ready, self.turned, self.high, self.low = (c.sem(f"{tag}_{n}") for n in ("z", "turned", "high", "low"))
        self.affine = Affine(c, tag, self.z_ready)

    def statistics(self, dve, chain, g, half):
        self.affine.statistics(dve, chain, self.keep.x[:, g * TPS:(g + 1) * TPS, :], g, half)

    def act_apply(self, act, g):
        act.wait_ge(self.affine.ready, g + 1)
        if g:
            act.wait_ge(self.turned, KT * g)
        apply(act, self.z, self.keep.x[:, g * TPS:(g + 1) * TPS, :], self.affine).then_inc(self.z_ready, 1)

    def pe_turn(self, pe, g):
        pe.wait_ge(self.z_ready, g + 1)
        for k in range(KT):
            if g:
                pe.wait_ge(self.low, KT * (g - 1) + k + 1)
            for j in range(TPS):
                last = pe.transpose(self.banks[k][:, j * P:(j + 1) * P], self.z[:, j, k * P:(k + 1) * P], self.keep.ident[:])
            last.then_inc(self.turned, 1)

    def act_high(self, act, g):
        for k in range(KT):
            act.wait_ge(self.turned, KT * g + k + 1)
            act.activation(self.keep.xT_hi[:, k, g * SEG:(g + 1) * SEG], self.banks[k][:], ACT.Copy).then_inc(self.high, 1)

    def dve_low(self, dve, g):
        for k in range(KT):
            dve.wait_ge(self.high, KT * g + k + 1)
            at = slice(g * SEG, (g + 1) * SEG)
            dve.tensor_tensor(self.keep.xT_lo[:, k, at], self.banks[k][:], self.keep.xT_hi[:, k, at].bitcast(F32),
                              ALU.subtract).then_inc(self.low, 1)


class Fetched:

    def __init__(self, c, widths, up, down):
        self.widths = widths
        self.raw = up.rearrange("p (k n) -> p k n", k=KT)
        self.raw_d = down.rearrange("p (j f) -> p j f", f=HID)
        self.up_in, self.down_in = c.sem("up_in"), c.sem("down_in")

    def load(self, sp, w_up, w_down):
        for f in range(KT):
            sp.dma_start(self.raw[:, f, :], w_up[f * P:(f + 1) * P, :]).then_inc(self.up_in, DMA)
        for j, w in enumerate(self.widths):
            start = sum(self.widths[:j])
            sp.dma_start(self.raw_d[0:w, j, :], w_down[start:start + w, :]).then_inc(self.down_in, DMA)


class SwigluWeights:

    def __init__(self, c, widths, fetched=None):
        J, W = len(widths), sum(widths)
        n_up = KT * 2 * W
        if fetched is None:
            self.loaded = c.sb("loaded", [P, n_up + J * HID])
            fetched = Fetched(c, widths, self.loaded[:, 0:n_up], self.loaded[:, n_up:])
        self.raw, self.raw_d, self.up_in, self.down_in, self.load = fetched.raw, fetched.raw_d, fetched.up_in, fetched.down_in, fetched.load
        self.w_lo, self.w_hi = c.sb("w_lo", [P, KT, 2 * W], F32R), c.sb("w_hi", [P, KT, 2 * W], F32R)
        self.d_lo, self.d_hi = c.sb("d_lo", [P, J, HID], F32R), c.sb("d_hi", [P, J, HID], F32R)
        self.up_hi, self.down_hi, self.up_lo, self.down_lo = (c.sem(n) for n in ("up_hi", "down_hi", "up_lo", "down_lo"))


class Swiglu:

    def __init__(self, nc, c, keep, y, banks, widths, start=0, weights=None):
        self.start = start
        self.nc, self.keep, self.y, self.bank, self.widths = nc, keep, y, banks, widths
        self.J, self.W = len(widths), sum(widths)
        self.starts = [sum(widths[:j]) for j in range(self.J)]
        J, W = self.J, self.W
        self.weights = w = weights or SwigluWeights(c, widths)
        self.raw, self.raw_d, self.w_lo, self.w_hi, self.d_lo, self.d_hi = w.raw, w.raw_d, w.w_lo, w.w_hi, w.d_lo, w.d_hi
        self.up_in, self.down_in, self.up_hi, self.down_hi, self.up_lo, self.down_lo = w.up_in, w.down_in, w.up_hi, w.down_hi, w.up_lo, w.down_lo
        self.silu, self.h = c.sb("silu", [P, 2, SEG]), c.sb("h", [P, 2, SEG])
        self.h_hi, self.h_lo = c.sb("h_hi", [P, 2, SEG], F32R), c.sb("h_lo", [P, 2, SEG], F32R)
        self.g_mm, self.u_mm, self.down_mm, self.silu_sb, self.h_sb, self.y_sb = (
            c.sem(n) for n in ("g_mm", "u_mm", "down_mm", "silu", "h", "y"))

    def columns(self, j):
        return [slice(b + self.starts[j], b + self.starts[j] + self.widths[j]) for b in (0, self.W)]

    def act_high(self, act, j):
        w = self.widths[j]
        act.wait_ge(self.up_in, KT * DMA)
        for cols in self.columns(j):
            act.activation(self.w_hi[:, :, cols], self.raw[:, :, cols], ACT.Copy).then_inc(self.up_hi, 1)
        act.wait_ge(self.down_in, self.J * DMA)
        act.activation(self.d_hi[0:w, j, :], self.raw_d[0:w, j, :], ACT.Copy).then_inc(self.down_hi, 1)

    def dve_low(self, dve, j):
        w = self.widths[j]
        for i, cols in enumerate(self.columns(j)):
            dve.wait_ge(self.up_hi, 2 * j + i + 1)
            dve.tensor_tensor(self.w_lo[:, :, cols], self.raw[:, :, cols], self.w_hi[:, :, cols].bitcast(F32), ALU.subtract).then_inc(self.up_lo, 1)
        dve.wait_ge(self.down_hi, j + 1)
        dve.tensor_tensor(self.d_lo[0:w, j, :], self.raw_d[0:w, j, :], self.d_hi[0:w, j, :].bitcast(F32), ALU.subtract).then_inc(self.down_lo, 1)

    def act_step(self, act, g, j):
        n, w = (g - self.start) * self.J + j, self.widths[j]
        b = n % 2
        act.wait_ge(self.g_mm, n + 1)
        if n >= 2:
            act.wait_ge(self.h_sb, n - 1)
        act.activation(self.silu[0:w, b, :], self.bank[b][0:w, :], ACT.Silu).then_inc(self.silu_sb, 1)

    def act_output(self, act, g):
        act.wait_ge(self.down_mm, (g - self.start + 1) * self.J)
        for i in range(2):
            t = g * TPS + 2 * i
            act.activation(self.y[:, t:t + 2, :].rearrange("p t f -> p (t f)"), self.bank[4 + i][:], ACT.Copy).then_inc(self.y_sb, 1)

    def dve_step(self, dve, chain, g, j):
        n, w = (g - self.start) * self.J + j, self.widths[j]
        b = n % 2
        h, h_hi, h_lo = (a[0:w, b, :] for a in (self.h, self.h_hi, self.h_lo))
        dve.wait_ge(self.silu_sb, n + 1)
        dve.wait_ge(self.u_mm, n + 1)
        chain.link(dve.tensor_tensor(h, self.silu[0:w, b, :], self.bank[2 + b][0:w, :], ALU.mult))
        if n >= 2:
            dve.wait_ge(self.down_mm, n - 1)
        chain.link(dve.tensor_copy(h_hi, h))
        dve.tensor_tensor(h_lo, h, h_hi.bitcast(F32), ALU.subtract).then_inc(self.h_sb, 1)

    def pe_up(self, pe, g, j):
        n, w = (g - self.start) * self.J + j, self.widths[j]
        b = n % 2
        toks = slice(g * SEG, (g + 1) * SEG)
        if g == self.start:
            pe.wait_ge(self.up_lo, 2 * j + 2)
        if n >= 2:
            pe.wait_ge(self.h_sb, n - 1)
        for cols, to, sem in zip(self.columns(j), (self.bank[b], self.bank[2 + b]), (self.g_mm, self.u_mm)):
            for f in range(KT):
                last = three_passes(self.nc, to[0:w, :], (self.w_hi[:, f, cols], self.w_lo[:, f, cols]),
                                    (self.keep.xT_hi[:, f, toks], self.keep.xT_lo[:, f, toks]), f == 0, f == KT - 1)
            last.then_inc(sem, 1)

    def pe_down(self, pe, g, j):
        n, w = (g - self.start) * self.J + j, self.widths[j]
        b = n % 2
        pe.wait_ge(self.h_sb, n + 1)
        if g == self.start:
            pe.wait_ge(self.down_lo, j + 1)
        elif j == 0:
            pe.wait_ge(self.y_sb, 2 * (g - self.start))
        for t in range(TPS):
            to = self.bank[4 + t // 2][:, t % 2 * HID:(t % 2 + 1) * HID]
            toks = slice(t * P, (t + 1) * P)
            last = three_passes(self.nc, to, (self.h_hi[0:w, b, toks], self.h_lo[0:w, b, toks]), (self.d_hi[0:w, j, :], self.d_lo[0:w, j, :]),
                                j == 0 and t % 2 == 0, j == self.J - 1, skip=True)
        last.then_inc(self.down_mm, 1)


FFN = [P] * 8


def feed_forward(nc, keep, y, before, turn, fetched, out):
    with Scope(nc, "ffn") as c:
        bank = c.banks(8)
        net = Swiglu(nc, c, keep, y, bank, FFN, weights=SwigluWeights(c, FFN, fetched))
        turn.banks = bank[6:8]
        after = AddNorm(c, keep, "after", y)
        own, pool_own, stored = c.sem("own"), c.sem("pool_own"), c.sem("stored")
        J = net.J
        with nc.Block() as block:
            @block.sync
            def _(sp):
                for g in range(SEGS):
                    sp.wait_ge(after.added, g + 1)
                    at = slice(g * TPS, (g + 1) * TPS)
                    sp.dma_start(out[:, at, :], keep.x[:, at, :]).then_inc(stored, DMA)
                sp.wait_ge(stored, SEGS * DMA)

            @block.gpsimd
            def _(pool):
                chain = Chain(pool, pool_own)
                before.affine.scale_and_shift(pool, chain, 1)
                before.add(pool, 1)
                for g in range(SEGS):
                    if g + 1 < SEGS:
                        turn.affine.scale_and_shift(pool, chain, g + 1)
                    if g:
                        after.affine.scale_and_shift(pool, chain, g - 1)
                        after.add(pool, g - 1)
                    if g + 2 < SEGS:
                        before.affine.scale_and_shift(pool, chain, g + 2)
                        before.add(pool, g + 2)

            @block.vector
            def _(dve):
                chain = Chain(dve, own)
                net.dve_low(dve, 0)
                turn.dve_low(dve, 0)
                net.dve_low(dve, 1)
                for g in range(SEGS):
                    for j in range(J):
                        if g == 0 and j + 2 < J:
                            net.dve_low(dve, j + 2)
                        net.dve_step(dve, chain, g, j)
                        if j < 2 and g + 1 < SEGS:
                            dve.wait_ge(before.added, g + 2)
                            turn.statistics(dve, chain, g + 1, j)
                        if 2 <= j < 4 and g:
                            dve.wait_ge(net.y_sb, 2 * g)
                            after.statistics(dve, chain, g - 1, j - 2)
                        if j == 4 and g + 1 < SEGS:
                            turn.dve_low(dve, g + 1)
                        if 5 <= j < 7 and g + 2 < SEGS:
                            before.statistics(dve, chain, g + 2, j - 5)
                for half in range(2):
                    dve.wait_ge(net.y_sb, 2 * SEGS - 1 + half)
                    after.statistics(dve, chain, SEGS - 1, half)
                after.affine.dve_quick_scale(dve, chain, SEGS - 1)
                after.dve_apply(dve, chain, SEGS - 1)
                after.add(dve, SEGS - 1)

            @block.scalar
            def _(act):
                net.act_high(act, 0)
                turn.act_high(act, 0)
                net.act_high(act, 1)
                before.act_apply(act, 1)
                for g in range(SEGS):
                    for j in range(J):
                        if g == 0 and j + 2 < J:
                            net.act_high(act, j + 2)
                        net.act_step(act, g, j)
                        if g + 1 < SEGS:
                            if j == 2:
                                turn.act_apply(act, g + 1)
                            if j == 3:
                                turn.act_high(act, g + 1)
                        if j == 4 and g:
                            after.act_apply(act, g - 1)
                        if j == 1 and g:
                            net.act_output(act, g - 1)
                        if j == 7 and g + 2 < SEGS:
                            before.act_apply(act, g + 2)
                net.act_output(act, SEGS - 1)
                after.affine.act_root(act)

            @block.tensor
            def _(pe):
                turn.pe_turn(pe, 0)
                for g in range(SEGS):
                    pe.wait_ge(turn.low, KT * (g + 1))
                    for j in range(J):
                        net.pe_up(pe, g, j)
                        if j >= 2 or g:
                            n = g * J + j - 2
                            net.pe_down(pe, n // J, n % J)
                        if j == 3 and g + 1 < SEGS:
                            turn.pe_turn(pe, g + 1)
                for j in (J - 2, J - 1):
                    net.pe_down(pe, SEGS - 1, j)


NE, TOP, INNER = 16, 2, 176
IH = INNER // 2
SLOT_TILES = (TOP * TOK + NE * (P - 1)) // P
SLOT_TILES += SLOT_TILES % 2
SLOTS = SLOT_TILES * P


class Router:

    def __init__(self, nc, c, keep, banks, place):
        self.nc, self.keep = nc, keep
        used = [0]

        def placed(*shape):
            n = int(np.prod(shape))
            part = place[:, used[0]:used[0] + n]
            used[0] += n
            return part if len(shape) == 1 else part.rearrange("p (a b) -> p a b", b=shape[1])
        self.logits_bank, self.turned_bank, self.ranks_bank, self.tokens_bank = banks
        self.gate = c.sb("gate", [P, KT, P])
        self.g_hi, self.g_lo = c.sb("g_hi", [P, KT, P], F32R), c.sb("g_lo", [P, KT, P], F32R)
        self.logits_T = c.sb("logits_T", [NE, TPS, P])
        full = lambda n, dt=F32: c.sb(n, [P, TT, NE], dt)
        self.score, self.key, self.rest, self.one1, self.one2 = (placed(TT, NE) for _ in range(5))
        self.top, self.total, self.best, self.where = (c.sb(n, [P, TT]) for n in ("top", "total", "best", "where"))
        self.chosen = full("chosen", BF16)
        self.before, self.every = c.sb("before", [P, P], BF16), c.sb("every", [P, P], BF16)
        self.rank_first, self.thresholds = c.sb("rank_first", [P, NE]), c.sb("thresholds", [P, NE])
        self.upto, self.counts_over = c.sb("upto", [P, NE, NE]), c.sb("counts_over", [P, NE, NE])
        self.tiles, self.tiles_to, self.base = (c.sb(n, [P, NE]) for n in ("tiles", "tiles_to", "base"))
        self.tile_no, self.expert_f = c.sb("tile_no", [1, SLOT_TILES]), c.sb("expert_f", [1, SLOT_TILES])
        self.row_i, self.tile_i, self.row_f, self.tile_f = (
            [c.sb(f"{n}{b}", [P, TT], dt) for b in range(2)] for n, dt in (("row_i", I32), ("tile_i", I32), ("row_f", F32), ("tile_f", F32)))
        hot = keep.squares[:].bitcast(BF16).rearrange("p (b t r) -> p b t r", b=2, t=TT)
        self.row_hot = [hot[:, b] for b in range(2)]
        self.tile_hot = placed(TT, SLOT_TILES)
        self.passed = self.tile_hot.rearrange("p a b -> p (a b)").rearrange("p (s e) -> p s e", e=NE)[0:1]
        self.token_hot = [c.sb(f"token_hot{b}", [P, TT, 2, SLOT_TILES], BF16) for b in range(2)]
        self.row_no, self.slot_tile_no, self.token_tile_no, self.part_no = (
            c.sb(n, shape) for n, shape in (("row_no", [P, P]), ("slot_tile_no", [P, SLOT_TILES]), ("token_tile_no", [P, TT]), ("part_no", [P, 1])))
        self.token_f = c.sb("token_f", [P, SLOT_TILES])
        self.rows_ready, self.row_hot_ready, self.token_hot_ready, self.tokens_mm = (
            c.sem(n) for n in ("rows", "row_hot", "token_hot", "tokens_mm"))
        self.zeroed, self.gate_in, self.gate_hi, self.gate_lo, self.made, self.logits_mm, self.logits_sb, self.logits_T_mm = (
            c.sem(n) for n in ("zeroed", "gate_in", "gate_hi", "gate_lo", "made", "logits_mm", "logits_sb", "logits_T_mm"))
        self.score_in, self.shifted, self.exps, self.chosen_ready, self.ranks = (
            c.sem(n) for n in ("score_in", "shifted", "exps", "chosen_ready", "ranks"))
        self.over_e = lambda a: a.rearrange("p (t o) -> p t o", o=1).broadcast_to([P, TT, NE])
        self.over_t = lambda a: a.rearrange("p (o e) -> p o e", o=1).broadcast_to([P, TT, NE])

    def load(self, sp, gate_w):
        sp.wait_ge(self.zeroed, 1)
        sp.dma_start(self.gate[:, :, 0:NE], gate_w).then_inc(self.gate_in, DMA)

    def pool_constants(self, pool):
        made, upto, before = self.made, self.upto, self.before
        iota = lambda out, pattern, base, mult: pool.iota(out, pattern=pattern, base=base, channel_multiplier=mult,
                                                          allow_small_or_imprecise_dtypes=True).then_inc(made, 1)
        iota(self.rank_first[:], [[-1, NE]], NE, 0)
        iota(self.thresholds[:], [[P, NE]], 0, 0)
        iota(self.tile_no[:], [[1, SLOT_TILES]], 0, 0)
        iota(self.row_no[:], [[1, P]], 0, 0)
        iota(self.slot_tile_no[:], [[1, SLOT_TILES]], 0, 0)
        iota(self.token_tile_no[:], [[1, TT]], 0, 0)
        iota(self.part_no[:], [[0, 1]], 0, 1)
        pool.memset(upto[:], 1.0).then_inc(made, 1)
        pool.memset(before[:], 1.0).then_inc(made, 1)
        pool.memset(self.every[:], 1.0).then_inc(made, 1)
        pool.wait_ge(made, 10)
        pool.affine_select(out=upto[:], in_=upto[:], compare_op=ALU.is_ge, fill=0.0, base=0,
                           pattern=[[1, NE], [-1, NE]], channel_multiplier=0).then_inc(made, 1)
        pool.affine_select(out=before[:], in_=before[:], compare_op=ALU.is_gt, fill=0.0, base=0,
                           pattern=[[1, P]], channel_multiplier=-1).then_inc(made, 1)

    def dve_row_one_hot(self, dve, b):
        dve.wait_ge(self.rows_ready, 4)
        row = self.row_f[b][:].rearrange("p (t o) -> p t o", o=1).broadcast_to([P, TT, P])
        number = self.row_no[:].rearrange("p (o r) -> p o r", o=1).broadcast_to([P, TT, P])
        dve.tensor_tensor(self.row_hot[b], row, number, ALU.is_equal).then_inc(self.row_hot_ready, 1)

    def dve_token_one_hot(self, dve, chain, b):
        tiles = lambda a: a.rearrange("p (t o) -> p t o", o=1).broadcast_to([P, TT, SLOT_TILES])
        number = self.slot_tile_no[:].rearrange("p (o s) -> p o s", o=1).broadcast_to([P, TT, SLOT_TILES])
        chain.link(dve.tensor_tensor(self.tile_hot[:], tiles(self.tile_f[b][:]), number, ALU.is_equal))
        chain.step(dve.tensor_tensor(self.token_hot[b][:, :, 0, :], self.tile_hot[:], tiles(self.token_tile_no[:]), ALU.mult))
        chain.wait()
        dve.tensor_scalar(self.token_hot[b][:, :, 1, :], self.tile_hot[:], self.part_no[:, 0:1], None, ALU.mult).then_inc(self.token_hot_ready, 1)

    def pe_tokens(self, pe):
        pe.wait_ge(self.row_hot_ready, 2)
        pe.wait_ge(self.token_hot_ready, 2)
        for b in range(2):
            for t in range(TT):
                last = pe.matmul(self.tokens_bank[:, 0:2 * SLOT_TILES], self.row_hot[b][:, t, :], self.token_hot[b][:, t, :, :].rearrange("p a s -> p (a s)"),
                                 start=b == 0 and t == 0, stop=b == 1 and t == TT - 1)
        last.then_inc(self.tokens_mm, 1)

    def dve_tokens(self, dve, chain):
        dve.wait_ge(self.tokens_mm, 1)
        chain.link(dve.tensor_scalar(self.token_f[:], self.tokens_bank[:, 0:SLOT_TILES], float(P), None, ALU.mult))
        chain.link(dve.tensor_tensor(self.token_f[:], self.token_f[:], self.tokens_bank[:, SLOT_TILES:2 * SLOT_TILES], ALU.add))
        chain.link(dve.tensor_copy(self.keep.slot_token[:], self.token_f[:]))

    def act_gate(self, act):
        act.wait_ge(self.gate_in, DMA)
        act.activation(self.g_hi[:], self.gate[:], ACT.Copy).then_inc(self.gate_hi, 1)

    def dve_gate(self, dve):
        dve.wait_ge(self.gate_hi, 1)
        dve.tensor_tensor(self.g_lo[:], self.gate[:], self.g_hi[:].bitcast(F32), ALU.subtract).then_inc(self.gate_lo, 1)

    def pe_logits(self, pe, g):
        toks = slice(g * SEG, (g + 1) * SEG)
        if g == 0:
            pe.wait_ge(self.gate_lo, 1)
        else:
            pe.wait_ge(self.logits_sb, g)
        for f in range(KT):
            last = three_passes(self.nc, self.logits_bank[:], (self.g_hi[:, f, :], self.g_lo[:, f, :]),
                                (self.keep.xT_hi[:, f, toks], self.keep.xT_lo[:, f, toks]), f == 0, f == KT - 1)
        last.then_inc(self.logits_mm, 1)

    def act_logits(self, act, g):
        act.wait_ge(self.logits_mm, g + 1)
        if g:
            act.wait_ge(self.logits_T_mm, g)
        act.activation(self.logits_T[:].rearrange("e t p -> e (t p)"), self.logits_bank[0:NE, :], ACT.Copy).then_inc(self.logits_sb, 1)

    def pe_turn(self, pe, g):
        pe.wait_ge(self.logits_sb, g + 1)
        if g:
            pe.wait_ge(self.score_in, g)
        for t in range(TPS):
            last = pe.transpose(self.turned_bank[:, t * NE:(t + 1) * NE], self.logits_T[:, t, :], self.keep.ident[0:NE, 0:NE])
        last.then_inc(self.logits_T_mm, 1)

    def act_score(self, act, g):
        act.wait_ge(self.logits_T_mm, g + 1)
        act.activation(self.score[:, g * TPS:(g + 1) * TPS, :].rearrange("p t e -> p (t e)"), self.turned_bank[:, 0:TPS * NE],
                       ACT.Copy).then_inc(self.score_in, 1)

    def dve_shift(self, dve, chain):
        score, top = self.score, self.top
        dve.wait_ge(self.score_in, SEGS)
        chain.link(dve.tensor_reduce(top[:], score[:], AX.X, ALU.max))
        dve.tensor_tensor(score[:], score[:], self.over_e(top[:]), ALU.subtract).then_inc(self.shifted, 1)

    def act_exp(self, act):
        act.wait_ge(self.shifted, 1)
        act.activation(self.score[:], self.score[:], ACT.Exp).then_inc(self.exps, 1)

    def dve_scores(self, dve, chain):
        score, top, total = self.score, self.top, self.total
        dve.wait_ge(self.exps, 1)
        chain.link(dve.tensor_reduce(total[:], score[:], AX.X, ALU.add))
        chain.link(dve.reciprocal(top[:], total[:]))
        chain.link(dve.tensor_tensor(score[:], score[:], self.over_e(top[:]), ALU.mult))

    def dve_choose(self, dve, chain, n):
        key, best = self.key, self.best
        left, one, weight = ((self.score, self.one1, self.keep.weight1), (self.rest, self.one2, self.keep.weight2))[n]
        chain.link(dve.tensor_reduce(weight[:], left[:], AX.X, ALU.max))
        chain.link(dve.tensor_tensor(key[:], left[:], self.over_e(weight[:]), ALU.is_equal))
        dve.wait_ge(self.made, 12)
        chain.link(dve.tensor_tensor(key[:], key[:], self.over_t(self.rank_first[:]), ALU.mult))
        chain.link(dve.tensor_reduce(best[:], key[:], AX.X, ALU.max))
        chain.link(dve.tensor_tensor(one[:], key[:], self.over_e(best[:]), ALU.is_equal))
        if n == 0:
            chain.link(dve.scalar_tensor_tensor(self.rest[:], one[:], -2.0, self.score[:], ALU.mult, ALU.add))
        else:
            dve.tensor_tensor(self.chosen[:], self.one1[:], self.one2[:], ALU.add).then_inc(self.chosen_ready, 1)

    def pe_ranks(self, pe):
        chosen, every, bank = self.chosen, self.every, self.ranks_bank
        pe.wait_ge(self.chosen_ready, 1)
        pe.wait_ge(self.made, 12)
        for t in range(TT):
            pe.matmul(bank[:, TT * NE:TT * NE + NE], every[:], chosen[:, t, :], start=t == 0, stop=t == TT - 1, skip_group_check=True)
        pe.matmul(bank[:, 0:TT * NE], self.before[:], chosen[:].rearrange("p t e -> p (t e)"), start=False, stop=False, skip_group_check=True)
        for t in range(TT - 1):
            later = TT - 1 - t
            last = pe.matmul(bank[:, (t + 1) * NE:TT * NE].rearrange("p (t e) -> p t e", e=NE), every[:],
                             chosen[:, t:t + 1, :].broadcast_to([P, later, NE]), start=False, stop=t == TT - 2, skip_group_check=True)
        last.then_inc(self.ranks, 1)

    def dve_slots(self, dve, chain):
        counts_over, tiles, tiles_to, base, rest, key, where = (
            self.counts_over, self.tiles, self.tiles_to, self.base, self.rest, self.key, self.where)
        dve.wait_ge(self.ranks, 1)
        per = lambda a: a.rearrange("p (e o) -> p e o", o=1).broadcast_to([P, NE, NE])
        along = lambda a: a.rearrange("p (o e) -> p o e", o=1).broadcast_to([P, NE, NE])
        chain.link(dve.tensor_copy(base[:], self.ranks_bank[:, TT * NE:TT * NE + NE]))
        chain.link(dve.tensor_tensor(counts_over[:], per(base[:]), along(self.thresholds[:]), ALU.is_gt))
        chain.link(dve.tensor_reduce(tiles[:], counts_over[:], AX.X, ALU.add))
        chain.link(dve.tensor_tensor(counts_over[:], self.upto[:], along(tiles[:]), ALU.mult))
        chain.link(dve.tensor_reduce(tiles_to[:], counts_over[:], AX.X, ALU.add))
        chain.link(dve.tensor_tensor(base[:], tiles_to[:], tiles[:], ALU.subtract))
        chain.link(dve.tensor_scalar(base[:], base[:], float(P), None, ALU.mult))
        chain.link(dve.tensor_tensor(rest[:], self.ranks_bank[:, 0:TT * NE].rearrange("p (t e) -> p t e", e=NE), self.over_t(base[:]), ALU.add))
        for b, (one, slot) in enumerate(((self.one1, self.keep.slot1), (self.one2, self.keep.slot2))):
            chain.link(dve.tensor_tensor(key[:], rest[:], one[:], ALU.mult))
            chain.link(dve.tensor_reduce(where[:], key[:], AX.X, ALU.add))
            chain.link(dve.tensor_copy(slot[:], where[:]))
            chain.step(dve.tensor_scalar(self.row_i[b][:], slot[:], P - 1, None, ALU.bitwise_and))
            chain.link(dve.tensor_scalar(self.tile_i[b][:], slot[:], P.bit_length() - 1, None, ALU.logical_shift_right))
            dve.tensor_copy(self.row_f[b][:], self.row_i[b][:]).then_inc(self.rows_ready, 1)
            dve.tensor_copy(self.tile_f[b][:], self.tile_i[b][:]).then_inc(self.rows_ready, 1)

    def dve_tiles(self, dve, chain):
        ends = self.tiles_to[0:1, :].rearrange("p (o e) -> p o e", o=1).broadcast_to([1, SLOT_TILES, NE])
        numbers = self.tile_no[:].rearrange("p (i o) -> p i o", o=1).broadcast_to([1, SLOT_TILES, NE])
        dve.wait_ge(self.token_hot_ready, 2)
        chain.link(dve.tensor_tensor(self.passed[:], numbers, ends, ALU.is_ge))
        chain.link(dve.tensor_reduce(self.expert_f[:], self.passed[:], AX.X, ALU.add))
        chain.link(dve.tensor_scalar(self.expert_f[:], self.expert_f[:], float(NE - 1), None, ALU.min))
        chain.link(dve.tensor_copy(self.keep.expert_of[:], self.expert_f[:]))


SHARED = [P, P, 2 * INNER - 2 * P]
SHARED_EARLY = SEGS // 2


def close_attention_and_route(nc, keep, y, output, norms, w_up, w_down, gate_w, tokens_x, expert_up):
    with Scope(nc, "route") as c:
        bank = c.banks(8)
        normed = norms.z_all
        norms.banks = bank[6:8]
        net = Swiglu(nc, c, keep, y, bank, SHARED, weights=keep.shared)
        router = Router(nc, c, keep, (bank[4], bank[5], bank[6], bank[7]), net.weights.loaded)
        stored, own = c.sem("stored"), c.sem("own")
        L = SEGS - 1
        J = net.J
        STEPS = [(g, j) for g in range(SHARED_EARLY) for j in range(J)]
        with nc.Block() as block:
            @block.sync
            def _(sp):
                router.load(sp, gate_w)
                net.weights.load(sp, w_up, w_down)
                for e in range(NE):
                    sp.dma_start(keep.expert_up[:, e], expert_up[e]).then_inc(keep.expert_up_in, DMA)
                tiles = tokens_x.rearrange("(t p) f -> p t f", p=P)
                for g in range(SEGS):
                    sp.wait_ge(norms.z_x_ready, g + 1)
                    at = slice(g * TPS, (g + 1) * TPS)
                    sp.dma_start(tiles[:, at, :], normed[:, at, :]).then_inc(stored, DMA)
                sp.wait_ge(stored, SEGS * DMA)

            @block.gpsimd
            def _(pool):
                router.pool_constants(pool)

            @block.vector
            def _(dve):
                chain = Chain(dve, own)
                dve.memset(router.gate[:], 0.0).then_inc(router.zeroed, 1)
                output.dve_factor(dve, L, bank[0:2])
                router.dve_gate(dve)
                for j in range(J):
                    net.dve_low(dve, j)
                norms.dve_low(dve, 0)
                norms.dve_round(dve, chain, L, lambda half: dve.wait_ge(output.y_ready, 2 * L + half + 1), split=False)
                norms.dve_low(dve, 1)
                norms.dve_round(dve, chain, L + 1, split=False)
                norms.dve_low(dve, 2)
                norms.dve_low(dve, 3)
                router.dve_shift(dve, chain)
                for n, (g, j) in enumerate(STEPS):
                    net.dve_step(dve, chain, g, j)
                    if n == 0:
                        router.dve_scores(dve, chain)
                        router.dve_choose(dve, chain, 0)
                    if n == 1:
                        router.dve_choose(dve, chain, 1)
                    if n == 2:
                        router.dve_slots(dve, chain)
                    if n == 3:
                        router.dve_row_one_hot(dve, 0)
                        router.dve_token_one_hot(dve, chain, 0)
                router.dve_row_one_hot(dve, 1)
                router.dve_token_one_hot(dve, chain, 1)
                router.dve_tiles(dve, chain)
                router.dve_tokens(dve, chain)

            @block.scalar
            def _(act):
                output.act_root(act, L)
                router.act_gate(act)
                for j in range(J):
                    net.act_high(act, j)
                norms.act_high(act, 0)
                output.act_take(act, L, bank[0:2])
                norms.act_root(act, L, split=False)
                router.act_logits(act, 0)
                norms.act_high(act, 1)
                router.act_score(act, 0)
                norms.act_apply(act, L)
                router.act_logits(act, 1)
                norms.act_root(act, L + 1, split=False)
                norms.act_high(act, 2)
                router.act_score(act, 1)
                norms.act_apply(act, L + 1)
                router.act_logits(act, 2)
                norms.act_high(act, 3)
                router.act_score(act, 2)
                router.act_logits(act, 3)
                router.act_score(act, 3)
                router.act_exp(act)
                for n, (g, j) in enumerate(STEPS):
                    net.act_step(act, g, j)
                    if j == 1 and g:
                        net.act_output(act, g - 1)
                net.act_output(act, SHARED_EARLY - 1)

            @block.tensor
            def _(pe):
                output.pe_sums(pe, L, bank[0:2])
                norms.pe_turn(pe, 0)
                output.pe_turn(pe, L, bank[0:2])
                for g in range(SEGS):
                    if g:
                        norms.pe_turn(pe, g)
                        router.pe_turn(pe, g - 1)
                    pe.wait_ge(norms.low, KT * (g + 1))
                    router.pe_logits(pe, g)
                router.pe_turn(pe, L)
                for n, (g, j) in enumerate(STEPS):
                    net.pe_up(pe, g, j)
                    if n >= 2:
                        net.pe_down(pe, *STEPS[n - 2])
                    if n == 2:
                        router.pe_ranks(pe)
                net.pe_down(pe, *STEPS[-2])
                net.pe_down(pe, *STEPS[-1])
                router.pe_tokens(pe)


def experts(nc, keep, w_down, tokens_x, sorted_y):
    with Scope(nc, "experts") as c:
        up, down_w = keep.expert_up, c.sb("down", [IH, NE, 2, HID])
        place = keep.acc[:].rearrange("p s k t -> p (s k t)")
        widths = (HID, KT * P, INNER, INNER, 2 * P, HID)
        starts = [2 * sum(widths[:n]) for n in range(len(widths))]
        xs, xT, silu, h, hT, ys = ([place[:, start + b * width:start + (b + 1) * width] for b in range(2)] for start, width in zip(starts, widths))
        xT = [a.rearrange("p (k t) -> p k t", k=KT) for a in xT]
        hT = [a[0:IH, :].rearrange("p (i t) -> p i t", i=2) for a in hT]
        bank = c.banks(8)
        down_in = c.sem("down_in")
        xs_in = [c.sem("xs_in0"), c.sem("xs_in1")]
        stored = [c.sem("stored0"), c.sem("stored1")]
        x_turned, xT_sb, gu_mm, silu_sb, h_sb, h_turned, hT_sb, y_mm, ys_sb = (
            c.sem(n) for n in ("x_turned", "xT", "gu_mm", "silu", "h", "h_turned", "hT", "y_mm", "ys"))
        PASSES = SLOT_TILES // 2
        row = lambda a, i: a[bass.ds(i * P, P), :]

        def passes(eng, body):
            body(0, True, False)
            with eng.Fori(0, PASSES // 2 - 1) as n:
                body(2 * n + 1, False, False)
                body(2 * n + 2, False, False)
            body(PASSES - 1, False, True)

        with nc.Block() as block:
            @block.sync
            def _(sp):
                def store(k, first, last):
                    for b in range(2):
                        sp.wait_ge(ys_sb, 2 * k + b + 1)
                        sp.dma_start(row(sorted_y, 2 * k + b), ys[b][:]).then_inc(stored[b], DMA)

                for e in range(NE):
                    sp.dma_start(down_w[:, e], w_down[e]).then_inc(down_in, DMA)
                passes(sp, store)
                for b in range(2):
                    sp.wait_ge(stored[b], PASSES * DMA)

            @block.gpsimd
            def _(pool):
                for i in range(SLOT_TILES):
                    if i >= 2:
                        pool.wait_ge(x_turned, i - 1)
                    pool.indirect_dma_start(out=xs[i % 2][:], out_offset=None, in_=tokens_x,
                                            in_offset=bass.IndirectOffsetOnAxis(ap=keep.slot_token[:, i:i + 1], axis=0)).then_inc(xs_in[i % 2], DMA)

            @block.tensor
            def _(pe):
                def turn_x(k, b):
                    pe.wait_ge(xs_in[b], (k + 1) * DMA)
                    for f in range(KT):
                        done = pe.transpose(bank[b][:, f * P:(f + 1) * P], xs[b][:, f * P:(f + 1) * P], keep.ident[:])
                    done.then_inc(x_turned, 1)

                def products(k, first, last):
                    of = [pe.value_load(keep.expert_of[0:1, bass.ds(2 * k + b, 1)], min_val=0, max_val=NE - 1) for b in range(2)]
                    for b, e in enumerate(of):
                        pe.wait_ge(xT_sb, 2 * k + b + 1)
                        for f in range(KT):
                            done = pe.matmul(bank[2 + b][:, 0:2 * INNER], xT[b][:, f, :], up[:, bass.ds(e, 1), f, :].rearrange("p a f -> p (a f)"),
                                             start=f == 0, stop=f == KT - 1)
                        done.then_inc(gu_mm, 1)
                    for b in range(2):
                        if not last:
                            turn_x(k + 1, b)
                        pe.wait_ge(h_sb, 2 * k + b + 1)
                        for i in range(2):
                            done = pe.transpose(bank[4 + b][0:IH, i * P:(i + 1) * P], h[b][:, i * IH:(i + 1) * IH], keep.ident[:])
                        done.then_inc(h_turned, 1)
                    if first:
                        pe.wait_ge(down_in, NE * DMA)
                    for b, e in enumerate(of):
                        if not first:
                            pe.wait_ge(ys_sb, 2 * k + b - 1)
                        pe.wait_ge(hT_sb, 2 * k + b + 1)
                        for i in range(2):
                            done = pe.matmul(bank[6 + b][:, 0:HID], hT[b][:, i, :], down_w[:, bass.ds(e, 1), i, :].rearrange("p a f -> p (a f)"),
                                             start=i == 0, stop=i == 1)
                        done.then_inc(y_mm, 1)

                for b in range(2):
                    turn_x(0, b)
                pe.wait_ge(keep.expert_up_in, NE * DMA)
                passes(pe, products)

            @block.scalar
            def _(act):
                def copy_x(k):
                    for b in range(2):
                        act.wait_ge(x_turned, 2 * k + b + 1)
                        act.activation(xT[b][:].rearrange("p k t -> p (k t)"), bank[b][:, 0:HID], ACT.Copy).then_inc(xT_sb, 1)

                def body(k, first, last):
                    for b in range(2):
                        act.wait_ge(gu_mm, 2 * k + b + 1)
                        if not first:
                            act.wait_ge(h_sb, 2 * k + b - 1)
                        act.activation(silu[b][:], bank[2 + b][:, 0:INNER], ACT.Silu).then_inc(silu_sb, 1)
                    if not last:
                        copy_x(k + 1)
                copy_x(0)
                passes(act, body)

            @block.vector
            def _(dve):
                def body(k, first, last):
                    for b in range(2):
                        dve.wait_ge(silu_sb, 2 * k + b + 1)
                        dve.tensor_tensor(h[b][:], silu[b][:], bank[2 + b][:, INNER:2 * INNER], ALU.mult).then_inc(h_sb, 1)
                    for b in range(2):
                        dve.wait_ge(h_turned, 2 * k + b + 1)
                        dve.tensor_copy(hT[b][:].rearrange("p k t -> p (k t)"), bank[4 + b][0:IH, 0:HID]).then_inc(hT_sb, 1)
                    for b in range(2):
                        dve.wait_ge(y_mm, 2 * k + b + 1)
                        if not first:
                            dve.wait_ge(stored[b], k * DMA)
                        dve.tensor_copy(ys[b][:], bank[6 + b][:, 0:HID]).then_inc(ys_sb, 1)
                passes(dve, body)


def combine_and_norm(nc, keep, sorted_y, y, window, w):
    with Scope(nc, "combine") as c:
        got = [c.sb(f"got{b}", [P, TT, HID]) for b in range(2)]
        bank = c.banks(8)
        net = Swiglu(nc, c, keep, y, bank, SHARED, SHARED_EARLY, keep.shared)
        norms = Norms(c, keep, "norms", y, bank[6:8], pool_from=2)
        STEPS = [(g, j) for g in range(SHARED_EARLY, SEGS) for j in range(net.J)]
        arrived = [c.sem(f"arrived{t}") for t in range(TT)]
        own, weighted, first_added = c.sem("own"), c.sem("weighted"), c.sem("first_added")
        first = c.sb("first", [P, TPS, HID])
        with nc.Block() as block:
            @block.sync
            def _(sp):
                window.sp_load(sp, w)

            @block.gpsimd
            def _(pool):
                window.pool_zero(pool)
                for t in range(TT):
                    for b, slot in enumerate((keep.slot1, keep.slot2)):
                        pool.indirect_dma_start(out=got[b][:, t, :], out_offset=None, in_=sorted_y,
                                                in_offset=bass.IndirectOffsetOnAxis(ap=slot[:, t:t + 1], axis=0)).then_inc(arrived[t], DMA)
                for r in range(norms.pool_from, SEGS + 1):
                    norms.pool_add(pool, r)
                    if r == norms.pool_from:
                        pool.wait_ge(net.y_sb, 2 * (SEGS - SHARED_EARLY))
                        for t in range((SEGS - 1) * TPS, TT):
                            pool.wait_ge(arrived[t], 2 * DMA)
                            pool.tensor_scalar(first[:, t % TPS, :], got[0][:, t, :], keep.weight1[:, t:t + 1], None, ALU.mult).then_inc(weighted, 1)
                        pool.wait_ge(weighted, TPS)
                        last = slice((SEGS - 1) * TPS, TT)
                        pool.tensor_tensor(y[:, last, :], y[:, last, :], first[:], ALU.add).then_inc(first_added, 1)
                window.pool_low(pool)

            @block.vector
            def _(dve):
                chain = Chain(dve, own)
                for r in range(norms.ROUNDS):
                    beside = r < SEGS - SHARED_EARLY
                    if beside:
                        net.dve_step(dve, chain, SHARED_EARLY + r, 0)
                    if r < SEGS:
                        if r >= SHARED_EARLY:
                            dve.wait_ge(net.y_sb, 2 * (r - SHARED_EARLY + 1))
                        if r == SEGS - 1:
                            dve.wait_ge(first_added, 1)
                        for b, weight in enumerate((keep.weight1, keep.weight2)):
                            if r == SEGS - 1 and b == 0:
                                continue
                            for t in range(r * TPS, (r + 1) * TPS):
                                dve.wait_ge(arrived[t], 2 * DMA)
                                chain.step(dve.scalar_tensor_tensor(y[:, t, :], got[b][:, t, :], weight[:, t:t + 1], y[:, t, :], ALU.mult, ALU.add))
                            chain.wait()
                    if beside:
                        net.dve_step(dve, chain, SHARED_EARLY + r, 1)
                    norms.dve_round(dve, chain, r)
                    if beside:
                        net.dve_step(dve, chain, SHARED_EARLY + r, 2)

            @block.scalar
            def _(act):
                for r in range(norms.ROUNDS):
                    beside = r < SEGS - SHARED_EARLY
                    if beside:
                        net.act_step(act, SHARED_EARLY + r, 0)
                        net.act_step(act, SHARED_EARLY + r, 1)
                        if r:
                            net.act_output(act, SHARED_EARLY + r - 1)
                    norms.act_root(act, r)
                    norms.act_apply(act, r)
                    if beside:
                        net.act_step(act, SHARED_EARLY + r, 2)
                    if r == SEGS - SHARED_EARLY - 1:
                        net.act_output(act, SEGS - 1)
                        window.act_high(act)

            @block.tensor
            def _(pe):
                for n, step in enumerate(STEPS):
                    net.pe_up(pe, *step)
                    if n >= 2:
                        net.pe_down(pe, *STEPS[n - 2])
                for step in STEPS[-2:]:
                    net.pe_down(pe, *step)
                for g in range(SEGS):
                    norms.pe_turn(pe, g)


def moe_keep(keep, c):
    keep.weight1, keep.weight2 = c.sb("weight1", [P, TT]), c.sb("weight2", [P, TT])
    keep.slot1, keep.slot2 = c.sb("slot1", [P, TT], I32), c.sb("slot2", [P, TT], I32)
    keep.expert_of = c.sb("expert_of", [1, SLOT_TILES], I32)
    keep.slot_token = c.sb("slot_token", [P, SLOT_TILES], I32)


def lay_out_moe(gate_w, w_gate_up, w_down):
    return {"gw": np.ascontiguousarray(gate_w.reshape(NE, KT, P).transpose(2, 1, 0)),
            "wgu": np.ascontiguousarray(w_gate_up.reshape(NE, KT, P, 2 * INNER).transpose(0, 2, 1, 3)),
            "wdn": np.ascontiguousarray(w_down.reshape(NE, 2, IH, HID).transpose(0, 2, 1, 3))}


WH, WD, WG, WIN = 16, 16, 2, 32
REP = WH // WG
STEP = WIN // 2
USED = SEQ // WIN * STEP + STEP
WPAIRS = SEQ // WIN // 2
GD = WG * WD
RR = REP // 4


class WindowWeights:

    def __init__(self, c):
        sb = c.sb
        self.wq, self.wq_hi, self.wq_lo = sb("wq", [P, KT, HID]), sb("wq_hi", [P, KT, HID], F32R), sb("wq_lo", [P, KT, HID], F32R)
        self.wkv, self.wkv_hi, self.wkv_lo = sb("wkv", [P, KT, P]), sb("wkv_hi", [P, KT, P], F32R), sb("wkv_lo", [P, KT, P], F32R)
        self.wo, self.bo = sb("wo", [P, RR, HID]), sb("bo", [P, HID])
        self.bq, self.bkv = sb("bq", [P, RR]), sb("bkv", [2 * GD, 1])
        self.zero, self.arrived, self.split_hi, self.split_lo = (c.sem(n) for n in ("wkv_zero", "win_arrived", "win_split_hi", "win_split_lo"))

    def sp_load(self, sp, w):
        loads = [(self.wq[:], w["Wq"].rearrange("(k p) n -> p k n", p=P))]
        loads += [(self.wkv[:, :, n * GD:(n + 1) * GD], w[name].rearrange("(k p) n -> p k n", p=P)) for n, name in enumerate(("Wk", "Wv"))]
        loads += [(self.bkv[n * GD:(n + 1) * GD, :], w[name]) for n, name in enumerate(("bk", "bv"))]
        loads += [(self.bq[:], w["bq"]), (self.wo[:], w["Wo"].rearrange("(r n) f -> n r f", n=P)),
                  (self.bo[:], w["bo"].rearrange("(o f) -> o f", o=1).broadcast_to([P, HID]))]
        self.loads = len(loads)
        sp.wait_ge(self.zero, 1)
        for to, source in loads:
            sp.dma_start(to, source).then_inc(self.arrived, DMA)

    def pool_zero(self, pool):
        pool.memset(self.wkv[:], 0.0).then_inc(self.zero, 1)

    def act_high(self, act):
        act.wait_ge(self.arrived, self.loads * DMA)
        act.activation(self.wkv_hi[:], self.wkv[:], ACT.Copy).then_inc(self.split_hi, 1)
        act.activation(self.wq_hi[:], self.wq[:], ACT.Copy).then_inc(self.split_hi, 1)

    def pool_low(self, pool):
        for n, (whole, hi, lo) in enumerate(((self.wkv, self.wkv_hi, self.wkv_lo), (self.wq, self.wq_hi, self.wq_lo))):
            pool.wait_ge(self.split_hi, n + 1)
            pool.tensor_tensor(lo[:], whole[:], hi[:].bitcast(F32), ALU.subtract).then_inc(self.split_lo, 1)


def window_attention(nc, keep, y, weights, before, turn, fetched, w):
    with Scope(nc, "win") as c:
        sb = c.sb
        wq_hi, wq_lo, wkv_hi, wkv_lo = weights.wq_hi, weights.wq_lo, weights.wkv_hi, weights.wkv_lo
        wo, bo, bq, bkv = weights.wo, weights.bo, weights.bq, weights.bkv
        qT, kvT = sb("qT", [P, BATCH, RR, USED]), sb("kvT", [2 * GD, BATCH, USED])
        q2 = sb("q2", [P, REP, WPAIRS * WIN])
        q3 = sb("q3", [P, RR, WPAIRS, 4, WIN])
        k2 = sb("k2", [P, 2, WG, WPAIRS * WIN])
        vdup = y[:].rearrange("p t f -> p (t f)").rearrange("p (b m h g k) -> p b m h g k", b=BATCH, m=WPAIRS, h=2, g=WG)
        v2 = sb("v2", [P, BATCH, WPAIRS, 2 * GD])
        less, prob, norm = ([sb(f"{n}{b}", [P, SEG]) for b in range(2)] for n in ("less", "prob", "norm"))
        pT = [sb(f"pT{b}", [P, SEG]) for b in range(2)]
        most, total, inv = ([sb(f"{n}{b}", [P, SEG // WIN]) for b in range(2)] for n in ("most", "total", "inv"))
        o2 = [y[0:2 * GD].rearrange("p t f -> p (t f)").rearrange("p (r a m q) -> p r a m q", r=RR, a=4, m=WPAIRS),
              sb("o2", [2 * GD, RR, 4, WPAIRS, WIN])]
        oT = q2[:].rearrange("p r n -> p (r n)").rearrange("p (b r h m q) -> p b r h m q", b=BATCH, r=RR, h=2, m=WPAIRS)
        oP = q3[:].rearrange("p r m a q -> p (r m a q)").rearrange("p (b r m h q) -> p b r m h q", b=BATCH, r=RR, m=WPAIRS, h=2)
        q3_sb, oP_sb = c.sem("q3"), c.sem("oP")
        bank = c.banks(8)
        k_zero, v_zero, q_mm, kv_mm, q_sb, kv_sb = (c.sem(n) for n in ("k_zero", "v_zero", "q_mm", "kv_mm", "q_sb", "kv_sb"))
        (v_mm, v_sb, s_mm, most_sb, less_sb, prob_sb, total_sb, inv_sb, norm_sb, t_mm, pT_sb, o_mm, o_sb, y_mm, y_sb) = (
            c.sem(n) for n in ("v_mm", "v_sb", "s_mm", "most", "less", "prob", "total", "inv", "norm", "t_mm", "pT", "o_mm", "o", "y_mm", "y"))
        vdup_sb, own = c.sem("vdup"), c.sem("own")
        k_moved = [c.sem(f"k_moved{b}") for b in range(BATCH)]
        q_moved = [c.sem(f"q_moved{n}") for n in range(BATCH * RR)]
        o_moved = [c.sem(f"o_moved{b}") for b in range(BATCH)]
        HALF = USED // 2
        JOBS = [(b, rr, mq) for b in range(BATCH) for rr in range(RR) for mq in range(4)]
        NJ = len(JOBS)
        rows = lambda b, half, n=1: slice(b * 2 * GD + half * GD, b * 2 * GD + (half + n) * GD)
        by_window = lambda a: a.rearrange("p (w k) -> p w k", k=WIN)
        spread_w = lambda a: a.rearrange("p (w o) -> p w o", o=1).broadcast_to([P, SEG // WIN, WIN])

        with nc.Block() as block:
            @block.sync
            def _(sp):
                fetched.load(sp, w["ffn_up"], w["ffn_down"])
                for b in range(BATCH):
                    for rr in range(RR):
                        sp.wait_ge(q_sb, 2 * (b * RR + rr) + 2)
                        for half in range(2):
                            for r in range(4):
                                sp.dma_start(q2[rows(b, half), rr * 4 + r, :],
                                             qT[r * GD:(r + 1) * GD, b, rr, half * STEP:half * STEP + WPAIRS * WIN]).then_inc(q_moved[b * RR + rr], DMA)
                for b in range(BATCH):
                    for rr in range(RR):
                        sp.wait_ge(o_sb, (b * RR + rr) * 4 + 4)
                        for half in range(2):
                            for r in range(4):
                                sp.dma_start(oT[r * GD:(r + 1) * GD, b, rr, half], o2[b][half * GD:(half + 1) * GD, rr, r]).then_inc(o_moved[b], DMA)

            @block.gpsimd
            def _(pool):
                pool.memset(k2[:], 0.0).then_inc(k_zero, 1)
                pool.memset(v2[:], 0.0).then_inc(v_zero, 1)
                pool.wait_ge(k_zero, 1)
                for b in range(BATCH):
                    pool.wait_ge(kv_sb, 2 * b + 2)
                    for half in range(2):
                        for g in range(WG):
                            at = b * 2 * GD + half * GD + g * WD
                            pool.dma_start(k2[at:at + WD, half, g, :], kvT[g * WD:(g + 1) * WD, b, half * STEP:half * STEP + WPAIRS * WIN]).then_inc(k_moved[b], DMA)
                for i in range(NJ):
                    pool.wait_ge(inv_sb, i + 1)
                    if i >= 2:
                        pool.wait_ge(t_mm, i - 1)
                    pool.tensor_tensor(by_window(norm[i % 2][:]), by_window(prob[i % 2][:]), spread_w(inv[i % 2][:]), ALU.mult).then_inc(norm_sb, 1)

            @block.scalar
            def _(act):
                for b in range(BATCH):
                    for n in range(2):
                        act.wait_ge(kv_mm, 2 * b + n + 1)
                        act.activation(kvT[:, b, n * HALF:(n + 1) * HALF], bank[n][0:2 * GD, 0:HALF], ACT.Identity, bias=bkv[:, 0:1]).then_inc(kv_sb, 1)
                    for rr in range(RR):
                        for n in range(2):
                            i = (b * RR + rr) * 2 + n
                            act.wait_ge(q_mm, i + 1)
                            act.activation(qT[:, b, rr, n * HALF:(n + 1) * HALF], bank[2 + i % 4][:, 0:HALF], ACT.Identity, bias=bq[:, rr:rr + 1]).then_inc(q_sb, 1)
                for i in range(NJ + 5):
                    if 5 <= i:
                        n = i - 5
                        b, rr, mq = JOBS[n]
                        act.wait_ge(o_mm, n + 1)
                        act.activation(o2[b][:, rr, :, mq * 4:mq * 4 + 4, :].rearrange("p r m q -> p m r q"),
                                       bank[4 + n % 2][0:2 * GD, :].rearrange("p (m r q) -> p m r q", m=4, r=4), ACT.Copy).then_inc(o_sb, 1)
                    if 4 <= i < NJ + 4:
                        n = i - 4
                        act.wait_ge(t_mm, n + 1)
                        if n >= 2:
                            act.wait_ge(o_mm, n - 1)
                        act.activation(pT[n % 2][:], bank[2 + n % 2][:], ACT.Copy).then_inc(pT_sb, 1)
                    if i < NJ:
                        act.wait_ge(less_sb, i + 1)
                        if i >= 2:
                            act.wait_ge(norm_sb, i - 1)
                        act.activation(prob[i % 2][:], less[i % 2][:], ACT.Exp, scale=float(WD) ** -0.5).then_inc(prob_sb, 1)
                before.affine.act_root(act)
                turn.affine.act_root(act)
                turn.act_apply(act, 0)

            @block.vector
            def _(dve):
                chain = Chain(dve, own)
                for b in range(BATCH):
                    dve.wait_ge(kv_sb, 2 * b + 2)
                    for half in range(2):
                        v = kvT[GD:2 * GD, b, half * STEP:half * STEP + WPAIRS * WIN].rearrange("p (m k) -> p m k", k=WIN)
                        for g in range(WG):
                            last = dve.tensor_copy(vdup[GD:2 * GD, b, :, half, g, :], v)
                    last.then_inc(vdup_sb, 1)
                def arrange(n):
                    b, rr = n // RR, n % RR
                    dve.wait_ge(q_moved[n], 8 * DMA)
                    dve.tensor_copy(q3[rows(b, 0, 2), rr].rearrange("p m r q -> p r m q"),
                                    q2[rows(b, 0, 2), rr * 4:rr * 4 + 4, :].rearrange("p r (m q) -> p r m q", q=WIN)).then_inc(q3_sb, 1)

                dve.wait_ge(v_zero, 1)
                for b in range(BATCH):
                    dve.wait_ge(v_mm, b + 1)
                    for half in range(2):
                        for g in range(WG):
                            at = (half * WG + g) * WIN
                            col = half * GD + g * WD
                            last = dve.tensor_copy(v2[at:at + WIN, b, :, col:col + WD],
                                                   bank[6 + b][at:at + WIN, :].rearrange("p (m n) -> p m n", n=GD)[:, :, g * WD:(g + 1) * WD])
                    last.then_inc(v_sb, 1)
                arrange(0)
                for i in range(NJ + 1):
                    if i % 4 == 2 and i // 4 + 1 < BATCH * RR:
                        arrange(i // 4 + 1)
                    if i < NJ:
                        x = i % 2
                        scores = by_window(bank[x][:])
                        dve.wait_ge(s_mm, i + 1)
                        dve.tensor_reduce(most[x][:], scores, AX.X, ALU.max).then_inc(most_sb, 1)
                        dve.wait_ge(most_sb, i + 1)
                        dve.tensor_tensor(by_window(less[x][:]), scores, spread_w(most[x][:]), ALU.subtract).then_inc(less_sb, 1)
                    if 1 <= i <= NJ:
                        n = i - 1
                        x = n % 2
                        dve.wait_ge(prob_sb, n + 1)
                        dve.tensor_reduce(total[x][:], by_window(prob[x][:]), AX.X, ALU.add).then_inc(total_sb, 1)
                        dve.wait_ge(total_sb, n + 1)
                        if n >= 2:
                            dve.wait_ge(norm_sb, n - 1)
                        dve.reciprocal(inv[x][:], total[x][:]).then_inc(inv_sb, 1)
                for b in range(BATCH):
                    dve.wait_ge(o_moved[b], 16 * DMA)
                    for rr in range(RR):
                        dve.tensor_copy(oP[:, b, rr].rearrange("p m h q -> p h m q"), oT[:, b, rr]).then_inc(oP_sb, 1)
                    for t in range(b * TT // 4, (b + 1) * TT // 4):
                        if t in (2, 3):
                            dve.wait_ge(y_sb, t - 1)
                            before.statistics(dve, chain, 0, t - 2)
                        if t == TT // 4:
                            before.affine.dve_quick_scale(dve, chain, 0)
                            before.dve_apply(dve, chain, 0)
                            before.add(dve, 0)
                        if t == TT // 4 + 1:
                            dve.wait_ge(before.added, 1)
                            for half in range(2):
                                turn.statistics(dve, chain, 0, half)
                        if t == TT // 4 + 2:
                            turn.affine.dve_quick_scale(dve, chain, 0)
                        if t == TT // 4 + 3:
                            dve.wait_ge(y_sb, 4)
                            for half in range(2):
                                before.statistics(dve, chain, 1, half)
                        dve.wait_ge(y_mm, t + 1)
                        dve.tensor_tensor(y[:, 2 * t:2 * t + 2, :], bank[6 + t % 2][:].rearrange("p (a f) -> p a f", a=2),
                                          bo[:].rearrange("p (o f) -> p o f", o=1).broadcast_to([P, 2, HID]), ALU.add).then_inc(y_sb, 1)

            @block.tensor
            def _(pe):
                def project(to, w_hi, w_lo, cols, b, n):
                    toks = slice(b * SEQ + n * HALF, b * SEQ + (n + 1) * HALF)
                    for f in range(KT):
                        last = three_passes(nc, to[:, 0:HALF], (w_hi[:, f, cols], w_lo[:, f, cols]),
                                            (keep.xT_hi[:, f, toks], keep.xT_lo[:, f, toks]), f == 0, f == KT - 1)
                    return last

                for b in range(BATCH):
                    for n in range(2):
                        if b:
                            pe.wait_ge(kv_sb, n + 1)
                        project(bank[n], wkv_hi, wkv_lo, slice(0, P), b, n).then_inc(kv_mm, 1)
                    for rr in range(RR):
                        for n in range(2):
                            i = (b * RR + rr) * 2 + n
                            if i >= 4:
                                pe.wait_ge(q_sb, i - 3)
                            project(bank[2 + i % 4], wq_hi, wq_lo, slice(rr * P, (rr + 1) * P), b, n).then_inc(q_mm, 1)
                for b in range(BATCH):
                    pe.wait_ge(vdup_sb, b + 1)
                    for m in range(WPAIRS):
                        last = pe.transpose(bank[6 + b][:, m * GD:(m + 1) * GD], vdup[GD:2 * GD, b, m, :, :, :].rearrange("p h g k -> p (h g k)"),
                                            keep.ident[GD:2 * GD, GD:2 * GD])
                    last.then_inc(v_mm, 1)
                pe.wait_ge(q_sb, 4 * RR)
                pe.wait_ge(kv_sb, 4)
                for i in range(NJ + 4):
                    if i < NJ:
                        b, rr, mq = JOBS[i]
                        if i % (NJ // BATCH) == 0:
                            pe.wait_ge(k_moved[b], 4 * DMA)
                        pe.wait_ge(q3_sb, b * RR + rr + 1)
                        if i >= 2:
                            pe.wait_ge(less_sb, i - 1)
                        for j in range(4):
                            at = slice((mq * 4 + j) * WIN, (mq * 4 + j + 1) * WIN)
                            last = pe.matmul(bank[i % 2][:, j * P:(j + 1) * P].rearrange("p (a k) -> p a k", k=WIN), q3[rows(b, 0, 2), rr, mq * 4 + j].rearrange("p r q -> p (r q)"),
                                             k2[rows(b, 0, 2), :, :, at].rearrange("p a g k -> p (a g) k"), start=True, stop=True)
                        last.then_inc(s_mm, 1)
                    if 3 <= i < NJ + 3:
                        n = i - 3
                        pe.wait_ge(norm_sb, n + 1)
                        if n >= 2:
                            pe.wait_ge(pT_sb, n - 1)
                        for j in range(4):
                            last = pe.transpose(bank[2 + n % 2][:, j * P:(j + 1) * P], norm[n % 2][:, j * P:(j + 1) * P], keep.ident[:])
                        last.then_inc(t_mm, 1)
                    if 4 <= i < NJ + 4:
                        n = i - 4
                        b, rr, mq = JOBS[n]
                        pe.wait_ge(pT_sb, n + 1)
                        pe.wait_ge(v_sb, 2)
                        if n >= 2:
                            pe.wait_ge(o_sb, n - 1)
                        for j in range(4):
                            last = pe.matmul(bank[4 + n % 2][0:2 * GD, j * P:(j + 1) * P], v2[:, b, mq * 4 + j, :], pT[n % 2][:, j * P:(j + 1) * P],
                                             start=True, stop=True)
                        last.then_inc(o_mm, 1)
                for t in range(TT):
                    b, tile = t // (TT // BATCH), t % (TT // BATCH)
                    if t % (TT // BATCH) == 0:
                        pe.wait_ge(oP_sb, (b + 1) * RR)
                    if t >= 4 and t % 2 == 0:
                        pe.wait_ge(y_sb, t // 2 - 1)
                    for rr in range(RR):
                        o = oP[:, b, rr, 2 * tile:2 * tile + 2].rearrange("p m h q -> p (m h q)")
                        last = pe.matmul(bank[6 + t // 2 % 2][:, t % 2 * HID:(t % 2 + 1) * HID], o, wo[:, rr, :], start=rr == 0, stop=rr == RR - 1)
                    if t % 2:
                        last.then_inc(y_mm, 1)


def lay_out_window(Wq, bq, Wk, bk, Wv, bv, Wo, bo):
    return {"Wq": Wq, "bq": np.ascontiguousarray(bq.reshape(RR, P).T), "Wk": Wk, "bk": bk.reshape(GD, 1),
            "Wv": Wv, "bv": bv.reshape(GD, 1), "Wo": Wo, "bo": bo}


def build_program(nc, a, out, tokens_x, sorted_y):
    keep = Keep()
    with Scope(nc, "keep") as whole:
        allocate(nc, keep, whole)
        moe_keep(keep, whole)
        y = whole.sb("y", [P, TT, HID])
        with Scope(nc, "linear_out") as c:
            keep.acc, keep.squares = c.sb("acc", [P, SEGS, KT, SEG]), c.sb("squares", [P, TOK])
            output = AttentionOutput(c, keep, y)
            normed = keep.acc[:].rearrange("p s k t -> p (s k t)").rearrange("p (t f) -> p t f", f=HID)
            after = Norms(c, keep, "after", y, None, normed)
            linear_attention(nc, keep, a["x"], a["slope"], a["wp"], a["wop"], a["nw"], output, after)
            with Scope(nc, "window") as c_window:
                window = WindowWeights(c_window)
                with Scope(nc, "shared") as c_shared:
                    keep.shared = SwigluWeights(c_shared, SHARED)
                    with Scope(nc, "experts_up") as c_up:
                        keep.expert_up, keep.expert_up_in = c_up.sb("expert_up", [P, NE, KT, 2 * INNER]), c_up.sem("expert_up_in")
                        close_attention_and_route(nc, keep, y, output, after, a["shared_gate_up"], a["shared_down"], a["gw"], tokens_x, a["wgu"])
                        experts(nc, keep, a["wdn"], tokens_x, sorted_y)
                    combine_and_norm(nc, keep, sorted_y, y, window, a)
                before, turn = AddNorm(c_window, keep, "before", y), TurnNorm(c_window, keep, "turn", c_window.sb("turn_z", [P, TPS, HID])[:])
                fetched = Fetched(c_window, FFN, keep.acc[:].rearrange("p s k t -> p (s k t)"), keep.squares[:])
                window_attention(nc, keep, y, window, before, turn, fetched, a)
                feed_forward(nc, keep, y, before, turn, fetched, out.rearrange("b (t p) f -> p (b t) f", p=P))


def kernel(L0_attn_hidden_states, L0_attn_slope_rate, L0_attn_w_qkv, L0_attn_w_gate, L0_attn_w_out, L0_attn_norm_w,
           L0_ffn_gate_w, L0_ffn_w_gate_up, L0_ffn_w_down, L0_ffn_shared_gate_up, L0_ffn_shared_down,
           L1_attn_Wq, L1_attn_bq, L1_attn_Wk, L1_attn_bk, L1_attn_Wv, L1_attn_bv, L1_attn_Wo, L1_attn_bo,
           L1_ffn_w_gate_up, L1_ffn_w_down):
    import concourse.bacc as bacc
    from concourse.bass_utils import run_bass_kernel_spmd

    arrays = {
        "x": L0_attn_hidden_states, "slope": L0_attn_slope_rate,
        **lay_out_linear(L0_attn_w_qkv, L0_attn_w_gate, L0_attn_w_out, L0_attn_norm_w),
        **lay_out_moe(L0_ffn_gate_w, L0_ffn_w_gate_up, L0_ffn_w_down),
        "shared_gate_up": L0_ffn_shared_gate_up, "shared_down": L0_ffn_shared_down,
        **lay_out_window(L1_attn_Wq, L1_attn_bq, L1_attn_Wk, L1_attn_bk, L1_attn_Wv, L1_attn_bv, L1_attn_Wo, L1_attn_bo),
        "ffn_up": L1_ffn_w_gate_up.T, "ffn_down": L1_ffn_w_down.T,
    }
    arrays = {f"in_{n}": np.ascontiguousarray(v) for n, v in arrays.items()}
    nc = bacc.Bacc("TRN2", target_bir_lowering=False, num_devices=1)
    a = {n[3:]: nc.dram_tensor(n, v.shape, mybir.dt.from_np(v.dtype), kind="ExternalInput").ap() for n, v in arrays.items()}
    out = nc.dram_tensor("out", (BATCH, SEQ, HID), F32, kind="ExternalOutput").ap()
    tokens_x = nc.dram_tensor("tokens_x", (TOK, HID), F32).ap()
    sorted_y = nc.dram_tensor("sorted_y", (SLOTS, HID), F32).ap()
    build_program(nc, a, out, tokens_x, sorted_y)
    return run_bass_kernel_spmd(nc, [arrays], core_ids=[0]).results[0]["out"]
```
